# Optimizing a Trainium2 kernel written in Bass

```python
import numpy as np
import jax
import jax.numpy as jnp

def _softmax(x, axis=-1):
    return jax.nn.softmax(x, axis=axis)

def _gelu(x):
    return jax.nn.gelu(x, approximate=True)

def _silu(x):
    return jax.nn.silu(x)

def _sigmoid(x):
    return jax.nn.sigmoid(x)

def _layernorm(x, axis=-1, eps=1e-05):
    m = jnp.mean(x, axis=axis, keepdims=True)
    v = jnp.var(x, axis=axis, keepdims=True)
    return (x - m) / jnp.sqrt(v + eps)

def _scatter_add(tgt, idx, src, axis=0):
    return tgt.at[idx].add(src)

def _segment_sum(src, seg, n):
    return jax.ops.segment_sum(src, seg, n)
kernel_name = 'mk_gps_d1_gnn_r8_762b44'

def setup_inputs(seed: int=0):
    np.random.seed(seed)
    _w = jnp.asarray

    def _rec_inputs():
        import jax
        import jax.numpy as jnp
        _gk = jax.random.key(seed)
        x = -8.776e-05 + 1 * jax.random.normal(jax.random.fold_in(_gk, 1), (6250, 256), jnp.float32)
        src = jax.random.randint(jax.random.fold_in(_gk, 2), (100000,), 0, 6250, jnp.int32)
        dst = jnp.minimum((6250 * jax.random.uniform(jax.random.fold_in(_gk, 3), (100000,)) ** 2.0).astype(jnp.int32), 49999)
        _o = jnp.argsort(dst, stable=True)
        src = src[_o]
        dst = dst[_o]
        return (x, src, dst)
    x, src, dst = _rec_inputs()

    def _L0_gnn_setup():
        import jax, jax.numpy as jnp
        import numpy as np
        N = 2500
        E = 40000
        IN = 256
        HID = 256
        OUT = 256
        H1 = 8
        D1 = HID // H1
        H2 = 1

        def gat_conv(h, src, dst, fc_w, attn_l, attn_r, bias, heads, out_feats):
            n = h.shape[0]
            feat = (h @ fc_w.T).reshape(n, heads, out_feats)
            el = jnp.sum(feat * attn_l, axis=-1)
            er = jnp.sum(feat * attn_r, axis=-1)
            e = jax.nn.leaky_relu(el[src] + er[dst], 0.2)
            m = jax.ops.segment_max(e, dst, num_segments=n)
            m = jnp.where(jnp.isfinite(m), m, 0.0)
            ex = jnp.exp(e - m[dst])
            ssum = jax.ops.segment_sum(ex, dst, num_segments=n)
            a = ex / ssum[dst]
            rst = jax.ops.segment_sum(feat[src] * a[..., None], dst, num_segments=n)
            return rst + bias.reshape(heads, out_feats)
        key = jax.random.key(seed)
        ks = jax.random.split(key, 16)
        s = 0.05
        inputs = jax.random.normal(ks[0], (N, IN), jnp.float32)
        src = jax.random.randint(ks[1], (E,), 0, N, jnp.int32)
        dst = jax.random.randint(ks[2], (E,), 0, N, jnp.int32)
        return {'inputs': inputs, 'src': src, 'dst': dst, 'fc1_w': jax.random.normal(ks[3], (H1 * D1, IN), jnp.float32) * s, 'attn_l1': jax.random.normal(ks[4], (H1, D1), jnp.float32) * s, 'attn_r1': jax.random.normal(ks[5], (H1, D1), jnp.float32) * s, 'bias1': jax.random.normal(ks[6], (H1 * D1,), jnp.float32) * s, 'fc2_w': jax.random.normal(ks[7], (H2 * OUT, HID), jnp.float32) * s, 'attn_l2': jax.random.normal(ks[8], (H2, OUT), jnp.float32) * s, 'attn_r2': jax.random.normal(ks[9], (H2, OUT), jnp.float32) * s, 'bias2': jax.random.normal(ks[10], (H2 * OUT,), jnp.float32) * s, 'wb0': jax.random.normal(ks[11], (HID, IN), jnp.float32) * s, 'bb0': jax.random.normal(ks[12], (HID,), jnp.float32) * s, 'wb1': jax.random.normal(ks[13], (OUT, IN + HID), jnp.float32) * s, 'bb1': jax.random.normal(ks[14], (OUT,), jnp.float32) * s}
    _L0_gnn_all = _L0_gnn_setup()
    _L0_gnn_in = {k: v for k, v in _L0_gnn_all.items() if k in ('fc1_w', 'attn_l1', 'attn_r1', 'bias1', 'fc2_w', 'attn_l2', 'attn_r2', 'bias2', 'wb0', 'bb0', 'wb1', 'bb1')}
    del _L0_gnn_all

    def _L0_mix_setup():
        import jax, jax.numpy as jnp
        import numpy as np
        DIM = 256
        HEADS = 4
        HEAD_DIM = DIM // HEADS
        MLP_HIDDEN = DIM * 3
        B, N = (8, 512)
        EPS = 1e-05

        def _layernorm(x, g, b):
            mu = jnp.mean(x, axis=-1, keepdims=True)
            var = jnp.mean(jnp.square(x - mu), axis=-1, keepdims=True)
            return (x - mu) * jax.lax.rsqrt(var + EPS) * g + b
        key = jax.random.key(seed)
        ks = jax.random.split(key, 8)
        s = 0.02
        return {'x': jax.random.normal(ks[0], (B, N, DIM), dtype=jnp.float32), 'w_qkv': jax.random.normal(ks[1], (DIM, 3 * DIM), dtype=jnp.float32) * s, 'b_qkv': jnp.zeros((3 * DIM,), dtype=jnp.float32), 'norm_g': jnp.ones((DIM,), dtype=jnp.float32), 'norm_b': jnp.zeros((DIM,), dtype=jnp.float32), 'w_fc1': jax.random.normal(ks[2], (DIM, MLP_HIDDEN), dtype=jnp.float32) * s, 'b_fc1': jnp.zeros((MLP_HIDDEN,), dtype=jnp.float32), 'w_fc2': jax.random.normal(ks[3], (MLP_HIDDEN, DIM), dtype=jnp.float32) * s, 'b_fc2': jnp.zeros((DIM,), dtype=jnp.float32)}
    _L0_mix_all = _L0_mix_setup()
    _L0_mix_in = {k: v for k, v in _L0_mix_all.items() if k in ('w_qkv', 'b_qkv', 'norm_g', 'norm_b', 'w_fc1', 'b_fc1', 'w_fc2', 'b_fc2')}
    del _L0_mix_all

    def _L0_ffn_setup():
        import math
        import jax, jax.numpy as jnp
        import numpy as np
        CAPACITY_FACTOR = 1.25
        key = jax.random.key(seed)
        ks = jax.random.split(key, 5)
        B, L, D, F, E = (8, 1024, 256, 1024, 8)
        h = jax.random.normal(ks[0], (B, L, D), dtype=jnp.float32)
        gate_w = jax.random.normal(ks[1], (D, E), dtype=jnp.float32) * 0.02
        gate_b = jnp.zeros((E,), dtype=jnp.float32)
        w1 = jax.random.normal(ks[2], (E, D, F), dtype=jnp.float32) * (1.0 / math.sqrt(D))
        b1 = jnp.zeros((E, F), dtype=jnp.float32)
        w2 = jax.random.normal(ks[3], (E, F, D), dtype=jnp.float32) * (1.0 / math.sqrt(F))
        b2 = jnp.zeros((E, D), dtype=jnp.float32)
        return {'h': h, 'gate_w': gate_w, 'gate_b': gate_b, 'w1': w1, 'b1': b1, 'w2': w2, 'b2': b2}
    _L0_ffn_all = _L0_ffn_setup()
    _L0_ffn_in = {k: v for k, v in _L0_ffn_all.items() if k in ('gate_w', 'gate_b', 'w1', 'b1', 'w2', 'b2')}
    del _L0_ffn_all
    return {'x': x, 'src': src, 'dst': dst, 'L0_gnn_fc1_w': _L0_gnn_in['fc1_w'], 'L0_gnn_attn_l1': _L0_gnn_in['attn_l1'], 'L0_gnn_attn_r1': _L0_gnn_in['attn_r1'], 'L0_gnn_bias1': _L0_gnn_in['bias1'], 'L0_gnn_fc2_w': _L0_gnn_in['fc2_w'], 'L0_gnn_attn_l2': _L0_gnn_in['attn_l2'], 'L0_gnn_attn_r2': _L0_gnn_in['attn_r2'], 'L0_gnn_bias2': _L0_gnn_in['bias2'], 'L0_gnn_wb0': _L0_gnn_in['wb0'], 'L0_gnn_bb0': _L0_gnn_in['bb0'], 'L0_gnn_wb1': _L0_gnn_in['wb1'], 'L0_gnn_bb1': _L0_gnn_in['bb1'], 'L0_mix_w_qkv': _L0_mix_in['w_qkv'], 'L0_mix_b_qkv': _L0_mix_in['b_qkv'], 'L0_mix_norm_g': _L0_mix_in['norm_g'], 'L0_mix_norm_b': _L0_mix_in['norm_b'], 'L0_mix_w_fc1': _L0_mix_in['w_fc1'], 'L0_mix_b_fc1': _L0_mix_in['b_fc1'], 'L0_mix_w_fc2': _L0_mix_in['w_fc2'], 'L0_mix_b_fc2': _L0_mix_in['b_fc2'], 'L0_ffn_gate_w': _L0_ffn_in['gate_w'], 'L0_ffn_gate_b': _L0_ffn_in['gate_b'], 'L0_ffn_w1': _L0_ffn_in['w1'], 'L0_ffn_b1': _L0_ffn_in['b1'], 'L0_ffn_w2': _L0_ffn_in['w2'], 'L0_ffn_b2': _L0_ffn_in['b2']}

def reference(x, src, dst, L0_gnn_fc1_w, L0_gnn_attn_l1, L0_gnn_attn_r1, L0_gnn_bias1, L0_gnn_fc2_w, L0_gnn_attn_l2, L0_gnn_attn_r2, L0_gnn_bias2, L0_gnn_wb0, L0_gnn_bb0, L0_gnn_wb1, L0_gnn_bb1, L0_mix_w_qkv, L0_mix_b_qkv, L0_mix_norm_g, L0_mix_norm_b, L0_mix_w_fc1, L0_mix_b_fc1, L0_mix_w_fc2, L0_mix_b_fc2, L0_ffn_gate_w, L0_ffn_gate_b, L0_ffn_w1, L0_ffn_b1, L0_ffn_w2, L0_ffn_b2):
    import jax
    import jax.numpy as jnp

    def _L0_gnn_ref(inputs, src, dst, fc1_w, attn_l1, attn_r1, bias1, fc2_w, attn_l2, attn_r2, bias2, wb0, bb0, wb1, bb1):
        import jax, jax.numpy as jnp
        import numpy as np
        N = 2500
        E = 40000
        IN = 256
        HID = 256
        OUT = 256
        H1 = 8
        D1 = HID // H1
        H2 = 1

        def gat_conv(h, src, dst, fc_w, attn_l, attn_r, bias, heads, out_feats):
            n = h.shape[0]
            feat = (h @ fc_w.T).reshape(n, heads, out_feats)
            el = jnp.sum(feat * attn_l, axis=-1)
            er = jnp.sum(feat * attn_r, axis=-1)
            e = jax.nn.leaky_relu(el[src] + er[dst], 0.2)
            m = jax.ops.segment_max(e, dst, num_segments=n)
            m = jnp.where(jnp.isfinite(m), m, 0.0)
            ex = jnp.exp(e - m[dst])
            ssum = jax.ops.segment_sum(ex, dst, num_segments=n)
            a = ex / ssum[dst]
            rst = jax.ops.segment_sum(feat[src] * a[..., None], dst, num_segments=n)
            return rst + bias.reshape(heads, out_feats)
        n = inputs.shape[0]
        deg = jax.ops.segment_sum(jnp.ones_like(dst, jnp.float32), dst, num_segments=n)
        norm = (1.0 / jnp.clip(deg, 1.0, None))[:, None]
        h0 = gat_conv(inputs, src, dst, fc1_w, attn_l1, attn_r1, bias1, H1, D1)
        h0 = h0.reshape(n, H1 * D1)
        h1 = jax.nn.relu(h0 + norm * (inputs @ wb0.T + bb0))
        h2 = gat_conv(h1, src, dst, fc2_w, attn_l2, attn_r2, bias2, H2, OUT)
        h2 = h2.mean(axis=1)
        cat = jnp.concatenate([inputs, h1], axis=-1)
        return h2 + norm * (cat @ wb1.T + bb1)

    def _L0_mix_ref(x, w_qkv, b_qkv, norm_g, norm_b, w_fc1, b_fc1, w_fc2, b_fc2):
        import jax, jax.numpy as jnp
        import numpy as np
        DIM = 256
        HEADS = 4
        HEAD_DIM = DIM // HEADS
        MLP_HIDDEN = DIM * 3
        B, N = (8, 512)
        EPS = 1e-05

        def _layernorm(x, g, b):
            mu = jnp.mean(x, axis=-1, keepdims=True)
            var = jnp.mean(jnp.square(x - mu), axis=-1, keepdims=True)
            return (x - mu) * jax.lax.rsqrt(var + EPS) * g + b
        Bx, Nx, C = x.shape
        scale = HEAD_DIM ** (-0.5)
        qkv = (x @ w_qkv + b_qkv).reshape(Bx, Nx, 3, HEADS, HEAD_DIM)
        qkv = jnp.transpose(qkv, (2, 0, 3, 1, 4))
        q, k, v = (qkv[0], qkv[1], qkv[2])
        k = k * scale
        attn = jnp.einsum('bhnd,bhne->bhde', k, v)
        attn = jax.nn.softmax(attn, axis=-1)
        xf = jnp.einsum('bhde,bhne->bhnd', attn, q)
        xf = jnp.transpose(xf, (0, 2, 1, 3)).reshape(Bx, Nx, C)
        x = x + xf
        h = _layernorm(x, norm_g, norm_b)
        h = jax.nn.gelu(h @ w_fc1 + b_fc1, approximate=False) @ w_fc2 + b_fc2
        return x + h

    def _L0_ffn_ref(h, gate_w, gate_b, w1, b1, w2, b2):
        import math
        import jax, jax.numpy as jnp
        import numpy as np
        CAPACITY_FACTOR = 1.25
        B, L, D = h.shape
        E = gate_w.shape[1]
        T = B * L
        C = max(1, math.ceil(CAPACITY_FACTOR * T / E))
        x = h.reshape(T, D)
        logits = x @ gate_w + gate_b
        probs = jax.nn.softmax(logits, axis=-1)
        idx = jnp.argmax(probs, axis=-1)
        prb = jnp.take_along_axis(probs, idx[:, None], axis=1)[:, 0]
        one_hot = jax.nn.one_hot(idx, E, dtype=jnp.float32)
        pos = (jnp.cumsum(one_hot, axis=0) * one_hot).sum(-1).astype(jnp.int32) - 1
        kept = pos < C
        pos_safe = jnp.where(kept, pos, C)
        buf = jnp.zeros((E, C, D), dtype=h.dtype).at[idx, pos_safe].set(x, mode='drop')
        hmid = jax.nn.relu(jnp.einsum('ecd,edf->ecf', buf, w1) + b1[:, None, :])
        ybuf = jnp.einsum('ecf,efd->ecd', hmid, w2) + b2[:, None, :]
        pos_g = jnp.minimum(pos, C - 1)
        y_tok = ybuf[idx, pos_g] * (prb * kept)[:, None]
        y = y_tok.reshape(B, L, D)
        y = jnp.nan_to_num(y, nan=0.0, posinf=10000.0, neginf=-10000.0)
        return y
    xn = _layernorm(x, axis=-1)
    x = x + _L0_gnn_ref(xn, src, dst, L0_gnn_fc1_w, L0_gnn_attn_l1, L0_gnn_attn_r1, L0_gnn_bias1, L0_gnn_fc2_w, L0_gnn_attn_l2, L0_gnn_attn_r2, L0_gnn_bias2, L0_gnn_wb0, L0_gnn_bb0, L0_gnn_wb1, L0_gnn_bb1) + _L0_mix_ref(xn[None], L0_mix_w_qkv, L0_mix_b_qkv, L0_mix_norm_g, L0_mix_norm_b, L0_mix_w_fc1, L0_mix_b_fc1, L0_mix_w_fc2, L0_mix_b_fc2)[0]
    x = x + _L0_ffn_ref(_layernorm(x, axis=-1)[None], L0_ffn_gate_w, L0_ffn_gate_b, L0_ffn_w1, L0_ffn_b1, L0_ffn_w2, L0_ffn_b2)[0]
    return x

_drawn_inputs = setup_inputs


def setup_inputs(seed=0):
    import zlib

    import numpy as np

    out = dict(_drawn_inputs(seed))
    spreads = {'L0_mix_b_qkv': (0.0, 0.1),
     'L0_mix_norm_g': (1.0, 0.6),
     'L0_mix_norm_b': (0.0, 0.8),
     'L0_mix_b_fc1': (0.0, 0.492),
     'L0_mix_b_fc2': (0.0, 0.1),
     'L0_ffn_gate_b': (0.0, 0.1),
     'L0_ffn_b1': (0.0, 0.8),
     'L0_ffn_b2': (0.0, 0.8)}
    factors = {'L0_gnn_attn_l1': 8.0,
     'L0_gnn_attn_r1': 21.487,
     'L0_gnn_bias1': 4.281,
     'L0_gnn_attn_l2': 8.0,
     'L0_gnn_attn_r2': 8.0,
     'L0_gnn_wb0': 5.109,
     'L0_gnn_bb0': 24.3,
     'L0_gnn_bb1': 8.0}
    for name, (base, spread) in spreads.items():
        noise = np.random.default_rng([zlib.crc32(name.encode()), seed]).standard_normal(out[name].shape)
        drawn = base * np.exp(spread * noise) if base else spread * noise
        out[name] = jnp.asarray(drawn.astype(out[name].dtype))
    for name, factor in factors.items():
        out[name] = (out[name] * factor).astype(out[name].dtype)
    return out
```

```python
from contextlib import ExitStack

import concourse.bass as bass
from concourse import mybir

F32 = mybir.dt.float32
I32 = mybir.dt.int32
U32 = mybir.dt.uint32
BF16 = mybir.dt.bfloat16
ALU = mybir.AluOpType
ACT = mybir.ActivationFunctionType
AX = mybir.AxisListType.X

P = 128
N, D = 6250, 256
NODES_T = 125
NT = N // NODES_T
E = 100000
ET = -(-E // P)
ROWS = 112
RT = 7
ET_PAD = ROWS * RT
GROUP = 8
BATCHES = 104
UNROLL = 4
STEPS = (BATCHES + 2) * GROUP
GE = GROUP * P
WIN = P + 2
ROW_E = P + WIN
H1, D1 = 8, 32
BIG = 1e30
PAD_DST = 1000000
EPS = 1e-5
HIDDEN = 3 * D
EXPERTS, FF = 8, 1024
CAP = -(-5 * N // (4 * EXPERTS))
SLOTS = 1000
XROWS = EXPERTS * SLOTS + N
assert NODES_T * NT == N and ET + NT - 1 <= BATCHES * GROUP and ET < ET_PAD and CAP <= SLOTS and BATCHES % UNROLL == 0


class Memory:
    pass


class Chain:

    def __init__(self, eng, sem, turn=0, per_turn=0, base=0):
        self.eng, self.sem, self.turn, self.per_turn, self.base, self.n = eng, sem, turn, per_turn, base, 0

    def done(self, ins):
        ins.then_inc(self.sem, 1)
        self.n += 1
        return self.n

    def wait(self, n=None):
        n = self.n if n is None else n
        self.eng.wait_ge(self.sem, self.turn * self.per_turn + (self.base + n))

    def wait_apart(self, hold):
        self.wait()
        self.eng.sem_inc(hold, 1)

    def close(self):
        assert self.n == self.per_turn, (self.n, self.per_turn)
        return self.base + self.n


def sb(nc, scope, name, shape, dt=F32):
    return scope.enter_context(nc.sbuf_tensor(name, list(shape), dt))


def ps(nc, scope, name, shape=(P, 512), dt=F32):
    return scope.enter_context(nc.psum_tensor("ps_" + name, list(shape), dt))


def build_steps(nc, m):
    with ExitStack() as scope:
        ei = sb(nc, scope, "ei", [ROWS, RT, ROW_E], I32)
        ef = sb(nc, scope, "ef", [ROWS, RT, ROW_E])
        bounds = sb(nc, scope, "bounds", [P, NT - 1])
        junk = sb(nc, scope, "junk", [P, ET_PAD])
        last = sb(nc, scope, "last", [ROWS, RT])
        tile_no = sb(nc, scope, "tile_no", [ROWS, RT])
        crossed = sb(nc, scope, "crossed", [ROWS, RT])
        fin = sb(nc, scope, "fin", [ROWS, RT])
        fin_b = sb(nc, scope, "fin_b", [P, ET_PAD])
        step_no = sb(nc, scope, "step_no", [P, RT])
        edge_t = sb(nc, scope, "edge_t", [P, RT])
        edge_i = sb(nc, scope, "edge_i", [P, RT], I32)
        node_t = sb(nc, scope, "node_t", [P, RT])
        node_i = sb(nc, scope, "node_i", [P, RT], I32)
        base = sb(nc, scope, "base", [P, RT])
        rows = sb(nc, scope, "rows", [P, RT, ROW_E])
        dl = sb(nc, scope, "dl", [P, RT, P])
        ge = sb(nc, scope, "ge", [P, RT, P])
        valid = sb(nc, scope, "valid", [P, RT, P])
        edge = sb(nc, scope, "edge", [P, 2, RT, P])
        flag = sb(nc, scope, "flag", [P, 3, RT, P])
        cont = sb(nc, scope, "cont", [P, RT])
        tp = [ps(nc, scope, f"tp{k}") for k in range(4)]
        loaded = m.sem("edges_loaded")
        consts = m.sem("consts_made")
        padded = m.sem("pads_written")
        table = m.sem("edge_table_stored")
        fin_ready = m.sem("fin_ready")
        fin_moved = m.sem("fin_moved")
        tiles_known = m.sem("tiles_known")
        gathered = m.sem("rows_of_steps_gathered")
        flags_made = m.sem("flags_made")
        stored = m.sem("step_tables_stored")
        turned = m.sem("steps_turned")
        copied = m.sem("steps_copied")
        own = m.sem("steps_dve")
        n_loads = 0

        def rows_of(t):
            return min(ROWS, E // P - t * ROWS)

        with nc.Block() as block:
            @block.gpsimd
            def _(pool):
                pool.memset(ei[:, :, 0:P], 0).then_inc(padded, 1)
                pool.memset(ei[:, :, P:ROW_E], PAD_DST).then_inc(padded, 1)
                pool.memset(m.ones[:, :], 1.0).then_inc(consts, 1)
                pool.memset(m.ident[:, :], 0.0).then_inc(consts, 1)
                pool.wait_ge(consts, 2)
                pool.affine_select(out=m.ident[:, :], in_=m.ident[:, :], compare_op=ALU.not_equal, fill=1.0,
                                   base=0, pattern=[[-1, P]], channel_multiplier=1).then_inc(consts, 1)
                pool.iota(m.lane[:, :], pattern=[[0, 1]], base=0, channel_multiplier=1,
                          allow_small_or_imprecise_dtypes=True).then_inc(consts, 1)
                pool.iota(m.iota[:, :], pattern=[[1, NODES_T]], base=0, channel_multiplier=0,
                          allow_small_or_imprecise_dtypes=True).then_inc(consts, 1)
                pool.iota(bounds[:, :], pattern=[[NODES_T, NT - 1]], base=NODES_T, channel_multiplier=0,
                          allow_small_or_imprecise_dtypes=True).then_inc(consts, 1)
                pool.iota(tile_no[:, :], pattern=[[ROWS, RT]], base=0, channel_multiplier=1,
                          allow_small_or_imprecise_dtypes=True).then_inc(consts, 1)
                pool.iota(step_no[:, :], pattern=[[P, RT]], base=0, channel_multiplier=1,
                          allow_small_or_imprecise_dtypes=True).then_inc(consts, 1)
                pool.wait_ge(tiles_known, 1)
                pool.wait_ge(table, 16)
                for c in range(RT):
                    pool.indirect_dma_start(
                        out=rows[:, c, :], out_offset=None, in_=m.edge_tab[:, :],
                        in_offset=bass.IndirectOffsetOnAxis(ap=edge_i[:, c:c + 1].bitcast(U32), axis=0),
                    ).then_inc(gathered, 16)

            @block.sync
            def _(sp):
                nonlocal n_loads
                sp.wait_ge(padded, 2)
                for t in range(RT):
                    full = rows_of(t)
                    first = t * ROWS
                    sp.dma_start(ei[0:full, t, 0:P],
                                 bass.AP(tensor=m.src.tensor, offset=first * P, ap=[[P, full], [1, P]])
                                 ).then_inc(loaded, 16)
                    lo = 1 if t == 0 else 0
                    sp.dma_start(ei[lo:full, t, P:ROW_E],
                                 bass.AP(tensor=m.dst.tensor, offset=(first + lo) * P - 1,
                                         ap=[[P, full - lo], [1, WIN]])).then_inc(loaded, 16)
                    n_loads += 2
                rest = E - (E // P) * P
                row = E // P - (RT - 1) * ROWS
                sp.dma_start(ei[0:1, 0, P + 1:ROW_E], m.dst[0:WIN - 1].rearrange("(a b) -> a b", a=1)).then_inc(loaded, 16)
                sp.dma_start(ei[row:row + 1, RT - 1, 0:rest], m.src[E - rest:E].rearrange("(a b) -> a b", a=1)
                             ).then_inc(loaded, 16)
                sp.dma_start(ei[row:row + 1, RT - 1, P:P + 1 + rest],
                             m.dst[E - rest - 1:E].rearrange("(a b) -> a b", a=1)).then_inc(loaded, 16)
                n_loads += 3
                sp.wait_ge(own, 1)
                sp.dma_start(m.edge_tab.rearrange("(t p) c -> p t c", p=ROWS), ef[:, :, :]).then_inc(table, 16)
                sp.wait_ge(fin_ready, 1)
                sp.dma_start(m.last_step.rearrange("(t p) -> p t", p=ROWS), fin[:, :]).then_inc(fin_moved, 16)
                sp.wait_ge(fin_moved, 16)
                sp.dma_start(fin_b[:, :], m.last_step.rearrange("(a b) -> a b", a=1).to_broadcast([P, ET_PAD])
                             ).then_inc(fin_moved, 16)
                sp.wait_ge(tiles_known, 1)
                sp.dma_start(m.step_node.rearrange("(c p) -> p c", p=P), node_i[:, :]).then_inc(stored, 16)
                sp.wait_ge(flags_made, 1)
                whole = STEPS // P
                part = STEPS - whole * P
                for k, t in ((None, dl), (0, flag), (1, flag)):
                    there = m.step_dl if k is None else m.step_flags[k]
                    here = t if k is None else t[:, k]
                    sp.dma_start(there[0:whole * P].rearrange("(c p) e -> p c e", p=P),
                                 here[:, 0:whole, :]).then_inc(stored, 16)
                    sp.dma_start(there[whole * P:STEPS], here[0:part, whole, :]).then_inc(stored, 16)
                sp.dma_start(m.step_cont.rearrange("(c p) -> p c", p=P), cont[:, :]).then_inc(stored, 16)
                sp.wait_ge(stored, 16 * 8)
                sp.dma_start(m.node_tab[:, :], m.step_node[0:STEPS].rearrange("(a b) -> a b", a=1)).then_inc(stored, 16)
                sp.dma_start(m.cont_dl[:, :], bass.AP(tensor=m.step_cont.tensor, offset=0,
                                                      ap=[[0, H1], [GROUP, BATCHES + 2]])).then_inc(stored, 16)
                sp.wait_ge(stored, 16 * 10)

            @block.vector
            def _(dve):
                me = Chain(dve, own)
                dve.wait_ge(loaded, 16 * n_loads)
                me.done(dve.tensor_copy(ef[:, :, :], ei[:, :, :]))
                me.wait()
                dve.wait_ge(consts, 8)
                me.done(dve.tensor_scalar(last[:, :], ef[:, :, ROW_E - 2], float(N - 1), None, ALU.min))
                me.wait()
                for t in range(RT):
                    me.done(dve.tensor_scalar(junk[0:ROWS, 0:NT - 1], bounds[0:ROWS, :], last[:, t:t + 1], None,
                                              ALU.is_le, ALU.add, accum_out=crossed[:, t:t + 1]))
                    me.wait()
                dve.tensor_tensor(fin[:, :], crossed[:, :], tile_no[:, :], ALU.add).then_inc(fin_ready, 1)
                dve.wait_ge(fin_moved, 32)
                for c in range(RT):
                    me.done(dve.tensor_scalar(junk[:, :], fin_b[:, :], step_no[:, c:c + 1], None,
                                              ALU.is_lt, ALU.add, accum_out=edge_t[:, c:c + 1]))
                    me.wait()
                me.done(dve.tensor_tensor(node_t[:, :], step_no[:, :], edge_t[:, :], ALU.subtract))
                me.done(dve.tensor_scalar(edge_i[:, :], edge_t[:, :], float(ET_PAD - 1), None, ALU.min))
                me.wait()
                me.done(dve.tensor_scalar(node_t[:, :], node_t[:, :], float(NT - 1), None, ALU.min))
                me.wait()
                me.done(dve.tensor_scalar(base[:, :], node_t[:, :], float(NODES_T), None, ALU.mult))
                me.wait()
                dve.tensor_copy(node_i[:, :], node_t[:, :]).then_inc(tiles_known, 1)
                dve.wait_ge(gathered, 16 * RT)
                mid = rows[:, :, P + 1:ROW_E - 1]
                for c in range(RT):
                    me.done(dve.tensor_scalar(dl[:, c, :], rows[:, c, P + 1:ROW_E - 1], base[:, c:c + 1], None,
                                              ALU.subtract))
                me.done(dve.tensor_tensor(edge[:, 0], mid, rows[:, :, P:ROW_E - 2], ALU.not_equal))
                me.done(dve.tensor_tensor(edge[:, 1], mid, rows[:, :, P + 2:ROW_E], ALU.not_equal))
                me.wait()
                me.done(dve.tensor_scalar(ge[:, :, :], dl[:, :, :], 0.0, None, ALU.is_ge))
                me.wait()
                me.done(dve.scalar_tensor_tensor(valid[:, :, :], dl[:, :, :], float(NODES_T - 1), ge[:, :, :],
                                                 ALU.is_le, ALU.mult))
                me.wait()
                for k in range(2):
                    me.done(dve.scalar_tensor_tensor(flag[:, k], edge[:, k], -BIG, valid[:, :, :],
                                                     ALU.mult, ALU.mult))
                me.done(dve.tensor_scalar(flag[:, 2], valid[:, :, :], 2 * BIG, -BIG, ALU.mult, ALU.add))
                me.done(dve.tensor_scalar(ge[:, :, 0], edge[:, 0, :, 0], -1.0, 1.0, ALU.mult, ALU.add))
                me.wait()
                me.done(dve.tensor_tensor(ge[:, :, 0], ge[:, :, 0], valid[:, :, 0], ALU.mult))
                me.wait()
                me.done(dve.scalar_tensor_tensor(cont[:, :], dl[:, :, 0], 1.0, ge[:, :, 0], ALU.add, ALU.mult))
                me.wait()
                dve.tensor_scalar(cont[:, :], cont[:, :], -1.0, None, ALU.add).then_inc(flags_made, 1)
                for q in range(3 * RT):
                    c = q // 3
                    w = min(P, STEPS - c * P)
                    there = (m.idx_all, m.dl_all, m.in_all)[q % 3][:, c * P:c * P + w]
                    dve.wait_ge(turned, q + 1)
                    dve.tensor_copy(there, tp[q % 4][:, 0:w]).then_inc(copied, 1)

            @block.tensor
            def _(pe):
                pe.wait_ge(consts, 8)
                pe.wait_ge(gathered, 16 * RT)
                pe.wait_ge(flags_made, 1)
                for q in range(3 * RT):
                    c = q // 3
                    w = min(P, STEPS - c * P)
                    if q >= 4:
                        pe.wait_ge(copied, q - 3)
                    pe.transpose(tp[q % 4][:, 0:w], (rows[0:w, c, 0:P], dl[0:w, c, :], flag[0:w, 2, c, :])[q % 3],
                                 m.ident[0:w, 0:w]).then_inc(turned, 1)


def fold_weights(nc, m):
    with ExitStack() as scope:
        names = ["fc1", "wb0", "fc2", "wb1"]
        raw = sb(nc, scope, "raw", [P, 2, 3 * D + 2 * D])
        wqkv = sb(nc, scope, "wqkv", [P, 2, 3 * D])
        att = sb(nc, scope, "att", [P, 2, 4])
        head_of = sb(nc, scope, "head_of", [P, 2, H1])
        mask = sb(nc, scope, "mask", [P, 2, H1])
        spread = sb(nc, scope, "spread", [P, 2, 2 * H1 + 2])
        tp = [ps(nc, scope, f"wt{k}") for k in range(4)]
        fp = [ps(nc, scope, f"wf{k}") for k in range(2)]
        loaded = m.sem("weights_loaded")
        iota_done = m.sem("weights_iota")
        turned = m.sem("weights_turned")
        copied = m.sem("weights_copied")
        own = m.sem("weights_dve")
        folded = m.sem("weights_folded")
        blocks = []
        for k, (dest, off) in enumerate([(m.w1e, 0), (m.wb0T, 0), (m.w2e, 0)]):
            for r in range(2):
                for c in range(2):
                    blocks.append((raw[:, r, k * D + c * P:k * D + c * P + P], dest[:, c, r * P:r * P + P]))
        for r in range(2):
            for c in range(4):
                blocks.append((raw[:, r, 3 * D + c * P:3 * D + c * P + P], m.wb1T[:, c, r * P:r * P + P]))
        for r in range(2):
            for c in range(2):
                blocks.append((wqkv[:, r, c * P:c * P + P], m.wqT[:, c, r * P:r * P + P]))
        loads = 0

        with nc.Block() as block:
            @block.sync
            def _(sp):
                nonlocal loads
                def load(to, frm):
                    nonlocal loads
                    sp.dma_start(to, frm).then_inc(loaded, 16)
                    loads += 1
                for k, name in enumerate(["L0_gnn_fc1_w", "L0_gnn_wb0", "L0_gnn_fc2_w"]):
                    load(raw[:, :, k * D:k * D + D], m.io[name].rearrange("(r p) c -> p r c", p=P))
                load(raw[:, :, 3 * D:5 * D], m.io["L0_gnn_wb1"].rearrange("(r p) c -> p r c", p=P))
                load(wqkv[:, :, :], m.io["L0_mix_w_qkv"].rearrange("(r p) c -> p r c", p=P))
                for k, name in enumerate(["L0_gnn_attn_l1", "L0_gnn_attn_r1", "L0_gnn_attn_l2", "L0_gnn_attn_r2"]):
                    load(att[:, :, k], m.io[name].rearrange("h d -> (h d)").rearrange("(r p) -> p r", p=P))
                for k, name in enumerate(["L0_gnn_bias1", "L0_gnn_bias2", "L0_ffn_gate_b"]):
                    w = EXPERTS if k == 2 else D
                    to = m.gate_bb[:, :] if k == 2 else m.bias_b[:, k, :]
                    load(to, m.io[name].rearrange("(a b) -> a b", a=1).to_broadcast([P, w]))
                for k, name in enumerate(["L0_gnn_bb0", "L0_gnn_bb1", "L0_mix_b_fc2"]):
                    load(m.brow[:, k, :], m.io[name].rearrange("(a b) -> a b", a=1))
                load(m.brow[:, 3:6, :], m.io["L0_mix_b_qkv"].rearrange("(a k b) -> a k b", a=1, k=3))
                load(m.gate_w[:, :, :], m.io["L0_ffn_gate_w"].rearrange("(r p) c -> p r c", p=P))
                sp.wait_ge(loaded, 16 * loads)

            @block.gpsimd
            def _(pool):
                pool.iota(head_of[:, :, :], pattern=[[P, 2], [-D1, H1]], base=0, channel_multiplier=1,
                          allow_small_or_imprecise_dtypes=True).then_inc(iota_done, 1)
                pool.memset(m.zeros[:, :], 0.0).then_inc(iota_done, 1)
                pool.memset(m.half[:, :], -0.5).then_inc(iota_done, 1)

            @block.tensor
            def _(pe):
                pe.wait_ge(loaded, 16 * loads)
                for q, (frm, _to) in enumerate(blocks):
                    if q >= 4:
                        pe.wait_ge(copied, q - 3)
                    pe.transpose(tp[q % 4][:, 0:P], frm, m.ident[:, :]).then_inc(turned, 1)
                pe.wait_ge(folded, 1)
                for k, (w, cols, c0) in enumerate([(0, 2 * H1, 0), (2, 2, 2 * H1)]):
                    for c in range(2):
                        for r in range(2):
                            ins = pe.matmul(fp[k][:, c * 32:c * 32 + cols], raw[:, r, w * D + c * P:w * D + c * P + P],
                                            spread[:, r, c0:c0 + cols], start=(r == 0), stop=(r == 1))
                ins.then_inc(folded, 1)

            @block.vector
            def _(dve):
                me = Chain(dve, own)
                dve.wait_ge(loaded, 16 * loads)
                dve.wait_ge(iota_done, 3)
                me.done(dve.tensor_scalar(mask[:, :, :], head_of[:, :, :], 0.0, None, ALU.is_ge))
                me.wait()
                me.done(dve.scalar_tensor_tensor(mask[:, :, :], head_of[:, :, :], float(D1 - 1), mask[:, :, :],
                                                 ALU.is_le, ALU.mult))
                me.wait()
                for r in range(2):
                    for k in range(2):
                        me.done(dve.tensor_scalar(spread[:, r, k * H1:k * H1 + H1], mask[:, r, :], att[:, r, k:k + 1],
                                                  None, ALU.mult))
                me.done(dve.tensor_copy(spread[:, :, 2 * H1:2 * H1 + 2], att[:, :, 2:4]))
                me.wait()
                dve.sem_inc(folded, 1)
                for q, (_frm, to) in enumerate(blocks):
                    dve.wait_ge(turned, q + 1)
                    dve.tensor_copy(to, tp[q % 4][:, 0:P]).then_inc(copied, 1)
                dve.wait_ge(folded, 2)
                for c in range(2):
                    me.done(dve.tensor_copy(m.w1e[:, c, D:D + 2 * H1], fp[0][:, c * 32:c * 32 + 2 * H1]))
                    me.done(dve.tensor_copy(m.w2e[:, c, D:D + 2], fp[1][:, c * 32:c * 32 + 2]))
                me.done(dve.tensor_copy(m.wkv[:, :, :], wqkv[:, :, D:3 * D]))
                me.wait()


def project_nodes(nc, m):
    with ExitStack() as scope:
        xt = sb(nc, scope, "xt", [NODES_T, 2, D])
        stats = sb(nc, scope, "stats", [NODES_T, 2, 6])
        mv = sb(nc, scope, "mv", [NODES_T, 2, 2])
        rstd = sb(nc, scope, "rstd", [NODES_T, 2])
        xn = sb(nc, scope, "xn", [NODES_T, 2, D + 1])
        xT = sb(nc, scope, "xT", [P, 2, 2, NODES_T])
        stage = sb(nc, scope, "stage", [NODES_T, 2, ROW1])
        skip = sb(nc, scope, "skip", [NODES_T, 2, 2, D])
        pT = [ps(nc, scope, f"pT{k}") for k in range(2)]
        pA = [ps(nc, scope, f"pA{k}") for k in range(2)]
        pZ = [ps(nc, scope, f"pZ{k}") for k in range(2)]
        pG = [ps(nc, scope, f"pG{k}") for k in range(2)]
        x_in = [m.sem(f"x_loaded{u}") for u in range(2)]
        x_used = m.sem("x_used")
        var_ready = m.sem("var_ready")
        rstd_ready = m.sem("rstd_ready")
        xn_ready = m.sem("xn_ready")
        xn_used = m.sem("xn_used")
        xT_done = m.sem("xT_done")
        xT_ready = m.sem("xT_ready")
        proj_done = m.sem("proj_done")
        proj_copied = m.sem("proj_copied")
        sent = [m.sem(f"proj_sent{u}") for u in range(2)]
        own = m.sem("proj_dve")
        base_ready = m.sem("proj_base")

        with nc.Block() as block:
            @block.sync
            def _(sp):
                with nc.sync.Fori(0, NT // 2) as i:
                    for u in range(2):
                        t = i * 2 + u
                        sp.wait_ge(x_used, t + 1)
                        sp.dma_start(xt[:, u, :], m.x[bass.ds(t * NODES_T, NODES_T), :]).then_inc(x_in[u], 16)
                    for u in range(2):
                        t = i * 2 + u
                        at = bass.ds(t * NODES_T, NODES_T)
                        sp.wait_ge(xn_ready, t + 1)
                        sp.dma_start(m.xn_d[at, :], xn[:, u, 0:D]).then_inc(sent[u], 16)
                        sp.wait_ge(xT_ready, t + 1)
                        sp.dma_start(m.xT_d[bass.ds(t * P, P), :], xT[:, u].rearrange("p c n -> p (c n)")).then_inc(sent[u], 16)
                        sp.wait_ge(proj_copied, t + 1)
                        sp.dma_start(m.tab1[at, :], stage[:, u, :]).then_inc(sent[u], 16)
                        sp.dma_start(m.z0_d[at, :], skip[:, u, 0, :]).then_inc(sent[u], 16)
                        sp.dma_start(m.z1_d[at, :], skip[:, u, 1, :]).then_inc(sent[u], 16)
                for u in range(2):
                    sp.wait_ge(sent[u], 16 * 5 * (NT // 2) + 80)

            @block.gpsimd
            def _(pool):
                pool.memset(xn[:, :, D:D + 1], 1.0).then_inc(base_ready, 1)
                for u in range(2):
                    pool.memset(stage[:, u, 0:H1 * (D1 + 1)], 1.0).then_inc(base_ready, 1)
                with nc.gpsimd.Fori(0, NT) as t:
                    pool.wait_ge(var_ready, t + 1)
                    pool.tensor_tensor(rstd[:, 0:1], mv[:, 0, 1:2], m.half[0:NODES_T, :], ALU.pow).then_inc(rstd_ready, 1)

            @block.vector
            def _(dve):
                dve.sem_inc(x_used, 2)
                dve.sem_inc(xn_used, 2)
                dve.sem_inc(sent[0], 80)
                dve.sem_inc(sent[1], 80)
                dve.wait_ge(base_ready, 3)
                with nc.vector.Fori(0, NT // 2) as i:
                    me = Chain(dve, own, i, 8)
                    for u in range(2):
                        t = i * 2 + u
                        dve.wait_ge(x_in[u], 16 * i + 16)
                        me.done(dve.bn_stats(stats[:, u, :], xt[:, u, :]))
                        me.wait_apart(m.hold)
                        me.done(dve.bn_aggr(mv[:, 1, :], stats[:, u, :]))
                        me.wait()
                        dve.tensor_scalar(mv[:, 0, 1:2], mv[:, 1, 1:2], EPS, None, ALU.add).then_inc(var_ready, 1)
                        dve.wait_ge(rstd_ready, t + 1)
                        dve.wait_ge(xn_used, t + 1)
                        dve.wait_ge(sent[u], 80 * i + 80)
                        me.done(dve.tensor_scalar(xn[:, u, 0:D], xt[:, u, :], mv[:, 1, 0:1], rstd[:, 0:1],
                                                  ALU.subtract, ALU.mult))
                        me.wait()
                        dve.sem_inc(xn_ready, 1)
                        me.done(dve.tensor_copy(mv[:, 0, 0:1], mv[:, 1, 0:1]))
                        dve.sem_inc(x_used, 1)
                    me.close()

            @block.tensor
            def _(pe):
                for c in range(2):
                    pe.matmul(pG[c][:, 0:D + 1], m.zeros[:, 0:P], m.zeros[:, 0:D + 1], start=True, stop=False,
                              skip_group_check=True)
                with nc.tensor.Fori(0, NT // 2) as i:
                    for u in range(2):
                        t = i * 2 + u
                        pe.wait_ge(xn_ready, t + 1)
                        for c in range(2):
                            ins = pe.transpose(pT[u][:, c * NODES_T:(c + 1) * NODES_T], xn[:, u, c * P:c * P + P],
                                               m.ident[0:NODES_T, 0:NODES_T])
                        ins.then_inc(xT_done, 1)
                        for c in range(2):
                            ins = pe.matmul(pG[c][:, 0:D + 1], xn[:, u, c * P:c * P + P], xn[:, u, :], start=False,
                                            stop=False, skip_group_check=True)
                        ins.then_inc(xn_used, 1)
                        pe.wait_ge(xT_ready, t + 1)
                        for c in range(2):
                            pe.matmul(pA[u][0:NODES_T, 0:D + 16], xT[:, u, c, :], m.w1e[:, c, :],
                                      start=(c == 0), stop=(c == 1))
                        for k, w in enumerate((m.wb0T, m.wb1T)):
                            at = pZ[u][0:NODES_T, k * D:k * D + D]
                            for c in range(2):
                                pe.matmul(at, xT[:, u, c, :], w[:, c, :], start=(c == 0), stop=False)
                            ins = pe.matmul(at, m.ones[0:1, 0:NODES_T], m.brow[:, k, :], start=False, stop=True)
                        ins.then_inc(proj_done, 1)

            @block.scalar
            def _(act):
                with nc.scalar.Fori(0, NT // 2) as i:
                    for u in range(2):
                        t = i * 2 + u
                        act.wait_ge(xT_done, t + 1)
                        act.copy(xT[:, u].rearrange("p c n -> p (c n)"), pT[u][:, 0:2 * NODES_T]).then_inc(xT_ready, 1)
                        act.wait_ge(proj_done, t + 1)
                        act.copy(stage[:, u, 0:H1 * (D1 + 1)].rearrange("p (h c) -> p h c", h=H1)[:, :, 0:D1],
                                 pA[u][0:NODES_T, 0:D].rearrange("p (h c) -> p h c", h=H1)).then_inc(m.act_own, 1)
                        act.copy(stage[:, u, H1 * (D1 + 1):], pA[u][0:NODES_T, D:D + H1]).then_inc(m.act_own, 1)
                        act.copy(m.er1[:, bass.ds(t, 1), :], pA[u][0:NODES_T, D + H1:D + 2 * H1].rearrange("p (a h) -> p a h", a=1)).then_inc(m.act_own, 1)
                        act.copy(skip[:, u].rearrange("p k d -> p (k d)"), pZ[u][0:NODES_T, :]).then_inc(m.act_own, 1)
                        act.wait_ge(m.act_own, t * 4 + 4)
                        act.sem_inc(proj_copied, 1)

        with nc.Block() as block:
            @block.vector
            def _(dve):
                for c in range(2):
                    dve.tensor_copy(m.gram[:, c, :], pG[c][:, 0:D + 1]).then_inc(m.gram_ready, 1)
                dve.wait_ge(m.gram_ready, 2)


def mixer_attention(nc, m):
    with ExitStack() as scope:
        G = m.gram
        srow = sb(nc, scope, "srow", [1, D])
        U = sb(nc, scope, "U", [P, 2, D])
        u0 = sb(nc, scope, "u0", [1, D])
        nrow = sb(nc, scope, "nrow", [1, 1])
        bqT = sb(nc, scope, "bqT", [P, 2])
        L = sb(nc, scope, "L", [P, 2, 64])
        mx = sb(nc, scope, "mx", [P, 2])
        sm = sb(nc, scope, "sm", [P, 2])
        BD = sb(nc, scope, "BD", [P, 2, P])
        BDT = sb(nc, scope, "BDT", [P, 2, P])
        pb = [ps(nc, scope, f"mp{k}") for k in range(6)]
        w1n = sb(nc, scope, "w1n", [P, 2, 1])
        own = m.sem("mix_dve")
        pe_done = m.sem("mix_pe")
        act_done = m.sem("mix_act")
        loaded = m.sem("mix_loaded")
        bq, bk, bv = m.brow[:, 3, :], m.brow[:, 4, :], m.brow[:, 5, :]
        Wk, Wv = m.wkv[:, :, 0:D], m.wkv[:, :, D:2 * D]
        flat = lambda name: m.io[name].rearrange("(r p) -> p r", p=P)

        with nc.Block() as block:
            @block.sync
            def _(sp):
                sp.dma_start(m.wf1[:, :, :], m.io["L0_mix_w_fc1"].rearrange("(r p) c -> p r c", p=P)).then_inc(loaded, 16)
                sp.dma_start(m.wf2[:, :, :], m.io["L0_mix_w_fc2"].rearrange("(r p) c -> p r c", p=P)).then_inc(loaded, 16)
                sp.dma_start(m.gain[:, :], flat("L0_mix_norm_g")).then_inc(loaded, 16)
                sp.dma_start(m.shift[:, :], flat("L0_mix_norm_b")).then_inc(loaded, 16)
                sp.dma_start(m.b1col[:, :], m.io["L0_mix_b_fc1"].rearrange("(r p) -> p r", p=P)).then_inc(loaded, 16)
                sp.dma_start(bqT[:, :], m.io["L0_mix_b_qkv"][0:D].rearrange("(r p) -> p r", p=P)).then_inc(loaded, 16)
                sp.wait_ge(loaded, 96)

            @block.tensor
            def _(pe):
                for c in range(2):
                    ins = pe.transpose(pb[0][0:1, c * P:c * P + P], G[:, c, D:D + 1], m.ident[:, :])
                ins.then_inc(pe_done, 1)
                pe.wait_ge(own, 1)
                for c in range(2):
                    for r in range(2):
                        pe.matmul(pb[1 + c][:, 0:D], G[:, r, c * P:c * P + P], Wv[:, r, :], start=(r == 0), stop=False)
                    pe.matmul(pb[1 + c][:, 0:D], srow[:, c * P:c * P + P], bv, start=False, stop=True)
                for r in range(2):
                    pe.matmul(pb[3][0:1, 0:D], G[:, r, D:D + 1], Wv[:, r, :], start=(r == 0), stop=False)
                pe.wait_ge(own, 2)
                pe.matmul(pb[3][0:1, 0:D], nrow[:, :], bv, start=False, stop=True).then_inc(pe_done, 1)
                pe.wait_ge(own, 5)
                for c in range(2):
                    for r in range(2):
                        pe.matmul(pb[4 + c][:, 0:D], Wk[:, r, c * P:c * P + P], U[:, r, :], start=(r == 0), stop=False)
                    ins = pe.matmul(pb[4 + c][:, 0:D], bk[:, c * P:c * P + P], u0[:, :], start=False, stop=True)
                ins.then_inc(pe_done, 1)
                pe.wait_ge(loaded, 96)
                for q in range(6):
                    for r in range(2):
                        ins = pe.matmul(pb[0][:, 256 + q:257 + q], m.wf1[:, r, q * P:q * P + P], m.shift[:, r:r + 1],
                                        start=(r == 0), stop=(r == 1))
                ins.then_inc(pe_done, 1)
                pe.wait_ge(m.mix_bd, 1)
                for c in range(2):
                    ins = pe.transpose(pb[1][:, c * P:c * P + P], BD[:, c, :], m.ident[:, :])
                ins.then_inc(pe_done, 1)
                pe.wait_ge(m.mix_bd, 3)
                for c in range(2):
                    for r in range(2):
                        pe.matmul(pb[2 + r][:, c * P:c * P + P], m.wqT[:, c, r * P:r * P + P], BDT[:, c, :],
                                  start=True, stop=True)
                    ins = pe.matmul(pb[4][0:1, c * P:c * P + P], bqT[:, c:c + 1], BDT[:, c, :], start=True, stop=True)
                ins.then_inc(pe_done, 1)

            @block.vector
            def _(dve):
                me = Chain(dve, own)
                dve.wait_ge(pe_done, 1)
                me.done(dve.tensor_copy(srow[:, :], pb[0][0:1, 0:D]))
                me.done(dve.memset(nrow[:, :], float(N)))
                dve.wait_ge(pe_done, 2)
                for c in range(2):
                    me.done(dve.tensor_copy(U[:, c, :], pb[1 + c][:, 0:D]))
                me.done(dve.tensor_copy(u0[:, :], pb[3][0:1, 0:D]))
                me.done(dve.memset(BD[:, :, :], 0.0))
                dve.wait_ge(pe_done, 3)
                for c in range(2):
                    for h in range(2):
                        lo = 64 * h
                        me.done(dve.tensor_scalar(L[lo:lo + 64, c, :],
                                                  pb[4 + c][lo:lo + 64, (2 * c + h) * 64:(2 * c + h + 1) * 64],
                                                  64.0 ** -0.5, None, ALU.mult))
                me.wait()
                me.done(dve.tensor_reduce(mx[:, :], L[:, :, :], AX, ALU.max))
                me.wait()
                me.done(dve.tensor_scalar(mx[:, :], mx[:, :], -1.0, None, ALU.mult))
                me.wait()
                dve.sem_inc(m.mix_max, 1)
                dve.wait_ge(act_done, 2)
                me.done(dve.reciprocal(sm[:, :], sm[:, :]))
                me.wait()
                for c in range(2):
                    for h in range(2):
                        lo = 64 * h
                        me.done(dve.tensor_scalar(BD[lo:lo + 64, c, lo:lo + 64], L[lo:lo + 64, c, :],
                                                  sm[lo:lo + 64, c:c + 1], None, ALU.mult))
                me.wait()
                dve.sem_inc(m.mix_bd, 1)
                dve.wait_ge(pe_done, 5)
                for c in range(2):
                    dve.tensor_copy(BDT[:, c, :], pb[1][:, c * P:c * P + P]).then_inc(m.mix_bd, 1)
                me.done(dve.tensor_tensor(m.b1col[:, :], m.b1col[:, :], pb[0][:, 256:262], ALU.add))
                for r in range(2):
                    me.done(dve.tensor_scalar(m.wf1[:, r, :], m.wf1[:, r, :], m.gain[:, r:r + 1], None, ALU.mult))
                dve.wait_ge(pe_done, 6)
                for r in range(2):
                    me.done(dve.tensor_copy(m.wx[:, r, :], pb[2 + r][:, 0:D]))
                me.done(dve.tensor_copy(m.brow[:, 3, :], pb[4][0:1, 0:D]))
                me.wait()

            @block.scalar
            def _(act):
                act.wait_ge(m.mix_max, 1)
                for c in range(2):
                    act.activation(L[:, c, :], L[:, c, :], ACT.Exp, bias=mx[:, c:c + 1],
                                   accum_out=sm[:, c:c + 1]).then_inc(act_done, 1)


def mixer(nc, m):
    W = 2 * NODES_T
    with ExitStack() as scope:
        xn = sb(nc, scope, "mxn", [NODES_T, 2, 2, D])
        xT = sb(nc, scope, "mxT", [P, 2, 2, W])
        r = sb(nc, scope, "mr", [NODES_T, 2, 2, D])
        hn = sb(nc, scope, "mhn", [NODES_T, 2, D])
        stats = sb(nc, scope, "mstats", [NODES_T, 2, 6])
        mv = sb(nc, scope, "mmv", [NODES_T, 2, 2])
        var = sb(nc, scope, "mvar", [NODES_T, 2])
        rstd = sb(nc, scope, "mrstd", [NODES_T, 2])
        hT = sb(nc, scope, "mhT", [P, 2, W])
        gT = sb(nc, scope, "mgT", [P, 6, W])
        o = sb(nc, scope, "mo", [NODES_T, 2, 2, D])
        pX = ps(nc, scope, "pX")
        pH = ps(nc, scope, "pH")
        pF = [ps(nc, scope, f"pF{k}") for k in range(4)]
        pY = ps(nc, scope, "pY")
        inn = [m.sem(f"mix_in{u}") for u in range(2)]
        used = m.sem("mix_in_used")
        xf_done = m.sem("xf_done")
        var_ready = m.sem("mix_var")
        rstd_ready = m.sem("mix_rstd")
        hn_ready = m.sem("hn_ready")
        hT_done = m.sem("hT_done")
        hT_ready = m.sem("hT_ready")
        fc1_done = m.sem("fc1_done")
        gelu_done = m.sem("gelu_done")
        fc2_done = m.sem("fc2_done")
        out_ready = m.sem("mix_out_ready")
        sent = [m.sem(f"mix_sent{u}") for u in range(2)]
        own = m.sem("mixer_dve")
        pairs = NT // 2

        def both(eng, body):
            with eng.Fori(0, pairs // 2) as i:
                for u in range(2):
                    body(i * 2 + u, u, i)
            if pairs % 2:
                body(pairs - 1, 0, pairs // 2)

        with nc.Block() as block:
            @block.sync
            def _(sp):
                def turn(p, u, i):
                    at = bass.ds(p * W, W)
                    sp.wait_ge(used, p + 1)
                    sp.dma_start(xn[:, u], m.xn_d[at, :].rearrange("(k p) d -> p k d", p=NODES_T)).then_inc(inn[u], 16)
                    sp.dma_start(xT[:, u], m.xT_d[bass.ds(p * 2 * P, 2 * P), :].rearrange("(k p) d -> p k d", p=P)
                                 ).then_inc(inn[u], 16)
                both(nc.sync, turn)

            @block.gpsimd
            def _(pool):
                def turn(p, u, i):
                    pool.wait_ge(var_ready, p + 1)
                    pool.tensor_tensor(rstd[:, :], var[:, :], m.half[0:NODES_T, :].to_broadcast([NODES_T, 2]), ALU.pow).then_inc(rstd_ready, 1)
                both(nc.gpsimd, turn)

            @block.vector
            def _(dve):
                dve.sem_inc(used, 2)
                for u in range(2):
                    dve.sem_inc(sent[u], 16)

                def turn(p, u, i):
                    me = Chain(dve, own, p, 10)
                    dve.wait_ge(xf_done, p + 1)
                    me.done(dve.tensor_tensor(r[:, u].rearrange("p k d -> p (k d)"), xn[:, u].rearrange("p k d -> p (k d)"),
                                              pX[0:NODES_T, :], ALU.add))
                    me.wait()
                    dve.sem_inc(used, 1)
                    for k in range(2):
                        me.done(dve.bn_stats(stats[:, k, :], r[:, u, k, :]))
                    me.wait_apart(m.hold)
                    for k in range(2):
                        me.done(dve.bn_aggr(mv[:, k, :], stats[:, k, :]))
                    me.wait()
                    me.done(dve.tensor_scalar(var[:, :], mv[:, :, 1], EPS, None, ALU.add))
                    me.wait()
                    dve.sem_inc(var_ready, 1)
                    dve.wait_ge(rstd_ready, p + 1)
                    for k in range(2):
                        me.done(dve.tensor_scalar(hn[:, k, :], r[:, u, k, :], mv[:, k, 0:1], rstd[:, k:k + 1],
                                                  ALU.subtract, ALU.mult))
                    me.wait()
                    dve.sem_inc(hn_ready, 1)
                    dve.wait_ge(fc2_done, p + 1)
                    dve.wait_ge(sent[u], 16 * i + 16)
                    me.done(dve.tensor_tensor(o[:, u].rearrange("p k d -> p (k d)"), r[:, u].rearrange("p k d -> p (k d)"),
                                              pY[0:NODES_T, :], ALU.add))
                    me.wait()
                    me.done(dve.tensor_copy(mv[:, 0, 0:1], mv[:, 1, 0:1]))
                    dve.sem_inc(out_ready, 1)
                    me.close()
                both(nc.vector, turn)

            @block.tensor
            def _(pe):
                def turn(p, u, i):
                    pe.wait_ge(inn[u], 32 * i + 32)
                    for k in range(2):
                        at = pX[0:NODES_T, k * D:k * D + D]
                        for c in range(2):
                            pe.matmul(at, xT[:, u, k, c * NODES_T:(c + 1) * NODES_T], m.wx[:, c, :], start=(c == 0), stop=False)
                        ins = pe.matmul(at, m.ones[0:1, 0:NODES_T], m.brow[:, 3, :], start=False, stop=True)
                    ins.then_inc(xf_done, 1)
                    pe.wait_ge(hn_ready, p + 1)
                    for c in range(2):
                        for k in range(2):
                            ins = pe.transpose(pH[:, c * W + k * NODES_T:c * W + (k + 1) * NODES_T],
                                               hn[:, k, c * P:c * P + P], m.ident[0:NODES_T, 0:NODES_T])
                    ins.then_inc(hT_done, 1)
                    pe.wait_ge(hT_ready, p + 1)
                    for q in range(6):
                        if q >= 4:
                            pe.wait_ge(gelu_done, p * 6 + (q - 3))
                        for c in range(2):
                            ins = pe.matmul(pF[q % 4][:, 0:W], m.wf1[:, c, q * P:q * P + P], hT[:, c, :],
                                            start=(c == 0), stop=(c == 1))
                        ins.then_inc(fc1_done, 1)
                    pe.wait_ge(gelu_done, p * 6 + 6)
                    for k in range(2):
                        at = pY[0:NODES_T, k * D:k * D + D]
                        for q in range(6):
                            pe.matmul(at, gT[:, q, k * NODES_T:(k + 1) * NODES_T], m.wf2[:, q, :], start=(q == 0), stop=False)
                        ins = pe.matmul(at, m.ones[0:1, 0:NODES_T], m.brow[:, 2, :], start=False, stop=True)
                    ins.then_inc(fc2_done, 1)
                both(nc.tensor, turn)

            @block.scalar
            def _(act):
                def turn(p, u, i):
                    act.wait_ge(hT_done, p + 1)
                    act.copy(hT[:, :, :].rearrange("p c n -> p (c n)"), pH[:, 0:2 * W]).then_inc(hT_ready, 1)
                    for q in range(6):
                        act.wait_ge(fc1_done, p * 6 + (q + 1))
                        act.activation(gT[:, q, :], pF[q % 4][:, 0:W], ACT.Gelu, bias=m.b1col[:, q:q + 1]
                                       ).then_inc(gelu_done, 1)
                    act.wait_ge(out_ready, p + 1)
                    act.dma_start(m.mix_d[bass.ds(p * W, W), :].rearrange("(k p) d -> p k d", p=NODES_T), o[:, u]
                                  ).then_inc(sent[u], 16)
                both(nc.scalar, turn)
                act.wait_ge(sent[0], 16 * (pairs - pairs // 2) + 16)
                act.wait_ge(sent[1], 16 * (pairs // 2) + 16)


def convolve(nc, m, name, heads, width, table, er, acc, degree):
    H, C = heads, width + 1
    W = H * C + (1 if degree else 0)
    ROW = H * C + H
    folded = H == 1
    with ExitStack() as scope:
        def t(n, shape, dt=F32):
            return sb(nc, scope, f"{name}_{n}", shape, dt)

        idx = t("idx", [P, UNROLL, GROUP], I32)
        rows = t("rows", [P, UNROLL, GROUP, ROW])
        dl_b = t("dl_b", [NODES_T, 2, GE])
        flags = t("flags", [H, 2, 2, GE])
        hotT = t("hotT", [NODES_T, GE], BF16)
        hot = t("hot", [P, 2, GROUP, NODES_T])
        parts = t("parts", [NODES_T, NT, 3, H], BF16)
        rest = t("rest", [NODES_T, 2, NT, H])
        er_s = t("er_s", [NODES_T, 2, GROUP, 3, H], BF16)
        z = t("z", [P, GROUP, H])
        lz = t("lz", [P, GROUP, H])
        fw = t("fw", [H, GE])
        bw = t("bw", [H, GE])
        carry = t("carry", [H, 1])
        fall = t("fall", [H, 1])
        ln_scale = t("ln_scale", [H, NODES_T])
        scale = t("scale", [NODES_T, H])
        ex = t("ex", [P, GROUP, H])
        wr = t("wr", [P, GROUP, W]) if not folded else None
        pE = ps(nc, scope, f"{name}_pE")
        pT = ps(nc, scope, f"{name}_pT", (P, GE))
        pB = ps(nc, scope, f"{name}_pB")
        pA = [ps(nc, scope, f"{name}_pA{k}") for k in range(4)]
        s = lambda n: m.sem(f"{name}_{n}")
        loaded = [s(f"flags_in{u}") for u in range(2)]
        gathered = [s(f"rows_in{u}") for u in range(UNROLL)]
        idx_ready, rows_used, scans_done = s("idx_ready"), s("rows_used"), s("scans_done")
        hotT_ready, er_ready, er_done = s("hotT_ready"), s("er_ready"), s("er_done")
        lz_ready, lzT_done, c_back = s("lz_ready"), s("lzT_done"), s("c_back")
        sel_ready, sel_done, scale_ready = s("sel_ready"), s("sel_done"), s("scale_ready")
        t_ready, ex_ready, wr_ready = s("t_ready"), s("ex_ready"), s("wr_ready")
        agg_done, add_done, own, parts_ready = s("agg_done"), s("add_done"), s("own"), s("parts_ready")

        def turns(eng, body):
            with eng.Fori(0, BATCHES // UNROLL) as i:
                for u in range(UNROLL):
                    body(i * UNROLL + u, u, i)

        def after(u, i, ring, ahead=1):
            n = u + ahead
            return n % ring, i * (UNROLL // ring) + n // ring

        with nc.Block() as block:
            @block.sync
            def _(sp):
                def load(n, u):
                    sp.dma_start(dl_b[:, u, :],
                                 m.step_dl[bass.ds(n * GROUP, GROUP), :].rearrange("(a s) e -> a (s e)", a=1)
                                 .to_broadcast([NODES_T, GE])).then_inc(loaded[u], 16)
                    for k in range(2):
                        sp.dma_start(flags[:, u, k, :],
                                     m.step_flags[k, bass.ds(n * GROUP, GROUP), :].rearrange("(a s) e -> a (s e)", a=1)
                                     .to_broadcast([H, GE])).then_inc(loaded[u], 16)

                def turn(b, u, i):
                    sp.wait_ge(scans_done, b + 1)
                    load(b + 2, u % 2)
                load(0, 0)
                load(1, 1)
                turns(nc.sync, turn)

            @block.gpsimd
            def _(pool):
                def gather(n, u):
                    pool.wait_ge(rows_used, n + 1)
                    pool.sem_inc(m.hold, 1)
                    pool.tensor_copy(idx[:, u, :], m.idx_all[:, bass.ds(n * GROUP, GROUP)]).then_inc(idx_ready, 1)
                    pool.wait_ge(idx_ready, n + 1)
                    pool.sem_inc(m.hold, 1)
                    for k in range(GROUP):
                        pool.indirect_dma_start(
                            out=rows[:, u, k, :], out_offset=None, in_=table[:, :],
                            in_offset=bass.IndirectOffsetOnAxis(ap=idx[:, u, k:k + 1].bitcast(U32), axis=0),
                        ).then_inc(gathered[u], 16)
                gather(0, 0)
                turns(nc.gpsimd, lambda b, u, i: gather(b + 1, (u + 1) % UNROLL))

            @block.scalar
            def _(act):
                regs = [act.alloc_register(f"{name}_act{k}") for k in range(UNROLL * GROUP)]

                def take_er(par, lot):
                    for k in range(GROUP):
                        j = act.snap(lot[k], min_val=0, max_val=NT - 1)
                        act.copy(er_s[:, par, k:k + 1].rearrange("p a c h -> p a (c h)"),
                                 parts[:, bass.ds(j, 1)].rearrange("p a c h -> p a (c h)")).then_inc(er_ready, 1)

                def exps(n):
                    act.wait_ge(sel_done, n + 1)
                    act.activation(scale[:, :], pE[0:NODES_T, 256:256 + H], ACT.Exp).then_inc(scale_ready, 1)
                    act.wait_ge(t_ready, n + 1)
                    act.activation(ex[:, :, :], z[:, :, :], ACT.Exp).then_inc(ex_ready, 1)

                def turn(b, u, i):
                    if u == 0:
                        act.load(regs, m.node_tab[0:1, bass.ds(i * (UNROLL * GROUP) + 2 * GROUP, UNROLL * GROUP)])
                    exps(b + 1)
                    take_er(u % 2, regs[u * GROUP:(u + 1) * GROUP])
                act.wait_ge(parts_ready, 1)
                act.load(regs[0:2 * GROUP], m.node_tab[0:1, 0:2 * GROUP])
                take_er(0, regs[0:GROUP])
                exps(0)
                take_er(1, regs[GROUP:2 * GROUP])
                turns(nc.scalar, turn)

            @block.vector
            def _(dve):
                regs = [dve.alloc_register(f"{name}_dve{k}") for k in range(UNROLL * GROUP)]

                def one_hot_nodes(n, par, fill):
                    dve.wait_ge(loaded[par], fill * 48 + 48)
                    dve.tensor_scalar(hotT[:, :], dl_b[:, par, :], m.lane[0:NODES_T, :], None, ALU.is_equal
                                      ).then_inc(hotT_ready, 1)

                def one_hot_edges(me, n, par):
                    if not folded:
                        me.done(dve.tensor_tensor(hot[:, par], 
                                                  m.dl_all[:, bass.ds(n * GROUP, GROUP)].rearrange("p (k a) -> p k a", a=1)
                                                  .to_broadcast([P, GROUP, NODES_T]),
                                                  m.iota[:, :].rearrange("p (a n) -> p a n", a=1)
                                                  .to_broadcast([P, GROUP, NODES_T]), ALU.is_equal))

                def edge_logits(me, n, q, fill):
                    dve.wait_ge(er_done, n + 1)
                    dve.wait_ge(gathered[q], fill * (16 * GROUP) + 16 * GROUP)
                    me.done(dve.tensor_tensor(z[:, :, :], rows[:, q, :, H * C:ROW],
                                              pE[:, 0:GROUP * H].rearrange("p (k h) -> p k h", k=GROUP), ALU.add))
                    yield
                    me.wait()
                    me.done(dve.scalar_tensor_tensor(lz[:, :, :], z[:, :, :], 0.2, z[:, :, :], ALU.mult, ALU.max))
                    yield
                    me.wait()
                    dve.tensor_tensor(lz[:, :, :], lz[:, :, :],
                                      m.in_all[:, bass.ds(n * GROUP, GROUP)].rearrange("p (k a) -> p k a", a=1)
                                      .to_broadcast([P, GROUP, H]), ALU.min).then_inc(lz_ready, 1)

                def forward_max(me, n, par):
                    dve.wait_ge(lzT_done, n + 1)
                    me.forward = me.done(dve.tensor_tensor_scan(fw[:, :], flags[:, par, 0, :], pT[0:H, :], carry[:, 0:1],
                                                                ALU.add, ALU.max))

                def backward_max(me, n, par):
                    me.wait(me.forward)
                    dve.tensor_tensor_scan(bw[:, ::-1], flags[:, par, 1, ::-1], fw[:, ::-1], -BIG, ALU.add, ALU.max
                                           ).then_inc(scans_done, 1)

                def carry_over(me, n):
                    dve.wait_ge(scans_done, n + 1)
                    me.fell = me.done(dve.tensor_tensor(fall[:, :], carry[:, :], bw[:, 0:1], ALU.subtract))

                def carry_scale(me, n):
                    me.wait(me.fell)
                    dve.tensor_scalar(ln_scale[:, :], m.iota[0:H, :], m.cont_dl[0:H, bass.ds(n, 1)], fall[:, 0:1],
                                      ALU.is_equal, ALU.mult).then_inc(sel_ready, 1)
                    me.done(dve.tensor_copy(carry[:, :], fw[:, GE - 1:GE]))

                def running_max(me, n, par):
                    forward_max(me, n, par)
                    backward_max(me, n, par)
                    carry_over(me, n)
                    carry_scale(me, n)

                def shifted(n):
                    dve.wait_ge(c_back, n + 1)
                    dve.tensor_tensor(z[:, :, :], lz[:, :, :],
                                      pB[:, 0:GROUP * H].rearrange("p (k h) -> p k h", k=GROUP), ALU.subtract
                                      ).then_inc(t_ready, 1)

                def weighted(b, u):
                    dve.wait_ge(ex_ready, b + 1)
                    if folded:
                        for k in range(GROUP):
                            ins = dve.tensor_scalar(hot[:, 0, k, :], m.iota[:, :], m.dl_all[:, bass.ds(b * GROUP + k, 1)],
                                                    ex[:, k, :], ALU.is_equal, ALU.mult)
                            ins.then_inc(wr_ready, 1)
                    else:
                        dve.tensor_tensor(wr[:, :, 0:H * C].rearrange("p k (h c) -> p k h c", h=H),
                                          rows[:, u, :, 0:H * C].rearrange("p k (h c) -> p k h c", h=H),
                                          ex[:, :, :].rearrange("p k (h a) -> p k h a", a=1)
                                          .to_broadcast([P, GROUP, H, C]), ALU.mult).then_inc(wr_ready, 1)

                start = Chain(dve, own)
                for given, n in ((rows_used, UNROLL), (add_done, 4)):
                    dve.sem_inc(given, n)
                start.done(dve.memset(acc[:, :, :], 0.0))
                start.done(dve.memset(carry[:, :], -BIG))
                if degree:
                    start.done(dve.memset(wr[:, :, W - 1:W], 1.0))
                left = er[:, :, :]
                for k in range(3):
                    start.done(dve.tensor_copy(parts[:, :, k, :], left))
                    start.wait()
                    if k < 2:
                        start.done(dve.tensor_tensor(rest[:, k], left, parts[:, :, k, :], ALU.subtract))
                        start.wait()
                        left = rest[:, k]
                dve.sem_inc(parts_ready, 1)
                one_hot_nodes(0, 0, 0)
                one_hot_edges(start, 0, 0)
                for _ in edge_logits(start, 0, 0, 0):
                    pass
                running_max(start, 0, 0)
                one_hot_nodes(1, 1, 0)
                shifted(0)
                start.wait()

                def turn(b, u, i):
                    me = Chain(dve, own, b, 6 if folded else 7, start.n)
                    if u == 0:
                        dve.load(regs, m.node_tab[0:1, bass.ds(i * (UNROLL * GROUP), UNROLL * GROUP)])
                    nodes = [dve.snap(r, min_val=0, max_val=NT - 1) for r in regs[u * GROUP:(u + 1) * GROUP]]
                    par, _fill = after(u, i, 2)
                    q, qfill = after(u, i, UNROLL)

                    def add(k):
                        part = acc[:, bass.ds(nodes[k], 1), 0:W]
                        if k == 0:
                            me.wait(scaled)
                        else:
                            dve.wait_ge(add_done, b * GROUP + (k + 4))
                        dve.wait_ge(agg_done, b * GROUP + (k + 1))
                        dve.tensor_tensor(part, part, pA[k % 4][0:NODES_T, 0:W].rearrange("p (a c) -> p a c", a=1),
                                          ALU.add).then_inc(add_done, 1)

                    weighted(b, u)
                    one_hot_edges(me, b + 1, par)
                    logits = edge_logits(me, b + 1, q, qfill)
                    next(logits)
                    part = acc[:, bass.ds(nodes[0], 1), 0:H * C].rearrange("p a (h c) -> p (a h) c", h=H)
                    dve.wait_ge(add_done, b * GROUP + 4)
                    dve.wait_ge(scale_ready, b + 1)
                    scaled = me.done(dve.tensor_tensor(part, part, scale[:, :].rearrange("p (h a) -> p h a", a=1)
                                                       .to_broadcast([NODES_T, H, C]), ALU.mult))
                    next(logits)
                    add(0)
                    for _ in logits:
                        pass
                    if not folded:
                        dve.wait_ge(wr_ready, b + 1)
                        dve.sem_inc(rows_used, 1)
                    add(1)
                    add(2)
                    forward_max(me, b + 1, par)
                    add(3)
                    backward_max(me, b + 1, par)
                    add(4)
                    carry_over(me, b + 1)
                    add(5)
                    carry_scale(me, b + 1)
                    add(6)
                    one_hot_nodes(b + 2, *after(u, i, 2, 2))
                    shifted(b + 1)
                    add(7)
                    if folded:
                        dve.sem_inc(rows_used, 1)
                    me.close()
                turns(nc.vector, turn)

            @block.tensor
            def _(pe):
                def spread_er(n, par):
                    pe.wait_ge(hotT_ready, n + 1)
                    pe.wait_ge(er_ready, n * GROUP + GROUP)
                    for k in range(GROUP):
                        for c in range(3):
                            ins = pe.matmul(pE[:, k * H:(k + 1) * H], hotT[:, k * P:(k + 1) * P], er_s[:, par, k, c, :],
                                            start=(c == 0), stop=(c == 2))
                    ins.then_inc(er_done, 1)

                def turn_logits(n):
                    pe.wait_ge(lz_ready, n + 1)
                    for k in range(GROUP):
                        ins = pe.transpose(pT[0:H, k * P:(k + 1) * P], lz[:, k, :], m.ident[:, :])
                    ins.then_inc(lzT_done, 1)

                def turn_max(n):
                    pe.wait_ge(scans_done, n + 1)
                    pe.sem_inc(m.hold, 1)
                    for k in range(GROUP):
                        ins = pe.transpose(pB[:, k * H:(k + 1) * H], bw[:, k * P:(k + 1) * P], m.ident[0:H, 0:H])
                    ins.then_inc(c_back, 1)
                    pe.wait_ge(sel_ready, n + 1)
                    pe.matmul(pE[0:NODES_T, 256:256 + H], ln_scale[:, :], m.ident[0:H, 0:H], start=True, stop=True
                              ).then_inc(sel_done, 1)

                def sum_step(b, u, k):
                    if folded:
                        pe.wait_ge(wr_ready, b * GROUP + (k + 1))
                    elif k == 0:
                        pe.wait_ge(wr_ready, b + 1)
                    pe.wait_ge(add_done, b * GROUP + (k + 1))
                    pe.matmul(pA[k % 4][0:NODES_T, 0:W], hot[:, 0 if folded else u % 2, k, :],
                              rows[:, u, k, 0:C] if folded else wr[:, k, :], start=True, stop=True).then_inc(agg_done, 1)

                spread_er(0, 0)
                turn_logits(0)
                turn_max(0)

                def turn(b, u, i):
                    pe.wait_ge(scale_ready, b + 1)
                    spread_er(b + 1, (u + 1) % 2)
                    sum_step(b, u, 0)
                    turn_logits(b + 1)
                    for k in range(1, GROUP):
                        sum_step(b, u, k)
                    turn_max(b + 1)
                turns(nc.tensor, turn)


def finish_first(nc, m):
    with ExitStack() as scope:
        z0 = sb(nc, scope, "z0", [NODES_T, 2, D])
        z1 = sb(nc, scope, "z1", [NODES_T, 2, D])
        inv = sb(nc, scope, "inv", [NODES_T, NT, H1])
        h = sb(nc, scope, "h", [NODES_T, 2, D])
        hT = sb(nc, scope, "hT", [P, 2, NODES_T])
        stage = sb(nc, scope, "stage2", [NODES_T, 2, C2 + 1])
        z1n = sb(nc, scope, "z1n", [NODES_T, 2, D])
        pT = [ps(nc, scope, f"qT{k}") for k in range(2)]
        pA = [ps(nc, scope, f"qA{k}") for k in range(2)]
        pZ = [ps(nc, scope, f"qZ{k}") for k in range(2)]
        inn = [m.sem(f"skip_in{u}") for u in range(2)]
        used, h_ready, hT_done, hT_ready = m.sem("skip_used"), m.sem("h1_ready"), m.sem("h1T_done"), m.sem("h1T_ready")
        proj_done, proj_copied = m.sem("second_done"), m.sem("second_copied")
        sent = [m.sem(f"second_sent{u}") for u in range(2)]
        own, ones_in = m.sem("finish_first_dve"), m.sem("second_ones")

        with nc.Block() as block:
            @block.sync
            def _(sp):
                with nc.sync.Fori(0, NT // 2) as i:
                    for u in range(2):
                        t = i * 2 + u
                        at = bass.ds(t * NODES_T, NODES_T)
                        sp.wait_ge(used, t + 1)
                        sp.dma_start(z0[:, u, :], m.z0_d[at, :]).then_inc(inn[u], 16)
                        sp.dma_start(z1[:, u, :], m.z1_d[at, :]).then_inc(inn[u], 16)
                    for u in range(2):
                        t = i * 2 + u
                        at = bass.ds(t * NODES_T, NODES_T)
                        sp.wait_ge(m.second_copied2, t + 1)
                        sp.dma_start(m.tab2[at, :], stage[:, u, :]).then_inc(sent[u], 16)
                        sp.wait_ge(proj_copied, t + 1)
                        sp.dma_start(m.z1_d2[at, :], z1n[:, u, :]).then_inc(sent[u], 16)
                for u in range(2):
                    sp.wait_ge(sent[u], 32 * (NT // 2) + 32)

            @block.gpsimd
            def _(pool):
                pool.memset(stage[:, :, :], 1.0).then_inc(ones_in, 1)

            @block.vector
            def _(dve):
                start = Chain(dve, own)
                dve.sem_inc(used, 2)
                dve.sem_inc(sent[0], 32)
                dve.sem_inc(sent[1], 32)
                acc = m.acc[:, :, :]
                start.done(dve.tensor_scalar(inv[:, :, :], acc[:, :, 0:H1 * C1].rearrange("p t (h c) -> p t h c", h=H1)[:, :, :, D1],
                                             1e-30, None, ALU.max))
                start.done(dve.tensor_scalar(m.norm[:, :], acc[:, :, H1 * C1], 1.0, None, ALU.max))
                start.wait()
                start.done(dve.reciprocal(inv[:, :, :], inv[:, :, :]))
                start.done(dve.reciprocal(m.norm[:, :], m.norm[:, :]))
                start.wait()
                with nc.vector.Fori(0, NT // 2) as i:
                    me = Chain(dve, own, i, 10, start.n)
                    for u in range(2):
                        t = i * 2 + u
                        dve.wait_ge(inn[u], 32 * i + 32)
                        me.done(dve.tensor_tensor(
                            h[:, u, :].rearrange("p (h c) -> p h c", h=H1),
                            m.acc[:, bass.ds(t, 1), 0:H1 * C1].rearrange("p a (h c) -> p (a h) c", h=H1)[:, :, 0:D1],
                            inv[:, bass.ds(t, 1), :].rearrange("p a h -> p h a").to_broadcast([NODES_T, H1, D1]), ALU.mult))
                        me.done(dve.scalar_tensor_tensor(z0[:, u, :], z0[:, u, :], m.norm[:, bass.ds(t, 1)],
                                                         m.bias_b[0:NODES_T, 0, :], ALU.mult, ALU.add))
                        me.wait()
                        me.done(dve.tensor_tensor(h[:, u, :], h[:, u, :], z0[:, u, :], ALU.add))
                        me.wait()
                        me.done(dve.tensor_scalar(h[:, u, :], h[:, u, :], 0.0, None, ALU.max))
                        me.wait()
                        dve.sem_inc(h_ready, 1)
                        dve.wait_ge(proj_done, t + 1)
                        dve.wait_ge(sent[u], 32 * i + 32)
                        me.done(dve.tensor_tensor(z1n[:, u, :], z1[:, u, :], pZ[u][0:NODES_T, 0:D], ALU.add))
                        me.wait()
                        dve.sem_inc(used, 1)
                        dve.sem_inc(proj_copied, 1)
                    me.close()

            @block.tensor
            def _(pe):
                with nc.tensor.Fori(0, NT // 2) as i:
                    for u in range(2):
                        t = i * 2 + u
                        pe.wait_ge(h_ready, t + 1)
                        for c in range(2):
                            ins = pe.transpose(pT[u][:, c * NODES_T:(c + 1) * NODES_T], h[:, u, c * P:c * P + P],
                                               m.ident[0:NODES_T, 0:NODES_T])
                        ins.then_inc(hT_done, 1)
                        pe.wait_ge(hT_ready, t + 1)
                        for c in range(2):
                            pe.matmul(pA[u][0:NODES_T, 0:D + 2], hT[:, c, :], m.w2e[:, c, :], start=(c == 0), stop=(c == 1))
                        for c in range(2):
                            ins = pe.matmul(pZ[u][0:NODES_T, 0:D], hT[:, c, :], m.wb1T[:, 2 + c, :], start=(c == 0), stop=(c == 1))
                        ins.then_inc(proj_done, 1)

            @block.scalar
            def _(act):
                act.wait_ge(ones_in, 1)
                with nc.scalar.Fori(0, NT // 2) as i:
                    for u in range(2):
                        t = i * 2 + u
                        act.wait_ge(hT_done, t + 1)
                        act.copy(hT[:, :, :].rearrange("p c n -> p (c n)"), pT[u][:, 0:2 * NODES_T]).then_inc(hT_ready, 1)
                        act.wait_ge(proj_done, t + 1)
                        act.wait_ge(sent[u], 32 * i + 32)
                        act.copy(stage[:, u, 0:D], pA[u][0:NODES_T, 0:D]).then_inc(m.act_own2, 1)
                        act.copy(stage[:, u, C2:C2 + 1], pA[u][0:NODES_T, D:D + 1]).then_inc(m.act_own2, 1)
                        act.copy(m.er2[:, bass.ds(t, 1), :], pA[u][0:NODES_T, D + 1:D + 2].rearrange("p (a h) -> p a h", a=1)).then_inc(m.act_own2, 1)
                        act.wait_ge(m.act_own2, t * 3 + 3)
                        act.sem_inc(m.second_copied2, 1)


def route(nc, m):
    with ExitStack() as scope:
        tin = sb(nc, scope, "tin", [NODES_T, 2, 3, D])
        inv = sb(nc, scope, "inv2", [NODES_T, NT])
        x2 = sb(nc, scope, "x2", [NODES_T, 2, D])
        xn = sb(nc, scope, "xn2", [NODES_T, 2, D])
        xT = sb(nc, scope, "xT2", [P, 2, NODES_T])
        stats = sb(nc, scope, "stats2", [NODES_T, 6])
        mv = sb(nc, scope, "mv2", [NODES_T, 2])
        var = sb(nc, scope, "var2", [NODES_T, 1])
        rstd = sb(nc, scope, "rstd2", [NODES_T, 1])
        logit = sb(nc, scope, "logit", [NODES_T, NT, EXPERTS])
        top = sb(nc, scope, "top", [NODES_T, NT])
        pick = sb(nc, scope, "pick", [NODES_T, NT, EXPERTS])
        hot = sb(nc, scope, "hot2", [NODES_T, NT, EXPERTS])
        first = sb(nc, scope, "first", [NODES_T, NT])
        eid = sb(nc, scope, "eid", [NODES_T, EXPERTS])
        before = sb(nc, scope, "before", [NODES_T, NT, EXPERTS])
        spare = sb(nc, scope, "spare", [NODES_T, NT])
        zero = sb(nc, scope, "zero", [NODES_T, NT])
        pos = sb(nc, scope, "pos", [NODES_T, NT])
        kept = sb(nc, scope, "kept", [NODES_T, NT])
        slot = sb(nc, scope, "slot", [NODES_T, NT])
        slot_i = sb(nc, scope, "slot_i", [NODES_T, NT], I32)
        tri = sb(nc, scope, "tri", [NODES_T, NODES_T])
        xrow = sb(nc, scope, "xrow", [NODES_T, 10, D])
        pT = ps(nc, scope, "rT")
        pL = ps(nc, scope, "rL")
        pC = [ps(nc, scope, f"rC{k}") for k in range(2)]
        s = m.sem
        inn = [s(f"route_in{u}") for u in range(2)]
        used, var_ready, rstd_ready, xn_ready = s("route_used"), s("route_var"), s("route_rstd"), s("route_xn")
        xT_done, xT_ready, gate_done, own = s("route_xT_done"), s("route_xT_ready"), s("gate_done"), s("route_dve")
        sent = [s(f"route_sent{u}") for u in range(2)]
        made = s("route_consts")
        hot_ready, counted, exp_ready, exp_done = s("hot2_ready"), s("counted"), s("exp_ready"), s("gate_exp")
        slots_ready, row_in, row_out, filled = s("slots_ready"), [s(f"row_in{k}") for k in range(10)], [s(f"row_out{k}") for k in range(10)], s("buffer_zeroed")

        with nc.Block() as block:
            @block.sync
            def _(sp):
                with nc.sync.Fori(0, NT // 2) as i:
                    for u in range(2):
                        t = i * 2 + u
                        at = bass.ds(t * NODES_T, NODES_T)
                        sp.wait_ge(used, t + 1)
                        for k, frm in enumerate((m.x, m.mix_d, m.z1_d2)):
                            sp.dma_start(tin[:, u, k, :], frm[at, :]).then_inc(inn[u], 16)
                    for u in range(2):
                        t = i * 2 + u
                        at = bass.ds(t * NODES_T, NODES_T)
                        sp.wait_ge(xn_ready, t + 1)
                        sp.dma_start(m.x2_d[at, :], x2[:, u, :]).then_inc(sent[u], 16)
                        sp.dma_start(m.xn2_d[at, :], xn[:, u, :]).then_inc(sent[u], 16)
                for u in range(2):
                    sp.wait_ge(sent[u], 32 * (NT // 2) + 32)
                sp.wait_ge(made, 6)
                for k in range(EXPERTS * SLOTS // NODES_T):
                    sp.dma_start(m.xbuf[k * NODES_T:(k + 1) * NODES_T, :], m.zrow[:, :]).then_inc(filled, 16)
                sp.wait_ge(filled, 16 * (EXPERTS * SLOTS // NODES_T))

            @block.gpsimd
            def _(pool):
                pool.iota(eid[:, :], pattern=[[1, EXPERTS]], base=0, channel_multiplier=0,
                          allow_small_or_imprecise_dtypes=True).then_inc(made, 1)
                pool.memset(tri[:, :], 1.0).then_inc(made, 1)
                pool.memset(zero[:, :], 0.0).then_inc(made, 1)
                pool.memset(m.zrow[:, :], 0.0).then_inc(made, 1)
                pool.iota(spare[:, :], pattern=[[NODES_T, NT]], base=EXPERTS * SLOTS, channel_multiplier=1,
                          allow_small_or_imprecise_dtypes=True).then_inc(made, 1)
                pool.wait_ge(made, 5)
                pool.affine_select(out=tri[:, :], in_=tri[:, :], compare_op=ALU.is_ge, fill=0.0, base=0,
                                   pattern=[[1, NODES_T]], channel_multiplier=-1).then_inc(made, 1)
                with nc.gpsimd.Fori(0, NT) as t:
                    pool.wait_ge(var_ready, t + 1)
                    pool.tensor_tensor(rstd[:, :], var[:, :], m.half[0:NODES_T, :], ALU.pow).then_inc(rstd_ready, 1)

            @block.vector
            def _(dve):
                start = Chain(dve, own)
                dve.sem_inc(used, 2)
                dve.sem_inc(sent[0], 32)
                dve.sem_inc(sent[1], 32)
                start.done(dve.tensor_scalar(inv[:, :], m.acc[:, :, D], 1e-30, None, ALU.max))
                start.wait()
                start.done(dve.reciprocal(inv[:, :], inv[:, :]))
                start.wait()
                with nc.vector.Fori(0, NT // 2) as i:
                    me = Chain(dve, own, i, 20, start.n)
                    for u in range(2):
                        t = i * 2 + u
                        dve.wait_ge(inn[u], 48 * i + 48)
                        me.done(dve.scalar_tensor_tensor(tin[:, u, 2, :], tin[:, u, 2, :], m.norm[:, bass.ds(t, 1)],
                                                         m.bias_b[0:NODES_T, 1, :], ALU.mult, ALU.add))
                        me.wait()
                        me.done(dve.tensor_tensor(tin[:, u, 0, :], tin[:, u, 0, :], tin[:, u, 1, :], ALU.add))
                        me.done(dve.scalar_tensor_tensor(tin[:, u, 2, :], m.acc[:, bass.ds(t, 1), 0:D].rearrange("p a d -> p (a d)"),
                                                         inv[:, bass.ds(t, 1)], tin[:, u, 2, :], ALU.mult, ALU.add))
                        me.wait()
                        dve.wait_ge(sent[u], 32 * i + 32)
                        me.done(dve.tensor_tensor(x2[:, u, :], tin[:, u, 0, :], tin[:, u, 2, :], ALU.add))
                        me.wait()
                        dve.sem_inc(used, 1)
                        me.done(dve.bn_stats(stats[:, :], x2[:, u, :]))
                        me.wait_apart(m.hold)
                        me.done(dve.bn_aggr(mv[:, :], stats[:, :]))
                        me.wait()
                        me.done(dve.tensor_scalar(var[:, :], mv[:, 1:2], EPS, None, ALU.add))
                        me.wait()
                        dve.sem_inc(var_ready, 1)
                        dve.wait_ge(rstd_ready, t + 1)
                        me.done(dve.tensor_scalar(xn[:, u, :], x2[:, u, :], mv[:, 0:1], rstd[:, 0:1], ALU.subtract, ALU.mult))
                        me.wait()
                        dve.sem_inc(xn_ready, 1)
                        dve.wait_ge(gate_done, t + 1)
                        me.done(dve.tensor_tensor(logit[:, bass.ds(t, 1), :], pL[0:NODES_T, 0:EXPERTS].rearrange("p (a e) -> p a e", a=1),
                                                  m.gate_bb[0:NODES_T, :].rearrange("p (a e) -> p a e", a=1), ALU.add))
                        me.done(dve.tensor_copy(stats[:, 0:1], mv[:, 0:1]))
                        me.wait()
                    me.close()

            @block.tensor
            def _(pe):
                with nc.tensor.Fori(0, NT // 2) as i:
                    for u in range(2):
                        t = i * 2 + u
                        pe.wait_ge(xn_ready, t + 1)
                        for c in range(2):
                            ins = pe.transpose(pT[:, c * NODES_T:(c + 1) * NODES_T], xn[:, u, c * P:c * P + P],
                                               m.ident[0:NODES_T, 0:NODES_T])
                        ins.then_inc(xT_done, 1)
                        pe.wait_ge(xT_ready, t + 1)
                        for c in range(2):
                            ins = pe.matmul(pL[0:NODES_T, 0:EXPERTS], xT[:, c, :], m.gate_w[:, c, :], start=(c == 0), stop=(c == 1))
                        ins.then_inc(gate_done, 1)

            @block.scalar
            def _(act):
                with nc.scalar.Fori(0, NT) as t:
                    act.wait_ge(xT_done, t + 1)
                    act.copy(xT[:, :, :].rearrange("p c n -> p (c n)"), pT[:, 0:2 * NODES_T]).then_inc(xT_ready, 1)

        wide = [NODES_T, NT, EXPERTS]
        rep = lambda a: a.rearrange("p (t a) -> p t a", a=1).to_broadcast(wide)
        with nc.Block() as block:
            @block.vector
            def _(dve):
                me = Chain(dve, m.sem("places_dve"))
                lab = eid[:, :].rearrange("p (a e) -> p a e", a=1).to_broadcast(wide)
                me.done(dve.tensor_reduce(top[:, :], logit[:, :, :], AX, ALU.max))
                me.wait()
                me.done(dve.tensor_tensor(logit[:, :, :], logit[:, :, :], rep(top[:, :]), ALU.subtract))
                me.wait()
                me.done(dve.tensor_scalar(pick[:, :, :], logit[:, :, :], 0.0, -float(EXPERTS), ALU.is_ge, ALU.mult))
                me.wait()
                me.done(dve.tensor_tensor(pick[:, :, :], pick[:, :, :], lab, ALU.add))
                me.wait()
                me.done(dve.tensor_reduce(first[:, :], pick[:, :, :], AX, ALU.min))
                me.wait()
                me.done(dve.tensor_scalar(first[:, :], first[:, :], float(EXPERTS), None, ALU.add))
                me.wait()
                me.done(dve.tensor_tensor(hot[:, :, :], lab, rep(first[:, :]), ALU.is_equal))
                me.wait()
                dve.sem_inc(hot_ready, 1)
                dve.wait_ge(exp_done, 1)
                me.done(dve.tensor_reduce(m.prob[:, :], logit[:, :, :], AX, ALU.add))
                me.wait()
                me.done(dve.reciprocal(m.prob[:, :], m.prob[:, :]))
                dve.wait_ge(counted, 1)
                me.done(dve.memset(before[:, 0, :], 0.0))
                me.wait()
                for e in range(EXPERTS):
                    me.done(dve.tensor_tensor_scan(before[:, 1:NT, e], pC[1][0:NODES_T, 0:(NT - 1) * EXPERTS]
                                                   .rearrange("p (t e) -> p t e", e=EXPERTS)[:, :, e],
                                                   zero[:, 0:NT - 1], 0.0, ALU.add, ALU.add))
                me.wait()
                me.done(dve.tensor_tensor(before[:, :, :], before[:, :, :], pC[0][0:NODES_T, 0:NT * EXPERTS]
                                          .rearrange("p (t e) -> p t e", e=EXPERTS), ALU.add))
                me.wait()
                me.done(dve.tensor_tensor(before[:, :, :], before[:, :, :], hot[:, :, :], ALU.mult))
                me.wait()
                me.done(dve.tensor_reduce(pos[:, :], before[:, :, :], AX, ALU.add))
                me.wait()
                me.done(dve.tensor_scalar(pos[:, :], pos[:, :], -1.0, None, ALU.add))
                me.wait()
                me.done(dve.tensor_scalar(kept[:, :], pos[:, :], float(CAP), None, ALU.is_lt))
                me.done(dve.tensor_scalar(pos[:, :], pos[:, :], float(CAP - 1), None, ALU.min))
                me.wait()
                me.done(dve.tensor_tensor(m.prob[:, :], m.prob[:, :], kept[:, :], ALU.mult))
                me.done(dve.scalar_tensor_tensor(slot[:, :], first[:, :], float(SLOTS), pos[:, :], ALU.mult, ALU.add))
                me.wait()
                me.done(dve.tensor_copy(m.read_at[:, :], slot[:, :]))
                me.done(dve.tensor_tensor(slot[:, :], slot[:, :], spare[:, :], ALU.subtract))
                me.wait()
                me.done(dve.tensor_tensor(slot[:, :], slot[:, :], kept[:, :], ALU.mult))
                me.wait()
                me.done(dve.tensor_tensor(slot[:, :], slot[:, :], spare[:, :], ALU.add))
                me.wait()
                dve.tensor_copy(slot_i[:, :], slot[:, :]).then_inc(slots_ready, 1)

            @block.tensor
            def _(pe):
                pe.wait_ge(hot_ready, 1)
                flat = hot[:, :, :].rearrange("p t e -> p (t e)")
                pe.matmul(pC[0][0:NODES_T, 0:NT * EXPERTS], tri[:, :], flat, start=True, stop=True)
                pe.matmul(pC[1][0:NODES_T, 0:NT * EXPERTS], m.ones[0:NODES_T, 0:NODES_T], flat, start=True, stop=True
                          ).then_inc(counted, 1)

            @block.scalar
            def _(act):
                act.wait_ge(hot_ready, 1)
                act.activation(logit[:, :, :], logit[:, :, :], ACT.Exp).then_inc(exp_done, 1)

            @block.sync
            def _(sp):
                with nc.sync.Fori(0, NT // 10) as i:
                    for k in range(10):
                        sp.wait_ge(m.slot_moved, 2 * i + 1)
                        sp.dma_start(xrow[:, k, :], m.xn2_d[bass.ds((i * 10 + k) * NODES_T, NODES_T), :]).then_inc(row_in[k], 16)

            @block.gpsimd
            def _(pool):
                pool.sem_inc(m.slot_moved, 1)
                pool.wait_ge(slots_ready, 1)
                with nc.gpsimd.Fori(0, NT // 10) as i:
                    for k in range(10):
                        pool.wait_ge(row_in[k], 16 * i + 16)
                    pool.sem_inc(m.hold, 1)
                    pool.tensor_copy(m.slot10[:, :], slot_i[:, bass.ds(i * 10, 10)]).then_inc(m.slot_moved, 1)
                    pool.wait_ge(m.slot_moved, 2 * i + 2)
                    pool.sem_inc(m.hold, 1)
                    for k in range(10):
                        pool.indirect_dma_start(
                            out=m.xbuf[:, :], out_offset=bass.IndirectOffsetOnAxis(ap=m.slot10[:, k:k + 1].bitcast(U32), axis=0),
                            in_=xrow[:, k, :], in_offset=None).then_inc(row_out[k], 16)
                    for k in range(10):
                        pool.wait_ge(row_out[k], 16 * i + 16)
                    pool.sem_inc(m.slot_moved, 1)


def experts(nc, m):
    HT = 4
    W = HT * NODES_T
    FQ = FF // P
    with ExitStack() as scope:
        xr = sb(nc, scope, "xr", [NODES_T, 2, HT, D])
        xT = sb(nc, scope, "xTe", [P, 2, W])
        hT = sb(nc, scope, "hTe", [P, FQ, W])
        y = sb(nc, scope, "ye", [NODES_T, 2, HT, D])
        w1 = sb(nc, scope, "w1", [P, 2, 2, FF])
        w2 = sb(nc, scope, "w2", [P, 2, FQ, D])
        b1 = sb(nc, scope, "b1", [P, 2, FQ])
        b2 = sb(nc, scope, "b2", [1, 2, D])
        pT = [ps(nc, scope, f"eT{k}") for k in range(2)]
        pF = [ps(nc, scope, f"eF{k}") for k in range(4)]
        pY = [ps(nc, scope, f"eY{k}") for k in range(2)]
        s = m.sem
        w_in = [s(f"expert_w{u}") for u in range(2)]
        x_in = [s(f"expert_x{u}") for u in range(2)]
        w_used, x_used = s("expert_w_used"), s("expert_x_used")
        xT_done, xT_ready, fc1_done, h_ready = s("expert_xT_done"), s("expert_xT_ready"), s("expert_fc1"), s("expert_h")
        h_act = s("expert_h_act")
        fc2_done, y_ready = s("expert_fc2"), s("expert_y")
        sent = [s(f"expert_sent{u}") for u in range(2)]

        def turns(eng, body):
            with eng.Fori(0, EXPERTS // 2) as i:
                for v in range(2):
                    for u in range(2):
                        body(i * 4 + (v * 2 + u), v, u, i, i * 2 + v)

        with nc.Block() as block:
            @block.sync
            def _(sp):
                def turn(n, v, u, i, e):
                    if u == 0:
                        sp.wait_ge(w_used, e + 1)
                        sp.dma_start(w1[:, v], m.w1_flat[bass.ds(e * D, D), :].rearrange("(r p) f -> p r f", p=P)).then_inc(w_in[v], 16)
                        sp.dma_start(w2[:, v], m.w2_flat[bass.ds(e * FF, FF), :].rearrange("(q p) d -> p q d", p=P)).then_inc(w_in[v], 16)
                        sp.dma_start(b1[:, v], m.io["L0_ffn_b1"][bass.ds(e, 1), :].rearrange("a (q p) -> p (a q)", p=P)).then_inc(w_in[v], 16)
                        sp.dma_start(b2[:, v, :], m.io["L0_ffn_b2"][bass.ds(e, 1), :]).then_inc(w_in[v], 16)
                    sp.wait_ge(x_used, n + 1)
                    sp.dma_start(xr[:, u], m.xbuf[bass.ds(n * W, W), :].rearrange("(k p) d -> p k d", p=NODES_T)).then_inc(x_in[u], 16)
                turns(nc.sync, turn)

            @block.tensor
            def _(pe):
                def turn(n, v, u, i, e):
                    pe.wait_ge(x_in[u], 32 * i + (16 * v + 16))
                    for c in range(2):
                        for k in range(HT):
                            ins = pe.transpose(pT[c][:, k * NODES_T:(k + 1) * NODES_T], xr[:, u, k, c * P:c * P + P],
                                               m.ident[0:NODES_T, 0:NODES_T])
                    ins.then_inc(xT_done, 1)
                    pe.wait_ge(w_in[v], 64 * i + 64)
                    pe.wait_ge(xT_ready, n + 1)
                    for q in range(FQ):
                        if q >= 4:
                            pe.wait_ge(h_ready if q % 2 == 0 else h_act, n * (FQ // 2) + (q - 4) // 2 + 1)
                        for c in range(2):
                            ins = pe.matmul(pF[q % 4][:, 0:W], w1[:, v, c, q * P:q * P + P], xT[:, c, :],
                                            start=(c == 0), stop=(c == 1))
                        ins.then_inc(fc1_done, 1)
                    pe.wait_ge(h_ready, n * (FQ // 2) + FQ // 2)
                    pe.wait_ge(h_act, n * (FQ // 2) + FQ // 2)
                    for k in range(HT):
                        pe.wait_ge(y_ready, n * HT + (k + 1))
                        at = pY[k % 2][0:NODES_T, 0:D]
                        for q in range(FQ):
                            pe.matmul(at, hT[:, q, k * NODES_T:(k + 1) * NODES_T], w2[:, v, q, :], start=(q == 0), stop=False)
                        ins = pe.matmul(at, m.ones[0:1, 0:NODES_T], b2[:, v, :], start=False, stop=True)
                        ins.then_inc(fc2_done, 1)
                turns(nc.tensor, turn)

            @block.scalar
            def _(act):
                def turn(n, v, u, i, e):
                    act.wait_ge(xT_done, n + 1)
                    act.copy(xT[:, 0, :], pT[0][:, 0:W]).then_inc(m.xTe_own, 1)
                    act.copy(xT[:, 1, :], pT[1][:, 0:W]).then_inc(m.xTe_own, 1)
                    act.wait_ge(m.xTe_own, n * 2 + 2)
                    act.sem_inc(xT_ready, 1)
                    for q in range(1, FQ, 2):
                        act.wait_ge(fc1_done, n * FQ + (q + 1))
                        act.activation(hT[:, q, :], pF[q % 4][:, 0:W], ACT.Relu, bias=b1[:, v, q:q + 1]).then_inc(h_act, 1)
                    act.wait_ge(y_ready, n * HT + (HT + 2))
                    act.dma_start(m.ybuf[bass.ds(n * W, W), :].rearrange("(k p) d -> p k d", p=NODES_T), y[:, u]).then_inc(sent[u], 16)
                turns(nc.scalar, turn)
                for u in range(2):
                    act.wait_ge(sent[u], 16 * EXPERTS + 16)

            @block.vector
            def _(dve):
                for given, k in ((w_used, 2), (x_used, 2), (y_ready, 2), (sent[0], 16), (sent[1], 16)):
                    dve.sem_inc(given, k)

                def turn(n, v, u, i, e):
                    for q in range(0, FQ, 2):
                        dve.wait_ge(fc1_done, n * FQ + (q + 1))
                        dve.tensor_scalar(hT[:, q, :], pF[q % 4][:, 0:W], b1[:, v, q:q + 1], 0.0, ALU.add, ALU.max).then_inc(h_ready, 1)
                    dve.sem_inc(x_used, 1)
                    dve.wait_ge(sent[u], 32 * i + (16 * v + 16))
                    for k in range(HT):
                        dve.wait_ge(fc2_done, n * HT + (k + 1))
                        dve.tensor_copy(y[:, u, k, :], pY[k % 2][0:NODES_T, 0:D]).then_inc(y_ready, 1)
                    if u == 1:
                        dve.sem_inc(w_used, 1)
                turns(nc.vector, turn)


def combine(nc, m, out):
    K = 10
    with ExitStack() as scope:
        at = sb(nc, scope, "read10", [NODES_T, K], I32)
        yr = sb(nc, scope, "yr", [NODES_T, K, D])
        x2 = sb(nc, scope, "x2c", [NODES_T, K, D])
        r = sb(nc, scope, "rc", [NODES_T, K, D])
        mask = sb(nc, scope, "maskc", [NODES_T, K, D], U32)
        lim = sb(nc, scope, "lim", [NODES_T, 2, K, D])
        s = m.sem
        moved, y_in, x_in, done, own, sent = s("read_moved"), s("y_in"), s("x2_in"), s("combined"), s("combine_dve"), s("out_sent")
        lims = s("limits")
        with nc.Block() as block:
            @block.gpsimd
            def _(pool):
                pool.memset(lim[:, 0], 1e4).then_inc(lims, 1)
                pool.memset(lim[:, 1], -1e4).then_inc(lims, 1)
                with nc.gpsimd.Fori(0, NT // K) as i:
                    pool.wait_ge(done, i + 1)
                    pool.sem_inc(m.hold, 1)
                    pool.tensor_copy(at[:, :], m.read_at[:, bass.ds(i * K, K)]).then_inc(moved, 1)
                    pool.wait_ge(moved, i + 1)
                    pool.sem_inc(m.hold, 1)
                    for k in range(K):
                        pool.indirect_dma_start(out=yr[:, k, :], out_offset=None, in_=m.ybuf[:, :],
                                                in_offset=bass.IndirectOffsetOnAxis(ap=at[:, k:k + 1].bitcast(U32), axis=0)
                                                ).then_inc(y_in, 16)

            @block.sync
            def _(sp):
                with nc.sync.Fori(0, NT // K) as i:
                    sp.wait_ge(done, i + 1)
                    sp.wait_ge(sent, 16 * i + 16)
                    sp.dma_start(x2[:, :, :], m.x2_d[bass.ds(i * K * NODES_T, K * NODES_T), :].rearrange("(k p) d -> p k d", p=NODES_T)
                                 ).then_inc(x_in, 16)
                    sp.wait_ge(done, i + 2)
                    sp.dma_start(out[bass.ds(i * K * NODES_T, K * NODES_T), :].rearrange("(k p) d -> p k d", p=NODES_T), x2[:, :, :]
                                 ).then_inc(sent, 16)
                sp.wait_ge(sent, 16 * (NT // K) + 16)

            @block.vector
            def _(dve):
                dve.sem_inc(done, 1)
                dve.sem_inc(sent, 16)
                dve.wait_ge(lims, 2)
                with nc.vector.Fori(0, NT // K) as i:
                    me = Chain(dve, own, i, 9 + K)
                    dve.wait_ge(y_in, 16 * K * i + 16 * K)
                    for k in range(K):
                        me.done(dve.tensor_scalar(yr[:, k, :], yr[:, k, :], m.prob[:, bass.ds(i * K + k, 1)], None, ALU.mult))
                    me.done(dve.memset(r[:, :, :], 0.0))
                    me.wait()
                    me.done(dve.tensor_tensor(mask[:, :, :], yr[:, :, :], yr[:, :, :], ALU.is_equal))
                    me.wait_apart(m.hold)
                    me.done(dve.copy_predicated(r[:, :, :], mask[:, :, :], yr[:, :, :]))
                    me.wait()
                    for k, (op, lo) in enumerate(((ALU.is_gt, 3.4028235e38), (ALU.is_lt, -3.4028235e38))):
                        me.done(dve.tensor_scalar(mask[:, :, :], r[:, :, :], lo, None, op))
                        me.wait_apart(m.hold)
                        me.done(dve.copy_predicated(r[:, :, :], mask[:, :, :], lim[:, k]))
                        me.wait()
                    dve.wait_ge(x_in, 16 * i + 16)
                    me.done(dve.tensor_tensor(x2[:, :, :], x2[:, :, :], r[:, :, :], ALU.add))
                    me.wait()
                    dve.sem_inc(done, 1)
                    me.done(dve.tensor_copy(r[:, 0, 0:1], r[:, 0, 1:2]))
                    me.wait()
                    me.close()


C1, C2 = D1 + 1, D + 1
ROW1, ROW2 = H1 * C1 + H1, C2 + 1


def gps_layer(nc, io, out):
    with ExitStack() as ctx:
        def dram(name, shape, dt=F32):
            return nc.dram_tensor(name, shape, dt, kind="Internal").ap()

        m = Memory()
        in_phase = []

        def new_sem(name):
            in_phase.append(nc.alloc_semaphore(name))
            return in_phase[-1]

        def phase(work, *args):
            work(nc, m, *args)
            nc.clear_and_free_semaphores(in_phase)
            nc.all_engine_barrier()
            in_phase.clear()

        m.sem = new_sem
        m.io = io
        m.x, m.src, m.dst = io["x"], io["src"], io["dst"]
        m.w1_flat = io["L0_ffn_w1"].rearrange("e d f -> (e d) f")
        m.w2_flat = io["L0_ffn_w2"].rearrange("e f d -> (e f) d")
        m.edge_tab = dram("edge_tab", [ET_PAD, ROW_E])
        m.last_step = dram("last_step", [ET_PAD])
        m.step_dl = dram("step_dl", [STEPS, P])
        m.step_flags = dram("step_flags", [2, STEPS, P])
        m.step_node = dram("step_node", [RT * P], I32)
        m.step_cont = dram("step_cont", [RT * P])
        m.tab1 = dram("tab1", [N, ROW1])
        m.tab2 = dram("tab2", [N, ROW2])
        for_nodes = ["z0_d", "z1_d", "z1_d2", "mix_d", "xn_d", "x2_d", "xn2_d"]
        (m.z0_d, m.z1_d, m.z1_d2, m.mix_d, m.xn_d, m.x2_d, m.xn2_d) = [dram(n, [N, D]) for n in for_nodes]
        m.xT_d = dram("xT_d", [NT * P, 2 * NODES_T])
        m.xbuf = dram("xbuf", [XROWS, D])
        m.ybuf = dram("ybuf", [EXPERTS * SLOTS, D])

        t = lambda name, shape, dt=F32: sb(nc, ctx, name, shape, dt)
        m.ident, m.ones, m.lane, m.iota = t("ident", [P, P]), t("ones", [P, P]), t("lane", [P, 1]), t("iota", [P, NODES_T])
        m.zeros, m.half, m.zrow = t("zeros", [P, D + 1]), t("half", [P, 1]), t("zrow", [NODES_T, D])
        m.idx_all, m.dl_all = t("idx_all", [P, STEPS], I32), t("dl_all", [P, STEPS])
        m.in_all = t("in_all", [P, STEPS])
        m.node_tab, m.cont_dl = t("node_tab", [1, STEPS], I32), t("cont_dl", [H1, BATCHES + 2])
        m.norm = t("norm", [NODES_T, NT])
        m.w1e, m.wb0T, m.wb1T = t("w1e", [P, 2, D + 16]), t("wb0T", [P, 2, D]), t("wb1T", [P, 4, D])
        m.w2e, m.wqT, m.wkv = t("w2e", [P, 2, D + 2]), t("wqT", [P, 2, D]), t("wkv", [P, 2, 2 * D])
        m.er1, m.er2 = t("er1", [NODES_T, NT, H1]), t("er2", [NODES_T, NT, 1])
        m.brow, m.bias_b = t("brow", [1, 6, D]), t("bias_b", [P, 2, D])
        m.gate_w, m.gate_bb = t("gate_w", [P, 2, EXPERTS]), t("gate_bb", [P, EXPERTS])
        m.prob, m.read_at, m.slot10 = t("prob", [NODES_T, NT]), t("read_at", [NODES_T, NT], I32), t("slot10", [NODES_T, 10], I32)
        once = lambda name: ctx.enter_context(nc.semaphore(name))
        m.hold = once("hold")
        m.act_own = once("act_own")
        m.act_own2 = once("act_own2")
        m.second_copied2 = once("second_copied2")
        m.gram_ready = once("gram_ready")
        m.mix_bd = once("mix_bd")
        m.mix_max = once("mix_max")
        m.slot_moved = once("slot_moved")
        m.xTe_own = once("xTe_own")

        ctx.enter_context(nc.allow_non_contiguous_dma(reason="small vectors, laid out by partition once"))
        phase(build_steps)
        phase(fold_weights)
        with ExitStack() as mix:
            tm = lambda name, shape: sb(nc, mix, name, shape)
            m.gram, m.wx = tm("gram", [P, 2, D + 1]), tm("wx", [P, 2, D])
            m.wf1, m.wf2 = tm("wf1", [P, 2, HIDDEN]), tm("wf2", [P, 6, D])
            m.gain, m.shift, m.b1col = tm("gain", [P, 2]), tm("shift", [P, 2]), tm("b1col", [P, 6])
            phase(project_nodes)
            phase(mixer_attention)
            phase(mixer)
        with ExitStack() as conv:
            m.acc = sb(nc, conv, "acc", [NODES_T, NT, H1 * C1 + 1])
            phase(convolve, "conv1", H1, D1, m.tab1, m.er1, m.acc, True)
            phase(finish_first)
            phase(convolve, "conv2", 1, D, m.tab2, m.er2, m.acc, False)
            phase(route)
        phase(experts)
        phase(combine, out)


_INS = ['x', 'src', 'dst', 'L0_gnn_fc1_w', 'L0_gnn_attn_l1', 'L0_gnn_attn_r1', 'L0_gnn_bias1', 'L0_gnn_fc2_w',
        'L0_gnn_attn_l2', 'L0_gnn_attn_r2', 'L0_gnn_bias2', 'L0_gnn_wb0', 'L0_gnn_bb0', 'L0_gnn_wb1', 'L0_gnn_bb1',
        'L0_mix_w_qkv', 'L0_mix_b_qkv', 'L0_mix_norm_g', 'L0_mix_norm_b', 'L0_mix_w_fc1', 'L0_mix_b_fc1',
        'L0_mix_w_fc2', 'L0_mix_b_fc2', 'L0_ffn_gate_w', 'L0_ffn_gate_b', 'L0_ffn_w1', 'L0_ffn_b1', 'L0_ffn_w2',
        'L0_ffn_b2']


def kernel(**inputs):
    import numpy as _np
    import concourse.bacc as _bacc
    from concourse import mybir as _mybir
    from concourse.bass_utils import run_bass_kernel_spmd as _run

    nc = _bacc.Bacc("TRN2", target_bir_lowering=False, num_devices=1)
    arrays, io = {}, {}
    for name in _INS:
        a = _np.ascontiguousarray(inputs[name])
        arrays[f"in_{name}_dram"] = a
        io[name] = nc.dram_tensor(f"in_{name}_dram", a.shape, _mybir.dt.from_np(a.dtype), kind="ExternalInput").ap()
    out = nc.dram_tensor("out_0_dram", (N, D), F32, kind="ExternalOutput").ap()
    gps_layer(nc, io, out)
    r = _run(nc, [arrays], core_ids=[0])
    return r.results[0]["out_0_dram"]
```

```python
from contextlib import ExitStack

import concourse.bass as bass
from concourse import mybir

F32 = mybir.dt.float32
I32 = mybir.dt.int32
U32 = mybir.dt.uint32
BF16 = mybir.dt.bfloat16
ALU = mybir.AluOpType
ACT = mybir.ActivationFunctionType
AX = mybir.AxisListType.X

P = 128
N, D = 6250, 256
NODES_T = 125
NT = N // NODES_T
E = 100000
ET = -(-E // P)
ROWS = 112
RT = 7
ET_PAD = ROWS * RT
GROUP = 8
BATCHES = 104
UNROLL = 4
STEPS = (BATCHES + 2) * GROUP
GE = GROUP * P
WIN = P + 2
ROW_E = P + WIN
H1, D1 = 8, 32
BIG = 1e30
PAD_DST = 1000000
EPS = 1e-5
HIDDEN = 3 * D
EXPERTS, FF = 8, 1024
CAP = -(-5 * N // (4 * EXPERTS))
SLOTS = 1000
XROWS = EXPERTS * SLOTS + N
assert NODES_T * NT == N and ET + NT - 1 <= BATCHES * GROUP and ET < ET_PAD and CAP <= SLOTS and BATCHES % UNROLL == 0


class Memory:
    pass


class Chain:

    def __init__(self, eng, sem, turn=0, per_turn=0, base=0):
        self.eng, self.sem, self.turn, self.per_turn, self.base, self.n = eng, sem, turn, per_turn, base, 0

    def done(self, ins):
        ins.then_inc(self.sem, 1)
        self.n += 1
        return self.n

    def wait(self, n=None):
        n = self.n if n is None else n
        self.eng.wait_ge(self.sem, self.turn * self.per_turn + (self.base + n))

    def wait_apart(self, hold):
        self.wait()
        self.eng.sem_inc(hold, 1)

    def close(self):
        assert self.n == self.per_turn, (self.n, self.per_turn)
        return self.base + self.n


def sb(nc, scope, name, shape, dt=F32):
    return scope.enter_context(nc.sbuf_tensor(name, list(shape), dt))


def ps(nc, scope, name, shape=(P, 512), dt=F32):
    return scope.enter_context(nc.psum_tensor("ps_" + name, list(shape), dt))


def over_pairs(eng, body, ring=2):
    pairs = NT // 2
    assert NT % 2 == 0 and pairs % ring == 1
    with eng.Fori(0, pairs // ring) as i:
        for u in range(ring):
            body(i * ring + u, u, i, True)
    body(pairs - 1, 0, pairs // ring, False)


def place(u, i, ring, n, ahead=0):
    return (u + ahead) % n, i * (ring // n) + (u + ahead) // n


def of_pair(dram, p):
    return dram[bass.ds(p * 2 * NODES_T, 2 * NODES_T), :].rearrange("(k p) d -> p k d", p=NODES_T)


def build_steps(nc, m):
    with ExitStack() as scope:
        ei = sb(nc, scope, "ei", [ROWS, RT, ROW_E], I32)
        ef = sb(nc, scope, "ef", [ROWS, RT, ROW_E])
        bounds = sb(nc, scope, "bounds", [P, NT - 1])
        junk = sb(nc, scope, "junk", [P, ET_PAD])
        last = sb(nc, scope, "last", [ROWS, RT])
        tile_no = sb(nc, scope, "tile_no", [ROWS, RT])
        crossed = sb(nc, scope, "crossed", [ROWS, RT])
        fin = sb(nc, scope, "fin", [ROWS, RT])
        fin_b = sb(nc, scope, "fin_b", [P, ET_PAD])
        step_no = sb(nc, scope, "step_no", [P, RT])
        edge_t = sb(nc, scope, "edge_t", [P, RT])
        edge_i = sb(nc, scope, "edge_i", [P, RT], I32)
        node_t = sb(nc, scope, "node_t", [P, RT])
        node_i = sb(nc, scope, "node_i", [P, RT], I32)
        base = sb(nc, scope, "base", [P, RT])
        rows = sb(nc, scope, "rows", [P, RT, ROW_E])
        dl = sb(nc, scope, "dl", [P, RT, P])
        ge = sb(nc, scope, "ge", [P, RT, P])
        valid = sb(nc, scope, "valid", [P, RT, P])
        edge = sb(nc, scope, "edge", [P, 2, RT, P])
        flag = sb(nc, scope, "flag", [P, 3, RT, P])
        cont = sb(nc, scope, "cont", [P, RT])
        tp = [ps(nc, scope, f"tp{k}") for k in range(4)]
        loaded = m.sem("edges_loaded")
        consts = m.sem("consts_made")
        padded = m.sem("pads_written")
        table = m.sem("edge_table_stored")
        fin_ready = m.sem("fin_ready")
        fin_moved = m.sem("fin_moved")
        tiles_known = m.sem("tiles_known")
        gathered = m.sem("rows_of_steps_gathered")
        flags_made = m.sem("flags_made")
        stored = m.sem("step_tables_stored")
        turned = m.sem("steps_turned")
        copied = m.sem("steps_copied")
        own = m.sem("steps_dve")
        n_loads = 0

        def rows_of(t):
            return min(ROWS, E // P - t * ROWS)

        with nc.Block() as block:
            @block.gpsimd
            def _(pool):
                pool.memset(ei[:, :, 0:P], 0).then_inc(padded, 1)
                pool.memset(ei[:, :, P:ROW_E], PAD_DST).then_inc(padded, 1)
                pool.memset(m.ones[:, :], 1.0).then_inc(consts, 1)
                pool.memset(m.ident[:, :], 0.0).then_inc(consts, 1)
                pool.wait_ge(consts, 2)
                pool.affine_select(out=m.ident[:, :], in_=m.ident[:, :], compare_op=ALU.not_equal, fill=1.0,
                                   base=0, pattern=[[-1, P]], channel_multiplier=1).then_inc(consts, 1)
                pool.iota(m.lane[:, :], pattern=[[0, 1]], base=0, channel_multiplier=1,
                          allow_small_or_imprecise_dtypes=True).then_inc(consts, 1)
                pool.iota(m.iota[:, :], pattern=[[1, NODES_T]], base=0, channel_multiplier=0,
                          allow_small_or_imprecise_dtypes=True).then_inc(consts, 1)
                pool.iota(bounds[:, :], pattern=[[NODES_T, NT - 1]], base=NODES_T, channel_multiplier=0,
                          allow_small_or_imprecise_dtypes=True).then_inc(consts, 1)
                pool.iota(tile_no[:, :], pattern=[[ROWS, RT]], base=0, channel_multiplier=1,
                          allow_small_or_imprecise_dtypes=True).then_inc(consts, 1)
                pool.iota(step_no[:, :], pattern=[[P, RT]], base=0, channel_multiplier=1,
                          allow_small_or_imprecise_dtypes=True).then_inc(consts, 1)
                pool.wait_ge(tiles_known, 1)
                pool.wait_ge(table, 16)
                for c in range(RT):
                    pool.indirect_dma_start(
                        out=rows[:, c, :], out_offset=None, in_=m.edge_tab[:, :],
                        in_offset=bass.IndirectOffsetOnAxis(ap=edge_i[:, c:c + 1].bitcast(U32), axis=0),
                    ).then_inc(gathered, 16)

            @block.sync
            def _(sp):
                nonlocal n_loads
                sp.wait_ge(padded, 2)
                for t in range(RT):
                    full = rows_of(t)
                    first = t * ROWS
                    sp.dma_start(ei[0:full, t, 0:P],
                                 bass.AP(tensor=m.src.tensor, offset=first * P, ap=[[P, full], [1, P]])
                                 ).then_inc(loaded, 16)
                    lo = 1 if t == 0 else 0
                    sp.dma_start(ei[lo:full, t, P:ROW_E],
                                 bass.AP(tensor=m.dst.tensor, offset=(first + lo) * P - 1,
                                         ap=[[P, full - lo], [1, WIN]])).then_inc(loaded, 16)
                    n_loads += 2
                rest = E - (E // P) * P
                row = E // P - (RT - 1) * ROWS
                sp.dma_start(ei[0:1, 0, P + 1:ROW_E], m.dst[0:WIN - 1].rearrange("(a b) -> a b", a=1)).then_inc(loaded, 16)
                sp.dma_start(ei[row:row + 1, RT - 1, 0:rest], m.src[E - rest:E].rearrange("(a b) -> a b", a=1)
                             ).then_inc(loaded, 16)
                sp.dma_start(ei[row:row + 1, RT - 1, P:P + 1 + rest],
                             m.dst[E - rest - 1:E].rearrange("(a b) -> a b", a=1)).then_inc(loaded, 16)
                n_loads += 3
                sp.wait_ge(own, 1)
                sp.dma_start(m.edge_tab.rearrange("(t p) c -> p t c", p=ROWS), ef[:, :, :]).then_inc(table, 16)
                sp.wait_ge(fin_ready, 1)
                sp.dma_start(m.last_step.rearrange("(t p) -> p t", p=ROWS), fin[:, :]).then_inc(fin_moved, 16)
                sp.wait_ge(fin_moved, 16)
                sp.dma_start(fin_b[:, :], m.last_step.rearrange("(a b) -> a b", a=1).to_broadcast([P, ET_PAD])
                             ).then_inc(fin_moved, 16)
                sp.wait_ge(tiles_known, 1)
                sp.dma_start(m.step_node.rearrange("(c p) -> p c", p=P), node_i[:, :]).then_inc(stored, 16)
                sp.wait_ge(flags_made, 1)
                whole = STEPS // P
                part = STEPS - whole * P
                for k, t in ((None, dl), (0, flag), (1, flag)):
                    there = m.step_dl if k is None else m.step_flags[k]
                    here = t if k is None else t[:, k]
                    sp.dma_start(there[0:whole * P].rearrange("(c p) e -> p c e", p=P),
                                 here[:, 0:whole, :]).then_inc(stored, 16)
                    sp.dma_start(there[whole * P:STEPS], here[0:part, whole, :]).then_inc(stored, 16)
                sp.dma_start(m.step_cont.rearrange("(c p) -> p c", p=P), cont[:, :]).then_inc(stored, 16)
                sp.wait_ge(stored, 16 * 8)
                sp.dma_start(m.node_tab[:, :], m.step_node[0:STEPS].rearrange("(a b) -> a b", a=1)).then_inc(stored, 16)
                sp.dma_start(m.cont_dl[:, :], bass.AP(tensor=m.step_cont.tensor, offset=0,
                                                      ap=[[0, H1], [GROUP, BATCHES + 2]])).then_inc(stored, 16)
                sp.wait_ge(stored, 16 * 10)

            @block.vector
            def _(dve):
                me = Chain(dve, own)
                dve.wait_ge(loaded, 16 * n_loads)
                me.done(dve.tensor_copy(ef[:, :, :], ei[:, :, :]))
                me.wait()
                dve.wait_ge(consts, 8)
                me.done(dve.tensor_scalar(last[:, :], ef[:, :, ROW_E - 2], float(N - 1), None, ALU.min))
                me.wait()
                for t in range(RT):
                    me.done(dve.tensor_scalar(junk[0:ROWS, 0:NT - 1], bounds[0:ROWS, :], last[:, t:t + 1], None,
                                              ALU.is_le, ALU.add, accum_out=crossed[:, t:t + 1]))
                    me.wait()
                dve.tensor_tensor(fin[:, :], crossed[:, :], tile_no[:, :], ALU.add).then_inc(fin_ready, 1)
                dve.wait_ge(fin_moved, 32)
                for c in range(RT):
                    me.done(dve.tensor_scalar(junk[:, :], fin_b[:, :], step_no[:, c:c + 1], None,
                                              ALU.is_lt, ALU.add, accum_out=edge_t[:, c:c + 1]))
                    me.wait()
                me.done(dve.tensor_tensor(node_t[:, :], step_no[:, :], edge_t[:, :], ALU.subtract))
                me.done(dve.tensor_scalar(edge_i[:, :], edge_t[:, :], float(ET_PAD - 1), None, ALU.min))
                me.wait()
                me.done(dve.tensor_scalar(node_t[:, :], node_t[:, :], float(NT - 1), None, ALU.min))
                me.wait()
                me.done(dve.tensor_scalar(base[:, :], node_t[:, :], float(NODES_T), None, ALU.mult))
                me.wait()
                dve.tensor_copy(node_i[:, :], node_t[:, :]).then_inc(tiles_known, 1)
                dve.wait_ge(gathered, 16 * RT)
                mid = rows[:, :, P + 1:ROW_E - 1]
                for c in range(RT):
                    me.done(dve.tensor_scalar(dl[:, c, :], rows[:, c, P + 1:ROW_E - 1], base[:, c:c + 1], None,
                                              ALU.subtract))
                me.done(dve.tensor_tensor(edge[:, 0], mid, rows[:, :, P:ROW_E - 2], ALU.not_equal))
                me.done(dve.tensor_tensor(edge[:, 1], mid, rows[:, :, P + 2:ROW_E], ALU.not_equal))
                me.wait()
                me.done(dve.tensor_scalar(ge[:, :, :], dl[:, :, :], 0.0, None, ALU.is_ge))
                me.wait()
                me.done(dve.scalar_tensor_tensor(valid[:, :, :], dl[:, :, :], float(NODES_T - 1), ge[:, :, :],
                                                 ALU.is_le, ALU.mult))
                me.wait()
                for k in range(2):
                    me.done(dve.scalar_tensor_tensor(flag[:, k], edge[:, k], -BIG, valid[:, :, :],
                                                     ALU.mult, ALU.mult))
                me.done(dve.tensor_scalar(flag[:, 2], valid[:, :, :], 2 * BIG, -BIG, ALU.mult, ALU.add))
                me.done(dve.tensor_scalar(ge[:, :, 0], edge[:, 0, :, 0], -1.0, 1.0, ALU.mult, ALU.add))
                me.wait()
                me.done(dve.tensor_tensor(ge[:, :, 0], ge[:, :, 0], valid[:, :, 0], ALU.mult))
                me.wait()
                me.done(dve.scalar_tensor_tensor(cont[:, :], dl[:, :, 0], 1.0, ge[:, :, 0], ALU.add, ALU.mult))
                me.wait()
                dve.tensor_scalar(cont[:, :], cont[:, :], -1.0, None, ALU.add).then_inc(flags_made, 1)
                for q in range(3 * RT):
                    c = q // 3
                    w = min(P, STEPS - c * P)
                    there = (m.idx_all, m.dl_all, m.in_all)[q % 3][:, c * P:c * P + w]
                    dve.wait_ge(turned, q + 1)
                    dve.tensor_copy(there, tp[q % 4][:, 0:w]).then_inc(copied, 1)

            @block.tensor
            def _(pe):
                pe.wait_ge(consts, 8)
                pe.wait_ge(gathered, 16 * RT)
                pe.wait_ge(flags_made, 1)
                for q in range(3 * RT):
                    c = q // 3
                    w = min(P, STEPS - c * P)
                    if q >= 4:
                        pe.wait_ge(copied, q - 3)
                    pe.transpose(tp[q % 4][:, 0:w], (rows[0:w, c, 0:P], dl[0:w, c, :], flag[0:w, 2, c, :])[q % 3],
                                 m.ident[0:w, 0:w]).then_inc(turned, 1)


def fold_weights(nc, m):
    with ExitStack() as scope:
        names = ["fc1", "wb0", "fc2", "wb1"]
        raw = sb(nc, scope, "raw", [P, 2, 3 * D + 2 * D])
        wqkv = sb(nc, scope, "wqkv", [P, 2, 3 * D])
        att = sb(nc, scope, "att", [P, 2, 4])
        head_of = sb(nc, scope, "head_of", [P, 2, H1])
        mask = sb(nc, scope, "mask", [P, 2, H1])
        spread = sb(nc, scope, "spread", [P, 2, 2 * H1 + 2])
        tp = [ps(nc, scope, f"wt{k}") for k in range(4)]
        fp = [ps(nc, scope, f"wf{k}") for k in range(2)]
        loaded = m.sem("weights_loaded")
        iota_done = m.sem("weights_iota")
        turned = m.sem("weights_turned")
        copied = m.sem("weights_copied")
        own = m.sem("weights_dve")
        folded = m.sem("weights_folded")
        blocks = []
        for k, (dest, off) in enumerate([(m.w1e, 0), (m.wb0T, 0), (m.w2e, 0)]):
            for r in range(2):
                for c in range(2):
                    blocks.append((raw[:, r, k * D + c * P:k * D + c * P + P], dest[:, c, r * P:r * P + P]))
        for r in range(2):
            for c in range(4):
                blocks.append((raw[:, r, 3 * D + c * P:3 * D + c * P + P], m.wb1T[:, c, r * P:r * P + P]))
        for r in range(2):
            for c in range(2):
                blocks.append((wqkv[:, r, c * P:c * P + P], m.wqT[:, c, r * P:r * P + P]))
        loads = 0

        with nc.Block() as block:
            @block.sync
            def _(sp):
                nonlocal loads
                def load(to, frm):
                    nonlocal loads
                    sp.dma_start(to, frm).then_inc(loaded, 16)
                    loads += 1
                for k, name in enumerate(["L0_gnn_fc1_w", "L0_gnn_wb0", "L0_gnn_fc2_w"]):
                    load(raw[:, :, k * D:k * D + D], m.io[name].rearrange("(r p) c -> p r c", p=P))
                load(raw[:, :, 3 * D:5 * D], m.io["L0_gnn_wb1"].rearrange("(r p) c -> p r c", p=P))
                load(wqkv[:, :, :], m.io["L0_mix_w_qkv"].rearrange("(r p) c -> p r c", p=P))
                for k, name in enumerate(["L0_gnn_attn_l1", "L0_gnn_attn_r1", "L0_gnn_attn_l2", "L0_gnn_attn_r2"]):
                    load(att[:, :, k], m.io[name].rearrange("h d -> (h d)").rearrange("(r p) -> p r", p=P))
                for k, name in enumerate(["L0_gnn_bias1", "L0_gnn_bias2", "L0_ffn_gate_b"]):
                    w = EXPERTS if k == 2 else D
                    to = m.gate_bb[:, :] if k == 2 else m.bias_b[:, k, :]
                    load(to, m.io[name].rearrange("(a b) -> a b", a=1).to_broadcast([P, w]))
                for k, name in enumerate(["L0_gnn_bb0", "L0_gnn_bb1", "L0_mix_b_fc2"]):
                    load(m.brow[:, k, :], m.io[name].rearrange("(a b) -> a b", a=1))
                load(m.brow[:, 3:6, :], m.io["L0_mix_b_qkv"].rearrange("(a k b) -> a k b", a=1, k=3))
                load(m.gate_w[:, :, :], m.io["L0_ffn_gate_w"].rearrange("(r p) c -> p r c", p=P))
                sp.wait_ge(loaded, 16 * loads)

            @block.gpsimd
            def _(pool):
                pool.iota(head_of[:, :, :], pattern=[[P, 2], [-D1, H1]], base=0, channel_multiplier=1,
                          allow_small_or_imprecise_dtypes=True).then_inc(iota_done, 1)
                pool.memset(m.zeros[:, :], 0.0).then_inc(iota_done, 1)
                pool.memset(m.half[:, :], -0.5).then_inc(iota_done, 1)

            @block.tensor
            def _(pe):
                pe.wait_ge(loaded, 16 * loads)
                for q, (frm, _to) in enumerate(blocks):
                    if q >= 4:
                        pe.wait_ge(copied, q - 3)
                    pe.transpose(tp[q % 4][:, 0:P], frm, m.ident[:, :]).then_inc(turned, 1)
                pe.wait_ge(folded, 1)
                for k, (w, cols, c0) in enumerate([(0, 2 * H1, 0), (2, 2, 2 * H1)]):
                    for c in range(2):
                        for r in range(2):
                            ins = pe.matmul(fp[k][:, c * 32:c * 32 + cols], raw[:, r, w * D + c * P:w * D + c * P + P],
                                            spread[:, r, c0:c0 + cols], start=(r == 0), stop=(r == 1))
                ins.then_inc(folded, 1)

            @block.vector
            def _(dve):
                me = Chain(dve, own)
                dve.wait_ge(loaded, 16 * loads)
                dve.wait_ge(iota_done, 3)
                me.done(dve.tensor_scalar(mask[:, :, :], head_of[:, :, :], 0.0, None, ALU.is_ge))
                me.wait()
                me.done(dve.scalar_tensor_tensor(mask[:, :, :], head_of[:, :, :], float(D1 - 1), mask[:, :, :],
                                                 ALU.is_le, ALU.mult))
                me.wait()
                for r in range(2):
                    for k in range(2):
                        me.done(dve.tensor_scalar(spread[:, r, k * H1:k * H1 + H1], mask[:, r, :], att[:, r, k:k + 1],
                                                  None, ALU.mult))
                me.done(dve.tensor_copy(spread[:, :, 2 * H1:2 * H1 + 2], att[:, :, 2:4]))
                me.wait()
                dve.sem_inc(folded, 1)
                for q, (_frm, to) in enumerate(blocks):
                    dve.wait_ge(turned, q + 1)
                    dve.tensor_copy(to, tp[q % 4][:, 0:P]).then_inc(copied, 1)
                dve.wait_ge(folded, 2)
                for c in range(2):
                    me.done(dve.tensor_copy(m.w1e[:, c, D:D + 2 * H1], fp[0][:, c * 32:c * 32 + 2 * H1]))
                    me.done(dve.tensor_copy(m.w2e[:, c, D:D + 2], fp[1][:, c * 32:c * 32 + 2]))
                me.done(dve.tensor_copy(m.wkv[:, :, :], wqkv[:, :, D:3 * D]))
                me.wait()


def project_nodes(nc, m):
    with ExitStack() as scope:
        xt = sb(nc, scope, "xt", [NODES_T, 2, D])
        stats = sb(nc, scope, "stats", [NODES_T, 2, 6])
        mv = sb(nc, scope, "mv", [NODES_T, 2, 2])
        rstd = sb(nc, scope, "rstd", [NODES_T, 2])
        xn = sb(nc, scope, "xn", [NODES_T, 2, D + 1])
        xT = sb(nc, scope, "xT", [P, 2, 2, NODES_T])
        stage = sb(nc, scope, "stage", [NODES_T, 2, ROW1])
        skip = sb(nc, scope, "skip", [NODES_T, 2, 2, D])
        pT = [ps(nc, scope, f"pT{k}") for k in range(2)]
        pA = [ps(nc, scope, f"pA{k}") for k in range(2)]
        pZ = [ps(nc, scope, f"pZ{k}") for k in range(2)]
        pG = [ps(nc, scope, f"pG{k}") for k in range(2)]
        x_in = [m.sem(f"x_loaded{u}") for u in range(2)]
        x_used = m.sem("x_used")
        var_ready = m.sem("var_ready")
        rstd_ready = m.sem("rstd_ready")
        xn_ready = m.sem("xn_ready")
        xn_used = m.sem("xn_used")
        xT_done = m.sem("xT_done")
        xT_ready = m.sem("xT_ready")
        proj_done = m.sem("proj_done")
        sent = [m.sem(f"proj_sent{u}") for u in range(2)]
        xn_sent = [m.sem(f"xn_sent{u}") for u in range(2)]
        own = m.sem("proj_dve")
        base_ready = m.sem("proj_base")
        psum_used = m.sem("proj_psum_used")

        with nc.Block() as block:
            @block.sync
            def _(sp):
                def load(i):
                    for u in range(2):
                        t = i * 2 + u
                        sp.wait_ge(x_used, t + 1)
                        sp.dma_start(xt[:, u, :], m.x[bass.ds(t * NODES_T, NODES_T), :]).then_inc(x_in[u], 16)

                def store(i):
                    for u in range(2):
                        t = i * 2 + u
                        sp.wait_ge(xn_ready, t + 1)
                        sp.dma_start(m.xn_d[bass.ds(t * NODES_T, NODES_T), :], xn[:, u, 0:D]).then_inc(xn_sent[u], 16)
                        sp.wait_ge(xT_ready, t + 1)
                        sp.dma_start(m.xT_d[bass.ds(t * P, P), :], xT[:, u].rearrange("p c n -> p (c n)")).then_inc(xn_sent[u], 16)

                load(0)
                with nc.sync.Fori(0, NT // 2 - 1) as i:
                    load(i + 1)
                    store(i)
                store(NT // 2 - 1)
                for u in range(2):
                    sp.wait_ge(sent[u], 16 * 2 * (NT // 2) + 32)
                    sp.wait_ge(xn_sent[u], 16 * 2 * (NT // 2) + 32)

            @block.gpsimd
            def _(pool):
                pool.memset(xn[:, :, D:D + 1], 1.0).then_inc(base_ready, 1)
                for u in range(2):
                    pool.memset(stage[:, u, 0:H1 * (D1 + 1)], 1.0).then_inc(base_ready, 1)
                with nc.gpsimd.Fori(0, NT) as t:
                    pool.wait_ge(var_ready, t + 1)
                    pool.tensor_tensor(rstd[:, 0:1], mv[:, 0, 1:2], m.half[0:NODES_T, :], ALU.pow).then_inc(rstd_ready, 1)

            @block.vector
            def _(dve):
                dve.sem_inc(x_used, 2)
                dve.sem_inc(xn_used, 2)
                for u in range(2):
                    dve.sem_inc(sent[u], 32)
                    dve.sem_inc(xn_sent[u], 32)
                dve.wait_ge(base_ready, 3)
                with nc.vector.Fori(0, NT // 2) as i:
                    me = Chain(dve, own, i, 8)
                    for u in range(2):
                        t = i * 2 + u
                        dve.wait_ge(x_in[u], 16 * i + 16)
                        me.done(dve.bn_stats(stats[:, u, :], xt[:, u, :]))
                        me.wait_apart(m.hold)
                        me.done(dve.bn_aggr(mv[:, 1, :], stats[:, u, :]))
                        me.wait()
                        dve.tensor_scalar(mv[:, 0, 1:2], mv[:, 1, 1:2], EPS, None, ALU.add).then_inc(var_ready, 1)
                        dve.wait_ge(rstd_ready, t + 1)
                        dve.wait_ge(xn_used, t + 1)
                        dve.wait_ge(xn_sent[u], 32 * i + 32)
                        me.done(dve.tensor_scalar(xn[:, u, 0:D], xt[:, u, :], mv[:, 1, 0:1], rstd[:, 0:1],
                                                  ALU.subtract, ALU.mult))
                        me.wait()
                        dve.sem_inc(xn_ready, 1)
                        me.done(dve.tensor_copy(mv[:, 0, 0:1], mv[:, 1, 0:1]))
                        dve.sem_inc(x_used, 1)
                    me.close()

            @block.tensor
            def _(pe):
                for c in range(2):
                    pe.matmul(pG[c][:, 0:D + 1], m.zeros[:, 0:P], m.zeros[:, 0:D + 1], start=True, stop=False,
                              skip_group_check=True)
                def turn_and_sum(t, u):
                    pe.wait_ge(xn_ready, t + 1)
                    for c in range(2):
                        ins = pe.transpose(pT[u][:, c * NODES_T:(c + 1) * NODES_T], xn[:, u, c * P:c * P + P],
                                           m.ident[0:NODES_T, 0:NODES_T])
                    ins.then_inc(xT_done, 1)
                    for c in range(2):
                        ins = pe.matmul(pG[c][:, 0:D + 1], xn[:, u, c * P:c * P + P], xn[:, u, :], start=False,
                                        stop=False, skip_group_check=True)
                    ins.then_inc(xn_used, 1)

                def project(t, u):
                    pe.wait_ge(xT_ready, t + 1)
                    pe.wait_ge(psum_used, t + 1)
                    for c in range(2):
                        pe.matmul(pA[u][0:NODES_T, 0:D + 16], xT[:, u, c, :], m.w1e[:, c, :],
                                  start=(c == 0), stop=(c == 1))
                    for k, w in enumerate((m.wb0T, m.wb1T)):
                        at = pZ[u][0:NODES_T, k * D:k * D + D]
                        for c in range(2):
                            pe.matmul(at, xT[:, u, c, :], w[:, c, :], start=(c == 0), stop=False)
                        ins = pe.matmul(at, m.ones[0:1, 0:NODES_T], m.brow[:, k, :], start=False, stop=True)
                    ins.then_inc(proj_done, 1)

                turn_and_sum(0, 0)
                with nc.tensor.Fori(0, NT // 2 - 1) as i:
                    for u in range(2):
                        turn_and_sum(i * 2 + (u + 1), 1 - u)
                        project(i * 2 + u, u)
                turn_and_sum(NT - 1, 1)
                project(NT - 2, 0)
                project(NT - 1, 1)

            @block.scalar
            def _(act):
                def take_turned(t, u, fill):
                    act.wait_ge(xT_done, t + 1)
                    act.wait_ge(xn_sent[u], 32 * fill + 32)
                    act.copy(xT[:, u].rearrange("p c n -> p (c n)"), pT[u][:, 0:2 * NODES_T]).then_inc(xT_ready, 1)

                def take_products(t, u, i):
                    act.wait_ge(proj_done, t + 1)
                    act.wait_ge(sent[u], 32 * i + 32)
                    act.copy(stage[:, u, 0:H1 * (D1 + 1)].rearrange("p (h c) -> p h c", h=H1)[:, :, 0:D1],
                             pA[u][0:NODES_T, 0:D].rearrange("p (h c) -> p h c", h=H1)).then_inc(m.act_own, 1)
                    act.copy(stage[:, u, H1 * (D1 + 1):], pA[u][0:NODES_T, D:D + H1]).then_inc(m.act_own, 1)
                    act.copy(m.er1[:, bass.ds(t, 1), :], pA[u][0:NODES_T, D + H1:D + 2 * H1].rearrange("p (a h) -> p a h", a=1)).then_inc(m.act_own, 1)
                    act.copy(skip[:, u].rearrange("p k d -> p (k d)"), pZ[u][0:NODES_T, :]).then_inc(m.act_own, 1)
                    act.wait_ge(m.act_own, t * 4 + 4)
                    act.sem_inc(psum_used, 1)
                    at = bass.ds(t * NODES_T, NODES_T)
                    act.dma_start(m.tab1[at, :], stage[:, u, :]).then_inc(sent[u], 16)
                    act.dma_start(m.z_d[at, :], skip[:, u].rearrange("p k d -> p (k d)")).then_inc(sent[u], 16)

                act.sem_inc(psum_used, 2)
                take_turned(0, 0, 0)
                with nc.scalar.Fori(0, NT // 2 - 1) as i:
                    for u in range(2):
                        take_turned(i * 2 + (u + 1), 1 - u, i + u)
                        take_products(i * 2 + u, u, i)
                take_turned(NT - 1, 1, NT // 2 - 1)
                take_products(NT - 2, 0, NT // 2 - 1)
                take_products(NT - 1, 1, NT // 2 - 1)

        with nc.Block() as block:
            @block.vector
            def _(dve):
                for c in range(2):
                    dve.tensor_copy(m.gram[:, c, :], pG[c][:, 0:D + 1]).then_inc(m.gram_ready, 1)
                dve.wait_ge(m.gram_ready, 2)


def mixer_attention(nc, m):
    with ExitStack() as scope:
        G = m.gram
        srow = sb(nc, scope, "srow", [1, D])
        U = sb(nc, scope, "U", [P, 2, D])
        u0 = sb(nc, scope, "u0", [1, D])
        nrow = sb(nc, scope, "nrow", [1, 1])
        bqT = sb(nc, scope, "bqT", [P, 2])
        L = sb(nc, scope, "L", [P, 2, 64])
        mx = sb(nc, scope, "mx", [P, 2])
        sm = sb(nc, scope, "sm", [P, 2])
        BD = sb(nc, scope, "BD", [P, 2, P])
        BDT = sb(nc, scope, "BDT", [P, 2, P])
        pb = [ps(nc, scope, f"mp{k}") for k in range(6)]
        w1n = sb(nc, scope, "w1n", [P, 2, 1])
        own = m.sem("mix_dve")
        pe_done = m.sem("mix_pe")
        act_done = m.sem("mix_act")
        loaded = m.sem("mix_loaded")
        bq, bk, bv = m.brow[:, 3, :], m.brow[:, 4, :], m.brow[:, 5, :]
        Wk, Wv = m.wkv[:, :, 0:D], m.wkv[:, :, D:2 * D]
        flat = lambda name: m.io[name].rearrange("(r p) -> p r", p=P)

        with nc.Block() as block:
            @block.sync
            def _(sp):
                sp.dma_start(m.wf1[:, :, :], m.io["L0_mix_w_fc1"].rearrange("(r p) c -> p r c", p=P)).then_inc(loaded, 16)
                sp.dma_start(m.wf2[:, :, :], m.io["L0_mix_w_fc2"].rearrange("(r p) c -> p r c", p=P)).then_inc(loaded, 16)
                sp.dma_start(m.gain[:, :], flat("L0_mix_norm_g")).then_inc(loaded, 16)
                sp.dma_start(m.shift[:, :], flat("L0_mix_norm_b")).then_inc(loaded, 16)
                sp.dma_start(m.b1col[:, :], m.io["L0_mix_b_fc1"].rearrange("(r p) -> p r", p=P)).then_inc(loaded, 16)
                sp.dma_start(bqT[:, :], m.io["L0_mix_b_qkv"][0:D].rearrange("(r p) -> p r", p=P)).then_inc(loaded, 16)
                sp.wait_ge(loaded, 96)

            @block.tensor
            def _(pe):
                for c in range(2):
                    ins = pe.transpose(pb[0][0:1, c * P:c * P + P], G[:, c, D:D + 1], m.ident[:, :])
                ins.then_inc(pe_done, 1)
                pe.wait_ge(own, 1)
                for c in range(2):
                    for r in range(2):
                        pe.matmul(pb[1 + c][:, 0:D], G[:, r, c * P:c * P + P], Wv[:, r, :], start=(r == 0), stop=False)
                    pe.matmul(pb[1 + c][:, 0:D], srow[:, c * P:c * P + P], bv, start=False, stop=True)
                for r in range(2):
                    pe.matmul(pb[3][0:1, 0:D], G[:, r, D:D + 1], Wv[:, r, :], start=(r == 0), stop=False)
                pe.wait_ge(own, 2)
                pe.matmul(pb[3][0:1, 0:D], nrow[:, :], bv, start=False, stop=True).then_inc(pe_done, 1)
                pe.wait_ge(own, 5)
                for c in range(2):
                    for r in range(2):
                        pe.matmul(pb[4 + c][:, 0:D], Wk[:, r, c * P:c * P + P], U[:, r, :], start=(r == 0), stop=False)
                    ins = pe.matmul(pb[4 + c][:, 0:D], bk[:, c * P:c * P + P], u0[:, :], start=False, stop=True)
                ins.then_inc(pe_done, 1)
                pe.wait_ge(loaded, 96)
                for q in range(6):
                    for r in range(2):
                        ins = pe.matmul(pb[0][:, 256 + q:257 + q], m.wf1[:, r, q * P:q * P + P], m.shift[:, r:r + 1],
                                        start=(r == 0), stop=(r == 1))
                ins.then_inc(pe_done, 1)
                pe.wait_ge(m.mix_bd, 1)
                for c in range(2):
                    ins = pe.transpose(pb[1][:, c * P:c * P + P], BD[:, c, :], m.ident[:, :])
                ins.then_inc(pe_done, 1)
                pe.wait_ge(m.mix_bd, 3)
                for c in range(2):
                    for r in range(2):
                        pe.matmul(pb[2 + r][:, c * P:c * P + P], m.wqT[:, c, r * P:r * P + P], BDT[:, c, :],
                                  start=True, stop=True)
                    ins = pe.matmul(pb[4][0:1, c * P:c * P + P], bqT[:, c:c + 1], BDT[:, c, :], start=True, stop=True)
                ins.then_inc(pe_done, 1)

            @block.vector
            def _(dve):
                me = Chain(dve, own)
                dve.wait_ge(pe_done, 1)
                me.done(dve.tensor_copy(srow[:, :], pb[0][0:1, 0:D]))
                me.done(dve.memset(nrow[:, :], float(N)))
                dve.wait_ge(pe_done, 2)
                for c in range(2):
                    me.done(dve.tensor_copy(U[:, c, :], pb[1 + c][:, 0:D]))
                me.done(dve.tensor_copy(u0[:, :], pb[3][0:1, 0:D]))
                me.done(dve.memset(BD[:, :, :], 0.0))
                dve.wait_ge(pe_done, 3)
                for c in range(2):
                    for h in range(2):
                        lo = 64 * h
                        me.done(dve.tensor_scalar(L[lo:lo + 64, c, :],
                                                  pb[4 + c][lo:lo + 64, (2 * c + h) * 64:(2 * c + h + 1) * 64],
                                                  64.0 ** -0.5, None, ALU.mult))
                me.wait()
                me.done(dve.tensor_reduce(mx[:, :], L[:, :, :], AX, ALU.max))
                me.wait()
                me.done(dve.tensor_scalar(mx[:, :], mx[:, :], -1.0, None, ALU.mult))
                me.wait()
                dve.sem_inc(m.mix_max, 1)
                dve.wait_ge(act_done, 2)
                me.done(dve.reciprocal(sm[:, :], sm[:, :]))
                me.wait()
                for c in range(2):
                    for h in range(2):
                        lo = 64 * h
                        me.done(dve.tensor_scalar(BD[lo:lo + 64, c, lo:lo + 64], L[lo:lo + 64, c, :],
                                                  sm[lo:lo + 64, c:c + 1], None, ALU.mult))
                me.wait()
                dve.sem_inc(m.mix_bd, 1)
                dve.wait_ge(pe_done, 5)
                for c in range(2):
                    dve.tensor_copy(BDT[:, c, :], pb[1][:, c * P:c * P + P]).then_inc(m.mix_bd, 1)
                me.done(dve.tensor_tensor(m.b1col[:, :], m.b1col[:, :], pb[0][:, 256:262], ALU.add))
                for r in range(2):
                    me.done(dve.tensor_scalar(m.wf1[:, r, :], m.wf1[:, r, :], m.gain[:, r:r + 1], None, ALU.mult))
                dve.wait_ge(pe_done, 6)
                for r in range(2):
                    me.done(dve.tensor_copy(m.wx[:, r, :], pb[2 + r][:, 0:D]))
                me.done(dve.tensor_copy(m.brow[:, 3, :], pb[4][0:1, 0:D]))
                me.wait()

            @block.scalar
            def _(act):
                act.wait_ge(m.mix_max, 1)
                for c in range(2):
                    act.activation(L[:, c, :], L[:, c, :], ACT.Exp, bias=mx[:, c:c + 1],
                                   accum_out=sm[:, c:c + 1]).then_inc(act_done, 1)


def mixer(nc, m):
    W = 2 * NODES_T
    with ExitStack() as scope:
        xn = sb(nc, scope, "mxn", [NODES_T, 2, 2, D])
        xT = sb(nc, scope, "mxT", [P, 2, 2, W])
        r = sb(nc, scope, "mr", [NODES_T, 2, 2, D])
        hn = sb(nc, scope, "mhn", [NODES_T, 2, D])
        stats = sb(nc, scope, "mstats", [NODES_T, 2, 6])
        mv = sb(nc, scope, "mmv", [NODES_T, 2, 2])
        var = sb(nc, scope, "mvar", [NODES_T, 2])
        rstd = sb(nc, scope, "mrstd", [NODES_T, 2])
        hT = sb(nc, scope, "mhT", [P, 2, W])
        gT = sb(nc, scope, "mgT", [P, 6, W])
        o = sb(nc, scope, "mo", [NODES_T, 2, 2, D])
        pX = ps(nc, scope, "pX")
        pH = ps(nc, scope, "pH")
        pF = [ps(nc, scope, f"pF{k}") for k in range(4)]
        pY = ps(nc, scope, "pY")
        inn = [m.sem(f"mix_in{u}") for u in range(2)]
        used = m.sem("mix_in_used")
        xf_done = m.sem("xf_done")
        var_ready = m.sem("mix_var")
        rstd_ready = m.sem("mix_rstd")
        hn_ready = m.sem("hn_ready")
        hT_done = m.sem("hT_done")
        hT_ready = m.sem("hT_ready")
        fc1_done = m.sem("fc1_done")
        gelu_done = m.sem("gelu_done")
        fc2_done = m.sem("fc2_done")
        out_ready = m.sem("mix_out_ready")
        y_used = m.sem("mix_y_used")
        sent = [m.sem(f"mix_sent{u}") for u in range(2)]
        own = m.sem("mixer_dve")
        pairs = NT // 2

        with nc.Block() as block:
            @block.sync
            def _(sp):
                def load(p, u):
                    at = bass.ds(p * W, W)
                    sp.wait_ge(used, p + 1)
                    sp.dma_start(xn[:, u], m.xn_d[at, :].rearrange("(k p) d -> p k d", p=NODES_T)).then_inc(inn[u], 16)
                    sp.dma_start(xT[:, u], m.xT_d[bass.ds(p * 2 * P, 2 * P), :].rearrange("(k p) d -> p k d", p=P)
                                 ).then_inc(inn[u], 16)

                def turn(p, u, i, more):
                    if more:
                        load(p + 1, 1 - u)
                    sp.wait_ge(out_ready, p + 1)
                    sp.dma_start(m.mix_d[bass.ds(p * W, W), :].rearrange("(k p) d -> p k d", p=NODES_T), o[:, u]
                                 ).then_inc(sent[u], 16)
                load(0, 0)
                over_pairs(nc.sync, turn)
                sp.wait_ge(sent[0], 16 * (pairs - pairs // 2) + 16)
                sp.wait_ge(sent[1], 16 * (pairs // 2) + 16)

            @block.gpsimd
            def _(pool):
                def turn(p, u, i, more):
                    pool.wait_ge(var_ready, p + 1)
                    pool.tensor_tensor(rstd[:, :], var[:, :], m.half[0:NODES_T, :].to_broadcast([NODES_T, 2]), ALU.pow).then_inc(rstd_ready, 1)
                over_pairs(nc.gpsimd, turn)

            @block.vector
            def _(dve):
                dve.sem_inc(used, 2)
                dve.sem_inc(y_used, 1)
                for u in range(2):
                    dve.sem_inc(sent[u], 16)

                def normalise(me, p, u):
                    dve.wait_ge(xf_done, p + 1)
                    me.done(dve.tensor_tensor(r[:, u].rearrange("p k d -> p (k d)"), xn[:, u].rearrange("p k d -> p (k d)"),
                                              pX[0:NODES_T, :], ALU.add))
                    me.wait()
                    dve.sem_inc(used, 1)
                    for k in range(2):
                        me.done(dve.bn_stats(stats[:, k, :], r[:, u, k, :]))
                    me.wait_apart(m.hold)
                    for k in range(2):
                        me.done(dve.bn_aggr(mv[:, k, :], stats[:, k, :]))
                    me.wait()
                    dve.tensor_scalar(var[:, :], mv[:, :, 1], EPS, None, ALU.add).then_inc(var_ready, 1)
                    dve.wait_ge(rstd_ready, p + 1)
                    for k in range(2):
                        me.done(dve.tensor_scalar(hn[:, k, :], r[:, u, k, :], mv[:, k, 0:1], rstd[:, k:k + 1],
                                                  ALU.subtract, ALU.mult))
                    me.wait()
                    dve.sem_inc(hn_ready, 1)

                def turn(p, u, i, more):
                    me = Chain(dve, own, p, 8 if more else 1, start.n if more else start.n + 7 * (pairs - 1))
                    if more:
                        normalise(me, p + 1, 1 - u)
                    dve.wait_ge(fc2_done, p + 1)
                    dve.wait_ge(sent[u], 16 * i + 16)
                    me.done(dve.tensor_tensor(o[:, u].rearrange("p k d -> p (k d)"), r[:, u].rearrange("p k d -> p (k d)"),
                                              pY[0:NODES_T, :], ALU.add))
                    me.wait()
                    dve.sem_inc(out_ready, 1)
                    dve.sem_inc(y_used, 1)
                    me.close()
                start = Chain(dve, own)
                normalise(start, 0, 0)
                over_pairs(nc.vector, turn)

            @block.tensor
            def _(pe):
                def attend(u, fill):
                    pe.wait_ge(inn[u], 32 * fill + 32)
                    for k in range(2):
                        at = pX[0:NODES_T, k * D:k * D + D]
                        for c in range(2):
                            pe.matmul(at, xT[:, u, k, c * NODES_T:(c + 1) * NODES_T], m.wx[:, c, :], start=(c == 0), stop=False)
                        ins = pe.matmul(at, m.ones[0:1, 0:NODES_T], m.brow[:, 3, :], start=False, stop=True)
                    ins.then_inc(xf_done, 1)

                def turn_normed(p):
                    pe.wait_ge(hn_ready, p + 1)
                    for c in range(2):
                        for k in range(2):
                            ins = pe.transpose(pH[:, c * W + k * NODES_T:c * W + (k + 1) * NODES_T],
                                               hn[:, k, c * P:c * P + P], m.ident[0:NODES_T, 0:NODES_T])
                    ins.then_inc(hT_done, 1)

                def turn(p, u, i, more):
                    pe.wait_ge(hT_ready, p + 1)
                    for q in range(6):
                        if q >= 4:
                            pe.wait_ge(gelu_done, p * 6 + (q - 3))
                        for c in range(2):
                            ins = pe.matmul(pF[q % 4][:, 0:W], m.wf1[:, c, q * P:q * P + P], hT[:, c, :],
                                            start=(c == 0), stop=(c == 1))
                        ins.then_inc(fc1_done, 1)
                    if more:
                        attend(1 - u, i + u)
                    pe.wait_ge(gelu_done, p * 6 + 6)
                    pe.wait_ge(y_used, p + 1)
                    for k in range(2):
                        at = pY[0:NODES_T, k * D:k * D + D]
                        for q in range(6):
                            pe.matmul(at, gT[:, q, k * NODES_T:(k + 1) * NODES_T], m.wf2[:, q, :], start=(q == 0), stop=False)
                        ins = pe.matmul(at, m.ones[0:1, 0:NODES_T], m.brow[:, 2, :], start=False, stop=True)
                        if k == 0 and more:
                            turn_normed(p + 1)
                    ins.then_inc(fc2_done, 1)
                attend(0, 0)
                turn_normed(0)
                over_pairs(nc.tensor, turn)

            @block.scalar
            def _(act):
                def turn(p, u, i, more):
                    act.wait_ge(hT_done, p + 1)
                    act.copy(hT[:, :, :].rearrange("p c n -> p (c n)"), pH[:, 0:2 * W]).then_inc(hT_ready, 1)
                    for q in range(6):
                        act.wait_ge(fc1_done, p * 6 + (q + 1))
                        act.activation(gT[:, q, :], pF[q % 4][:, 0:W], ACT.Gelu, bias=m.b1col[:, q:q + 1]
                                       ).then_inc(gelu_done, 1)
                over_pairs(nc.scalar, turn)


def convolve(nc, m, name, heads, width, table, er, acc, degree):
    H, C = heads, width + 1
    W = H * C + (1 if degree else 0)
    ROW = H * C + H
    folded = H == 1
    with ExitStack() as scope:
        def t(n, shape, dt=F32):
            return sb(nc, scope, f"{name}_{n}", shape, dt)

        idx = t("idx", [P, UNROLL, GROUP], I32)
        rows = t("rows", [P, UNROLL, GROUP, ROW])
        dl_b = t("dl_b", [NODES_T, 2, GE])
        flags = t("flags", [H, 2, 2, GE])
        hotT = t("hotT", [NODES_T, GE], BF16)
        hot = t("hot", [P, 2, GROUP, NODES_T])
        parts = t("parts", [NODES_T, NT, 3, H], BF16)
        rest = t("rest", [NODES_T, 2, NT, H])
        er_s = t("er_s", [NODES_T, 2, GROUP, 3, H], BF16)
        z = t("z", [P, GROUP, H])
        under = t("under", [P, GROUP, H])
        lz = t("lz", [P, GROUP, H])
        fw = t("fw", [H, GE])
        bw = t("bw", [H, GE])
        carry = t("carry", [H, 1])
        fall = t("fall", [H, 1])
        ln_scale = t("ln_scale", [H, NODES_T])
        scale = t("scale", [NODES_T, H])
        ex = t("ex", [P, GROUP, H])
        wr = t("wr", [P, GROUP, W]) if not folded else None
        pE = ps(nc, scope, f"{name}_pE")
        pT = ps(nc, scope, f"{name}_pT", (P, GE))
        pB = ps(nc, scope, f"{name}_pB")
        pA = [ps(nc, scope, f"{name}_pA{k}") for k in range(4)]
        s = lambda n: m.sem(f"{name}_{n}")
        loaded = [s(f"flags_in{u}") for u in range(2)]
        gathered = [s(f"rows_in{u}") for u in range(UNROLL)]
        idx_ready, rows_used, scans_done = s("idx_ready"), s("rows_used"), s("scans_done")
        hotT_ready, er_ready, er_done = s("hotT_ready"), s("er_ready"), s("er_done")
        lz_ready, lzT_done, c_back = s("lz_ready"), s("lzT_done"), s("c_back")
        sel_ready, sel_done, scale_ready = s("sel_ready"), s("sel_done"), s("scale_ready")
        t_ready, ex_ready, wr_ready = s("t_ready"), s("ex_ready"), s("wr_ready")
        agg_done, add_done, own, parts_ready = s("agg_done"), s("add_done"), s("own"), s("parts_ready")
        hot_ready, own_act = s("hot_ready"), s("own_act")

        def turns(eng, body):
            with eng.Fori(0, BATCHES // UNROLL) as i:
                for u in range(UNROLL):
                    body(i * UNROLL + u, u, i)

        def after(u, i, ring, ahead=1):
            n = u + ahead
            return n % ring, i * (UNROLL // ring) + n // ring

        with nc.Block() as block:
            @block.sync
            def _(sp):
                def load(n, u):
                    sp.dma_start(dl_b[:, u, :],
                                 m.step_dl[bass.ds(n * GROUP, GROUP), :].rearrange("(a s) e -> a (s e)", a=1)
                                 .to_broadcast([NODES_T, GE])).then_inc(loaded[u], 16)
                    for k in range(2):
                        sp.dma_start(flags[:, u, k, :],
                                     m.step_flags[k, bass.ds(n * GROUP, GROUP), :].rearrange("(a s) e -> a (s e)", a=1)
                                     .to_broadcast([H, GE])).then_inc(loaded[u], 16)

                def turn(b, u, i):
                    sp.wait_ge(scans_done, b + 1)
                    sp.wait_ge(hotT_ready, b + 1)
                    load(b + 2, u % 2)
                load(0, 0)
                load(1, 1)
                turns(nc.sync, turn)

            @block.gpsimd
            def _(pool):
                def gather(n, u):
                    pool.wait_ge(rows_used, n + 1)
                    pool.sem_inc(m.hold, 1)
                    pool.tensor_copy(idx[:, u, :], m.idx_all[:, bass.ds(n * GROUP, GROUP)]).then_inc(idx_ready, 1)
                    pool.wait_ge(idx_ready, n + 1)
                    pool.sem_inc(m.hold, 1)
                    for k in range(GROUP):
                        pool.indirect_dma_start(
                            out=rows[:, u, k, :], out_offset=None, in_=table[:, :],
                            in_offset=bass.IndirectOffsetOnAxis(ap=idx[:, u, k:k + 1].bitcast(U32), axis=0),
                        ).then_inc(gathered[u], 16)
                gather(0, 0)
                gather(1, 1)
                turns(nc.gpsimd, lambda b, u, i: gather(b + 2, (u + 2) % UNROLL))

            @block.scalar
            def _(act):
                regs = [act.alloc_register(f"{name}_act{k}") for k in range(UNROLL * GROUP)]

                def take_er(par, lot):
                    for k in range(GROUP):
                        j = act.snap(lot[k], min_val=0, max_val=NT - 1)
                        act.copy(er_s[:, par, k:k + 1].rearrange("p a c h -> p a (c h)"),
                                 parts[:, bass.ds(j, 1)].rearrange("p a c h -> p a (c h)")).then_inc(er_ready, 1)

                def one_hot_nodes(me, n, par, fill):
                    act.wait_ge(loaded[par], fill * 48 + 48)
                    me.done(act.activation(dl_b[:, par, :], dl_b[:, par, :], ACT.Abs, bias=m.lane[0:NODES_T, :],
                                           scale=-1.0))
                    me.wait()
                    act.activation(hotT[:, :], dl_b[:, par, :], ACT.Relu, bias=m.ones[0:NODES_T, 0:1], scale=-1.0
                                   ).then_inc(hotT_ready, 1)

                def one_hot_edges(me, n, par):
                    if folded:
                        return
                    for k in range(GROUP):
                        me.done(act.activation(hot[:, par, k, :], m.iota[:, :], ACT.Abs,
                                               bias=m.dl_all[:, bass.ds(n * GROUP + k, 1)], scale=-1.0))
                    me.wait()
                    act.activation(hot[:, par], hot[:, par], ACT.Relu, bias=m.ones[:, 0:1], scale=-1.0
                                   ).then_inc(hot_ready, 1)

                def exps(n):
                    act.wait_ge(sel_done, n + 1)
                    act.activation(scale[:, :], pE[0:NODES_T, 256:256 + H], ACT.Exp).then_inc(scale_ready, 1)
                    act.wait_ge(t_ready, n + 1)
                    act.activation(ex[:, :, :], under[:, :, :], ACT.Exp).then_inc(ex_ready, 1)

                start = Chain(act, own_act)
                act.wait_ge(parts_ready, 1)
                act.load(regs[0:2 * GROUP], m.node_tab[0:1, 0:2 * GROUP])
                one_hot_nodes(start, 0, 0, 0)
                take_er(0, regs[0:GROUP])
                one_hot_edges(start, 0, 0)
                act.wait_ge(er_done, 1)
                one_hot_nodes(start, 1, 1, 0)
                take_er(1, regs[GROUP:2 * GROUP])
                exps(0)

                def turn(b, u, i):
                    me = Chain(act, own_act, b, 1 if folded else 1 + GROUP, start.n)
                    if u == 0:
                        act.load(regs, m.node_tab[0:1, bass.ds(i * (UNROLL * GROUP) + 2 * GROUP, UNROLL * GROUP)])
                    take_er(u % 2, regs[u * GROUP:(u + 1) * GROUP])
                    act.wait_ge(er_done, b + 2)
                    one_hot_nodes(me, b + 2, *after(u, i, 2, 2))
                    act.wait_ge(add_done, b * GROUP + 4)
                    one_hot_edges(me, b + 1, (u + 1) % 2)
                    exps(b + 1)
                    me.close()
                turns(nc.scalar, turn)

            @block.vector
            def _(dve):
                regs = [dve.alloc_register(f"{name}_dve{k}") for k in range(UNROLL * GROUP)]

                def edge_logits(me, n, q, fill):
                    dve.wait_ge(er_done, n + 1)
                    dve.wait_ge(gathered[q], fill * (16 * GROUP) + 16 * GROUP)
                    me.done(dve.tensor_tensor(z[:, :, :], rows[:, q, :, H * C:ROW],
                                              pE[:, 0:GROUP * H].rearrange("p (k h) -> p k h", k=GROUP), ALU.add))
                    me.wait()
                    me.done(dve.scalar_tensor_tensor(lz[:, :, :], z[:, :, :], 0.2, z[:, :, :], ALU.mult, ALU.max))
                    me.wait()
                    dve.tensor_tensor(lz[:, :, :], lz[:, :, :],
                                      m.in_all[:, bass.ds(n * GROUP, GROUP)].rearrange("p (k a) -> p k a", a=1)
                                      .to_broadcast([P, GROUP, H]), ALU.min).then_inc(lz_ready, 1)

                def forward_max(me, n, par):
                    dve.wait_ge(lzT_done, n + 1)
                    me.forward = me.done(dve.tensor_tensor_scan(fw[:, :], flags[:, par, 0, :], pT[0:H, :], carry[:, 0:1],
                                                                ALU.add, ALU.max))

                def backward_max(me, n, par):
                    me.wait(me.forward)
                    dve.tensor_tensor_scan(bw[:, ::-1], flags[:, par, 1, ::-1], fw[:, ::-1], -BIG, ALU.add, ALU.max
                                           ).then_inc(scans_done, 1)

                def carry_over(me, n):
                    dve.wait_ge(scans_done, n + 1)
                    me.fell = me.done(dve.tensor_tensor(fall[:, :], carry[:, :], bw[:, 0:1], ALU.subtract))

                def carry_scale(me, n):
                    me.wait(me.fell)
                    dve.tensor_scalar(ln_scale[:, :], m.iota[0:H, :], m.cont_dl[0:H, bass.ds(n, 1)], fall[:, 0:1],
                                      ALU.is_equal, ALU.mult).then_inc(sel_ready, 1)
                    me.done(dve.tensor_copy(carry[:, :], fw[:, GE - 1:GE]))

                def running_max(me, n, par):
                    forward_max(me, n, par)
                    backward_max(me, n, par)
                    carry_over(me, n)
                    carry_scale(me, n)

                def shifted(n):
                    dve.wait_ge(c_back, n + 1)
                    dve.tensor_tensor(under[:, :, :], lz[:, :, :],
                                      pB[:, 0:GROUP * H].rearrange("p (k h) -> p k h", k=GROUP), ALU.subtract
                                      ).then_inc(t_ready, 1)

                def weighted(b, u):
                    dve.wait_ge(ex_ready, b + 1)
                    if folded:
                        for k in range(GROUP):
                            ins = dve.tensor_scalar(hot[:, 0, k, :], m.iota[:, :], m.dl_all[:, bass.ds(b * GROUP + k, 1)],
                                                    ex[:, k, :], ALU.is_equal, ALU.mult)
                            ins.then_inc(wr_ready, 1)
                    else:
                        half = GROUP // 2
                        for k in (0, half):
                            dve.tensor_tensor(wr[:, k:k + half, 0:H * C].rearrange("p k (h c) -> p k h c", h=H),
                                              rows[:, u, k:k + half, 0:H * C].rearrange("p k (h c) -> p k h c", h=H),
                                              ex[:, k:k + half, :].rearrange("p k (h a) -> p k h a", a=1)
                                              .to_broadcast([P, half, H, C]), ALU.mult).then_inc(wr_ready, 1)

                start = Chain(dve, own)
                for given, n in ((rows_used, UNROLL), (add_done, 4)):
                    dve.sem_inc(given, n)
                start.done(dve.memset(acc[:, :, :], 0.0))
                start.done(dve.memset(carry[:, :], -BIG))
                if degree:
                    start.done(dve.memset(wr[:, :, W - 1:W], 1.0))
                left = er[:, :, :]
                for k in range(3):
                    start.done(dve.tensor_copy(parts[:, :, k, :], left))
                    start.wait()
                    if k < 2:
                        start.done(dve.tensor_tensor(rest[:, k], left, parts[:, :, k, :], ALU.subtract))
                        start.wait()
                        left = rest[:, k]
                dve.sem_inc(parts_ready, 1)
                edge_logits(start, 0, 0, 0)
                running_max(start, 0, 0)
                shifted(0)
                edge_logits(start, 1, 1, 0)
                start.wait()

                def turn(b, u, i):
                    me = Chain(dve, own, b, 6, start.n)
                    if u == 0:
                        dve.load(regs, m.node_tab[0:1, bass.ds(i * (UNROLL * GROUP), UNROLL * GROUP)])
                    nodes = [dve.snap(r, min_val=0, max_val=NT - 1) for r in regs[u * GROUP:(u + 1) * GROUP]]
                    par = (u + 1) % 2

                    def add(k):
                        part = acc[:, bass.ds(nodes[k], 1), 0:W]
                        if k == 0:
                            me.wait(scaled)
                        else:
                            dve.wait_ge(add_done, b * GROUP + (k + 4))
                        dve.wait_ge(agg_done, b * GROUP + (k + 1))
                        dve.tensor_tensor(part, part, pA[k % 4][0:NODES_T, 0:W].rearrange("p (a c) -> p a c", a=1),
                                          ALU.add).then_inc(add_done, 1)

                    part = acc[:, bass.ds(nodes[0], 1), 0:H * C].rearrange("p a (h c) -> p (a h) c", h=H)
                    dve.wait_ge(add_done, b * GROUP + 4)
                    dve.wait_ge(scale_ready, b + 1)
                    scaled = me.done(dve.tensor_tensor(part, part, scale[:, :].rearrange("p (h a) -> p h a", a=1)
                                                       .to_broadcast([NODES_T, H, C]), ALU.mult))
                    weighted(b, u)
                    forward_max(me, b + 1, par)
                    if not folded:
                        dve.wait_ge(wr_ready, 2 * b + 2)
                        dve.sem_inc(rows_used, 1)
                    add(0)
                    add(1)
                    backward_max(me, b + 1, par)
                    add(2)
                    carry_over(me, b + 1)
                    add(3)
                    carry_scale(me, b + 1)
                    add(4)
                    shifted(b + 1)
                    add(5)
                    add(6)
                    edge_logits(me, b + 2, *after(u, i, UNROLL, 2))
                    add(7)
                    if folded:
                        dve.sem_inc(rows_used, 1)
                    me.close()
                turns(nc.vector, turn)

            @block.tensor
            def _(pe):
                def spread_er(n, par):
                    pe.wait_ge(hotT_ready, n + 1)
                    pe.wait_ge(er_ready, n * GROUP + GROUP)
                    for k in range(GROUP):
                        for c in range(3):
                            ins = pe.matmul(pE[:, k * H:(k + 1) * H], hotT[:, k * P:(k + 1) * P], er_s[:, par, k, c, :],
                                            start=(c == 0), stop=(c == 2))
                    ins.then_inc(er_done, 1)

                def turn_logits(n):
                    pe.wait_ge(lz_ready, n + 1)
                    for k in range(GROUP):
                        ins = pe.transpose(pT[0:H, k * P:(k + 1) * P], lz[:, k, :], m.ident[:, :])
                    ins.then_inc(lzT_done, 1)

                def turn_max(n):
                    pe.wait_ge(scans_done, n + 1)
                    pe.sem_inc(m.hold, 1)
                    for k in range(GROUP):
                        ins = pe.transpose(pB[:, k * H:(k + 1) * H], bw[:, k * P:(k + 1) * P], m.ident[0:H, 0:H])
                    ins.then_inc(c_back, 1)

                def turn_scale(n):
                    pe.wait_ge(sel_ready, n + 1)
                    pe.matmul(pE[0:NODES_T, 256:256 + H], ln_scale[:, :], m.ident[0:H, 0:H], start=True, stop=True
                              ).then_inc(sel_done, 1)

                def sum_step(b, u, k):
                    if folded:
                        pe.wait_ge(wr_ready, b * GROUP + (k + 1))
                    elif k == 0:
                        pe.wait_ge(hot_ready, b + 1)
                        pe.wait_ge(wr_ready, 2 * b + 1)
                    elif k == GROUP // 2:
                        pe.wait_ge(wr_ready, 2 * b + 2)
                    pe.wait_ge(add_done, b * GROUP + (k + 1))
                    pe.matmul(pA[k % 4][0:NODES_T, 0:W], hot[:, 0 if folded else u % 2, k, :],
                              rows[:, u, k, 0:C] if folded else wr[:, k, :], start=True, stop=True).then_inc(agg_done, 1)

                spread_er(0, 0)
                turn_logits(0)
                turn_max(0)
                turn_scale(0)
                pe.wait_ge(scale_ready, 1)
                spread_er(1, 1)
                turn_logits(1)

                def turn(b, u, i):
                    for k in range(GROUP):
                        sum_step(b, u, k)
                        if k == 4:
                            turn_max(b + 1)
                        if k == 5:
                            turn_scale(b + 1)
                        if k == 6:
                            pe.wait_ge(scale_ready, b + 2)
                            spread_er(b + 2, u % 2)
                    turn_logits(b + 2)
                turns(nc.tensor, turn)


def finish_first(nc, m):
    W = 2 * NODES_T
    with ExitStack() as scope:
        z = sb(nc, scope, "z", [NODES_T, 4, 2, 2, D])
        inv = sb(nc, scope, "inv", [NODES_T, NT, H1])
        h = sb(nc, scope, "h", [NODES_T, 2, 2, D])
        hT = sb(nc, scope, "hT", [P, 2, 2, W])
        stage = sb(nc, scope, "stage2", [NODES_T, 2, 2, ROW2])
        z1n = sb(nc, scope, "z1n", [NODES_T, 2, 2, D])
        pT = [ps(nc, scope, f"qT{k}") for k in range(2)]
        pA = [[ps(nc, scope, f"qA{k}{j}") for j in range(2)] for k in range(2)]
        pZ = [ps(nc, scope, f"qZ{k}") for k in range(2)]
        inn = [m.sem(f"skip_in{u}") for u in range(4)]
        used, h_ready, hT_done, hT_ready = m.sem("skip_used"), m.sem("h1_ready"), m.sem("h1T_done"), m.sem("h1T_ready")
        proj_done, z1_ready, psum_used = m.sem("second_done"), m.sem("z1_ready"), m.sem("second_psum_used")
        sent = [m.sem(f"second_sent{u}") for u in range(2)]
        z1_sent = [m.sem(f"z1_sent{u}") for u in range(2)]
        own, own_act, ones_in = m.sem("finish_first_dve"), m.sem("finish_first_act"), m.sem("second_ones")
        flat = lambda a: a.rearrange("p k d -> p (k d)")

        with nc.Block() as block:
            @block.sync
            def _(sp):
                def load(p, u, i, more):
                    sp.wait_ge(used, p + 1)
                    sp.dma_start(z[:, u].rearrange("p k j d -> p k (j d)"), of_pair(m.z_d, p)).then_inc(inn[u], 16)
                over_pairs(nc.sync, load, 4)
                for u in range(2):
                    n = (NT // 2 + 1 - u) // 2
                    sp.wait_ge(sent[u], 16 * n + 16)
                    sp.wait_ge(z1_sent[u], 16 * n + 16)

            @block.gpsimd
            def _(pool):
                pool.memset(stage[:, :, :, :], 1.0).then_inc(ones_in, 1)

            @block.vector
            def _(dve):
                start = Chain(dve, own)
                dve.sem_inc(used, 4)
                dve.sem_inc(psum_used, 1)
                for u in range(2):
                    dve.sem_inc(sent[u], 16)
                    dve.sem_inc(z1_sent[u], 16)
                acc = m.acc[:, :, :]
                start.done(dve.tensor_scalar(inv[:, :, :], acc[:, :, 0:H1 * C1].rearrange("p t (h c) -> p t h c", h=H1)[:, :, :, D1],
                                             1e-30, None, ALU.max))
                start.done(dve.tensor_scalar(m.norm[:, :], acc[:, :, H1 * C1], 1.0, None, ALU.max))
                start.wait()
                start.done(dve.reciprocal(inv[:, :, :], inv[:, :, :]))
                start.done(dve.reciprocal(m.norm[:, :], m.norm[:, :]))
                start.wait()

                def finish(me, p, q, fill, v):
                    dve.wait_ge(inn[q], 16 * fill + 16)
                    for k in range(2):
                        me.done(dve.scalar_tensor_tensor(z[:, q, k, 0, :], z[:, q, k, 0, :], m.norm[:, bass.ds(p * 2 + k, 1)],
                                                         m.bias_b[0:NODES_T, 0, :], ALU.mult, ALU.add))
                    for k in range(2):
                        me.done(dve.tensor_tensor(
                            h[:, v, k, :].rearrange("p (h c) -> p h c", h=H1),
                            m.acc[:, bass.ds(p * 2 + k, 1), 0:H1 * C1].rearrange("p a (h c) -> p (a h) c", h=H1)[:, :, 0:D1],
                            inv[:, bass.ds(p * 2 + k, 1), :].rearrange("p a h -> p h a").to_broadcast([NODES_T, H1, D1]),
                            ALU.mult))
                    me.wait()
                    dve.tensor_tensor(h[:, v], h[:, v], z[:, q, :, 0, :], ALU.add).then_inc(h_ready, 1)

                def turn(p, u, i, more):
                    me = Chain(dve, own, p, 5 if more else 1, start.n if more else start.n + 4 * (NT // 2 - 1))
                    if more:
                        finish(me, p + 1, *place(u, i, 4, 4, 1), (u + 1) % 2)
                    v, fill = place(u, i, 4, 2)
                    dve.wait_ge(proj_done, p + 1)
                    dve.wait_ge(z1_sent[v], fill * 16 + 16)
                    me.done(dve.tensor_tensor(z1n[:, v], z[:, u, :, 1, :],
                                              pZ[v][0:NODES_T, :].rearrange("p (k d) -> p k d", k=2), ALU.add))
                    me.wait()
                    dve.sem_inc(used, 1)
                    dve.sem_inc(z1_ready, 1)
                    me.close()
                finish(start, 0, 0, 0, 0)
                over_pairs(nc.vector, turn, 4)

            @block.tensor
            def _(pe):
                def turn_h(p, u):
                    pe.wait_ge(h_ready, p + 1)
                    for c in range(2):
                        for k in range(2):
                            ins = pe.transpose(pT[u][:, c * W + k * NODES_T:c * W + (k + 1) * NODES_T],
                                               h[:, u, k, c * P:c * P + P], m.ident[0:NODES_T, 0:NODES_T])
                    ins.then_inc(hT_done, 1)

                def turn(p, u, i, more):
                    v = u % 2
                    if more:
                        turn_h(p + 1, 1 - v)
                    pe.wait_ge(hT_ready, p + 1)
                    pe.wait_ge(psum_used, p + 1)
                    for k in range(2):
                        lhs = lambda c: hT[:, v, c, k * NODES_T:(k + 1) * NODES_T]
                        for c in range(2):
                            pe.matmul(pA[v][k][0:NODES_T, 0:D + 2], lhs(c), m.w2e[:, c, :], start=(c == 0), stop=(c == 1))
                        for c in range(2):
                            ins = pe.matmul(pZ[v][0:NODES_T, k * D:k * D + D], lhs(c), m.wb1T[:, 2 + c, :],
                                            start=(c == 0), stop=(c == 1))
                    ins.then_inc(proj_done, 1)
                turn_h(0, 0)
                over_pairs(nc.tensor, turn, 4)

            @block.scalar
            def _(act):
                act.wait_ge(ones_in, 1)

                def take_turned(p, u):
                    act.wait_ge(hT_done, p + 1)
                    act.activation(hT[:, u].rearrange("p c n -> p (c n)"), pT[u][:, 0:2 * W], ACT.Relu).then_inc(hT_ready, 1)

                def turn(p, u, i, more):
                    me = Chain(act, own_act, p, 6)
                    v, fill = place(u, i, 4, 2)
                    if more:
                        take_turned(p + 1, 1 - v)
                    act.wait_ge(proj_done, p + 1)
                    act.wait_ge(sent[v], fill * 16 + 16)
                    for k in range(2):
                        me.done(act.copy(stage[:, v, k, 0:D], pA[v][k][0:NODES_T, 0:D]))
                        me.done(act.copy(stage[:, v, k, C2:C2 + 1], pA[v][k][0:NODES_T, D:D + 1]))
                        me.done(act.copy(m.er2[:, bass.ds(p * 2 + k, 1), :],
                                         pA[v][k][0:NODES_T, D + 1:D + 2].rearrange("p (a h) -> p a h", a=1)))
                    me.wait()
                    act.dma_start(of_pair(m.tab2, p), stage[:, v]).then_inc(sent[v], 16)
                    act.wait_ge(z1_ready, p + 1)
                    act.sem_inc(psum_used, 1)
                    act.dma_start(of_pair(m.z1_d2, p), z1n[:, v]).then_inc(z1_sent[v], 16)
                    me.close()
                act.sem_inc(psum_used, 1)
                take_turned(0, 0)
                over_pairs(nc.scalar, turn, 4)


def route(nc, m):
    with ExitStack() as scope:
        tin = sb(nc, scope, "tin", [NODES_T, 2, 3, D])
        inv = sb(nc, scope, "inv2", [NODES_T, NT])
        x2 = sb(nc, scope, "x2", [NODES_T, 2, D])
        xn = sb(nc, scope, "xn2", [NODES_T, 2, D])
        xT = sb(nc, scope, "xT2", [P, 2, NODES_T])
        stats = sb(nc, scope, "stats2", [NODES_T, 6])
        mv = sb(nc, scope, "mv2", [NODES_T, 2])
        var = sb(nc, scope, "var2", [NODES_T, 1])
        rstd = sb(nc, scope, "rstd2", [NODES_T, 1])
        logit = sb(nc, scope, "logit", [NODES_T, NT, EXPERTS])
        top = sb(nc, scope, "top", [NODES_T, NT])
        pick = sb(nc, scope, "pick", [NODES_T, NT, EXPERTS])
        hot = sb(nc, scope, "hot2", [NODES_T, NT, EXPERTS])
        first = sb(nc, scope, "first", [NODES_T, NT])
        eid = sb(nc, scope, "eid", [NODES_T, EXPERTS])
        before = sb(nc, scope, "before", [NODES_T, NT, EXPERTS])
        spare = sb(nc, scope, "spare", [NODES_T, NT])
        zero = sb(nc, scope, "zero", [NODES_T, NT])
        pos = sb(nc, scope, "pos", [NODES_T, NT])
        kept = sb(nc, scope, "kept", [NODES_T, NT])
        slot = sb(nc, scope, "slot", [NODES_T, NT])
        slot_i = sb(nc, scope, "slot_i", [NODES_T, NT], I32)
        tri = sb(nc, scope, "tri", [NODES_T, NODES_T])
        xrow = sb(nc, scope, "xrow", [NODES_T, 10, D])
        pT = ps(nc, scope, "rT")
        pL = ps(nc, scope, "rL")
        pC = [ps(nc, scope, f"rC{k}") for k in range(2)]
        s = m.sem
        inn = [s(f"route_in{u}") for u in range(2)]
        used, var_ready, rstd_ready, xn_ready = s("route_used"), s("route_var"), s("route_rstd"), s("route_xn")
        xT_done, xT_ready, gate_done, own = s("route_xT_done"), s("route_xT_ready"), s("gate_done"), s("route_dve")
        sent = [s(f"route_sent{u}") for u in range(2)]
        made = s("route_consts")
        hot_ready, counted, exp_ready, exp_done = s("hot2_ready"), s("counted"), s("exp_ready"), s("gate_exp")
        slots_ready, row_in, row_out, filled = s("slots_ready"), [s(f"row_in{k}") for k in range(10)], [s(f"row_out{k}") for k in range(10)], s("buffer_zeroed")

        with nc.Block() as block:
            @block.sync
            def _(sp):
                with nc.sync.Fori(0, NT // 2) as i:
                    for u in range(2):
                        t = i * 2 + u
                        at = bass.ds(t * NODES_T, NODES_T)
                        sp.wait_ge(used, t + 1)
                        for k, frm in enumerate((m.x, m.mix_d, m.z1_d2)):
                            sp.dma_start(tin[:, u, k, :], frm[at, :]).then_inc(inn[u], 16)
                    for u in range(2):
                        t = i * 2 + u
                        at = bass.ds(t * NODES_T, NODES_T)
                        sp.wait_ge(xn_ready, t + 1)
                        sp.dma_start(m.x2_d[at, :], x2[:, u, :]).then_inc(sent[u], 16)
                        sp.dma_start(m.xn2_d[at, :], xn[:, u, :]).then_inc(sent[u], 16)
                for u in range(2):
                    sp.wait_ge(sent[u], 32 * (NT // 2) + 32)
                sp.wait_ge(made, 6)
                for k in range(EXPERTS * SLOTS // NODES_T):
                    sp.dma_start(m.xbuf[k * NODES_T:(k + 1) * NODES_T, :], m.zrow[:, :]).then_inc(filled, 16)
                sp.wait_ge(filled, 16 * (EXPERTS * SLOTS // NODES_T))

            @block.gpsimd
            def _(pool):
                pool.iota(eid[:, :], pattern=[[1, EXPERTS]], base=0, channel_multiplier=0,
                          allow_small_or_imprecise_dtypes=True).then_inc(made, 1)
                pool.memset(tri[:, :], 1.0).then_inc(made, 1)
                pool.memset(zero[:, :], 0.0).then_inc(made, 1)
                pool.memset(m.zrow[:, :], 0.0).then_inc(made, 1)
                pool.iota(spare[:, :], pattern=[[NODES_T, NT]], base=EXPERTS * SLOTS, channel_multiplier=1,
                          allow_small_or_imprecise_dtypes=True).then_inc(made, 1)
                pool.wait_ge(made, 5)
                pool.affine_select(out=tri[:, :], in_=tri[:, :], compare_op=ALU.is_ge, fill=0.0, base=0,
                                   pattern=[[1, NODES_T]], channel_multiplier=-1).then_inc(made, 1)
                with nc.gpsimd.Fori(0, NT) as t:
                    pool.wait_ge(var_ready, t + 1)
                    pool.tensor_tensor(rstd[:, :], var[:, :], m.half[0:NODES_T, :], ALU.pow).then_inc(rstd_ready, 1)

            @block.vector
            def _(dve):
                start = Chain(dve, own)
                dve.sem_inc(used, 2)
                dve.sem_inc(sent[0], 32)
                dve.sem_inc(sent[1], 32)
                start.done(dve.tensor_scalar(inv[:, :], m.acc[:, :, D], 1e-30, None, ALU.max))
                start.wait()
                start.done(dve.reciprocal(inv[:, :], inv[:, :]))
                start.wait()
                with nc.vector.Fori(0, NT // 2) as i:
                    me = Chain(dve, own, i, 20, start.n)
                    for u in range(2):
                        t = i * 2 + u
                        dve.wait_ge(inn[u], 48 * i + 48)
                        me.done(dve.scalar_tensor_tensor(tin[:, u, 2, :], tin[:, u, 2, :], m.norm[:, bass.ds(t, 1)],
                                                         m.bias_b[0:NODES_T, 1, :], ALU.mult, ALU.add))
                        me.wait()
                        me.done(dve.tensor_tensor(tin[:, u, 0, :], tin[:, u, 0, :], tin[:, u, 1, :], ALU.add))
                        me.done(dve.scalar_tensor_tensor(tin[:, u, 2, :], m.acc[:, bass.ds(t, 1), 0:D].rearrange("p a d -> p (a d)"),
                                                         inv[:, bass.ds(t, 1)], tin[:, u, 2, :], ALU.mult, ALU.add))
                        me.wait()
                        dve.wait_ge(sent[u], 32 * i + 32)
                        me.done(dve.tensor_tensor(x2[:, u, :], tin[:, u, 0, :], tin[:, u, 2, :], ALU.add))
                        me.wait()
                        dve.sem_inc(used, 1)
                        me.done(dve.bn_stats(stats[:, :], x2[:, u, :]))
                        me.wait_apart(m.hold)
                        me.done(dve.bn_aggr(mv[:, :], stats[:, :]))
                        me.wait()
                        me.done(dve.tensor_scalar(var[:, :], mv[:, 1:2], EPS, None, ALU.add))
                        me.wait()
                        dve.sem_inc(var_ready, 1)
                        dve.wait_ge(rstd_ready, t + 1)
                        me.done(dve.tensor_scalar(xn[:, u, :], x2[:, u, :], mv[:, 0:1], rstd[:, 0:1], ALU.subtract, ALU.mult))
                        me.wait()
                        dve.sem_inc(xn_ready, 1)
                        dve.wait_ge(gate_done, t + 1)
                        me.done(dve.tensor_tensor(logit[:, bass.ds(t, 1), :], pL[0:NODES_T, 0:EXPERTS].rearrange("p (a e) -> p a e", a=1),
                                                  m.gate_bb[0:NODES_T, :].rearrange("p (a e) -> p a e", a=1), ALU.add))
                        me.done(dve.tensor_copy(stats[:, 0:1], mv[:, 0:1]))
                        me.wait()
                    me.close()

            @block.tensor
            def _(pe):
                with nc.tensor.Fori(0, NT // 2) as i:
                    for u in range(2):
                        t = i * 2 + u
                        pe.wait_ge(xn_ready, t + 1)
                        for c in range(2):
                            ins = pe.transpose(pT[:, c * NODES_T:(c + 1) * NODES_T], xn[:, u, c * P:c * P + P],
                                               m.ident[0:NODES_T, 0:NODES_T])
                        ins.then_inc(xT_done, 1)
                        pe.wait_ge(xT_ready, t + 1)
                        for c in range(2):
                            ins = pe.matmul(pL[0:NODES_T, 0:EXPERTS], xT[:, c, :], m.gate_w[:, c, :], start=(c == 0), stop=(c == 1))
                        ins.then_inc(gate_done, 1)

            @block.scalar
            def _(act):
                with nc.scalar.Fori(0, NT) as t:
                    act.wait_ge(xT_done, t + 1)
                    act.copy(xT[:, :, :].rearrange("p c n -> p (c n)"), pT[:, 0:2 * NODES_T]).then_inc(xT_ready, 1)

        wide = [NODES_T, NT, EXPERTS]
        rep = lambda a: a.rearrange("p (t a) -> p t a", a=1).to_broadcast(wide)
        with nc.Block() as block:
            @block.vector
            def _(dve):
                me = Chain(dve, m.sem("places_dve"))
                lab = eid[:, :].rearrange("p (a e) -> p a e", a=1).to_broadcast(wide)
                me.done(dve.tensor_reduce(top[:, :], logit[:, :, :], AX, ALU.max))
                me.wait()
                me.done(dve.tensor_tensor(logit[:, :, :], logit[:, :, :], rep(top[:, :]), ALU.subtract))
                me.wait()
                me.done(dve.tensor_scalar(pick[:, :, :], logit[:, :, :], 0.0, -float(EXPERTS), ALU.is_ge, ALU.mult))
                me.wait()
                me.done(dve.tensor_tensor(pick[:, :, :], pick[:, :, :], lab, ALU.add))
                me.wait()
                me.done(dve.tensor_reduce(first[:, :], pick[:, :, :], AX, ALU.min))
                me.wait()
                me.done(dve.tensor_scalar(first[:, :], first[:, :], float(EXPERTS), None, ALU.add))
                me.wait()
                me.done(dve.tensor_tensor(hot[:, :, :], lab, rep(first[:, :]), ALU.is_equal))
                me.wait()
                dve.sem_inc(hot_ready, 1)
                dve.wait_ge(exp_done, 1)
                me.done(dve.tensor_reduce(m.prob[:, :], logit[:, :, :], AX, ALU.add))
                me.wait()
                me.done(dve.reciprocal(m.prob[:, :], m.prob[:, :]))
                dve.wait_ge(counted, 1)
                me.done(dve.memset(before[:, 0, :], 0.0))
                me.wait()
                for e in range(EXPERTS):
                    me.done(dve.tensor_tensor_scan(before[:, 1:NT, e], pC[1][0:NODES_T, 0:(NT - 1) * EXPERTS]
                                                   .rearrange("p (t e) -> p t e", e=EXPERTS)[:, :, e],
                                                   zero[:, 0:NT - 1], 0.0, ALU.add, ALU.add))
                me.wait()
                me.done(dve.tensor_tensor(before[:, :, :], before[:, :, :], pC[0][0:NODES_T, 0:NT * EXPERTS]
                                          .rearrange("p (t e) -> p t e", e=EXPERTS), ALU.add))
                me.wait()
                me.done(dve.tensor_tensor(before[:, :, :], before[:, :, :], hot[:, :, :], ALU.mult))
                me.wait()
                me.done(dve.tensor_reduce(pos[:, :], before[:, :, :], AX, ALU.add))
                me.wait()
                me.done(dve.tensor_scalar(pos[:, :], pos[:, :], -1.0, None, ALU.add))
                me.wait()
                me.done(dve.tensor_scalar(kept[:, :], pos[:, :], float(CAP), None, ALU.is_lt))
                me.done(dve.tensor_scalar(pos[:, :], pos[:, :], float(CAP - 1), None, ALU.min))
                me.wait()
                me.done(dve.tensor_tensor(m.prob[:, :], m.prob[:, :], kept[:, :], ALU.mult))
                me.done(dve.scalar_tensor_tensor(slot[:, :], first[:, :], float(SLOTS), pos[:, :], ALU.mult, ALU.add))
                me.wait()
                me.done(dve.tensor_copy(m.read_at[:, :], slot[:, :]))
                me.done(dve.tensor_tensor(slot[:, :], slot[:, :], spare[:, :], ALU.subtract))
                me.wait()
                me.done(dve.tensor_tensor(slot[:, :], slot[:, :], kept[:, :], ALU.mult))
                me.wait()
                me.done(dve.tensor_tensor(slot[:, :], slot[:, :], spare[:, :], ALU.add))
                me.wait()
                dve.tensor_copy(slot_i[:, :], slot[:, :]).then_inc(slots_ready, 1)

            @block.tensor
            def _(pe):
                pe.wait_ge(hot_ready, 1)
                flat = hot[:, :, :].rearrange("p t e -> p (t e)")
                pe.matmul(pC[0][0:NODES_T, 0:NT * EXPERTS], tri[:, :], flat, start=True, stop=True)
                pe.matmul(pC[1][0:NODES_T, 0:NT * EXPERTS], m.ones[0:NODES_T, 0:NODES_T], flat, start=True, stop=True
                          ).then_inc(counted, 1)

            @block.scalar
            def _(act):
                act.wait_ge(hot_ready, 1)
                act.activation(logit[:, :, :], logit[:, :, :], ACT.Exp).then_inc(exp_done, 1)

            @block.sync
            def _(sp):
                with nc.sync.Fori(0, NT // 10) as i:
                    for k in range(10):
                        sp.wait_ge(m.slot_moved, 2 * i + 1)
                        sp.dma_start(xrow[:, k, :], m.xn2_d[bass.ds((i * 10 + k) * NODES_T, NODES_T), :]).then_inc(row_in[k], 16)

            @block.gpsimd
            def _(pool):
                pool.sem_inc(m.slot_moved, 1)
                pool.wait_ge(slots_ready, 1)
                with nc.gpsimd.Fori(0, NT // 10) as i:
                    for k in range(10):
                        pool.wait_ge(row_in[k], 16 * i + 16)
                    pool.sem_inc(m.hold, 1)
                    pool.tensor_copy(m.slot10[:, :], slot_i[:, bass.ds(i * 10, 10)]).then_inc(m.slot_moved, 1)
                    pool.wait_ge(m.slot_moved, 2 * i + 2)
                    pool.sem_inc(m.hold, 1)
                    for k in range(10):
                        pool.indirect_dma_start(
                            out=m.xbuf[:, :], out_offset=bass.IndirectOffsetOnAxis(ap=m.slot10[:, k:k + 1].bitcast(U32), axis=0),
                            in_=xrow[:, k, :], in_offset=None).then_inc(row_out[k], 16)
                    for k in range(10):
                        pool.wait_ge(row_out[k], 16 * i + 16)
                    pool.sem_inc(m.slot_moved, 1)


def experts(nc, m):
    HT = 4
    W = HT * NODES_T
    FQ = FF // P
    with ExitStack() as scope:
        xr = sb(nc, scope, "xr", [NODES_T, 2, HT, D])
        xT = sb(nc, scope, "xTe", [P, 2, W])
        hT = sb(nc, scope, "hTe", [P, FQ, W])
        y = sb(nc, scope, "ye", [NODES_T, 2, HT, D])
        w1 = sb(nc, scope, "w1", [P, 2, 2, FF])
        w2 = sb(nc, scope, "w2", [P, 2, FQ, D])
        b1 = sb(nc, scope, "b1", [P, 2, FQ])
        b2 = sb(nc, scope, "b2", [1, 2, D])
        pT = [ps(nc, scope, f"eT{k}") for k in range(2)]
        pF = [ps(nc, scope, f"eF{k}") for k in range(4)]
        pY = [ps(nc, scope, f"eY{k}") for k in range(2)]
        s = m.sem
        w_in = [s(f"expert_w{u}") for u in range(2)]
        x_in = [s(f"expert_x{u}") for u in range(2)]
        w_used, x_used = s("expert_w_used"), s("expert_x_used")
        xT_done, xT_ready, fc1_done, h_ready = s("expert_xT_done"), s("expert_xT_ready"), s("expert_fc1"), s("expert_h")
        h_act = s("expert_h_act")
        fc2_done, y_ready = s("expert_fc2"), s("expert_y")
        sent = [s(f"expert_sent{u}") for u in range(2)]

        def turns(eng, body):
            with eng.Fori(0, EXPERTS // 2) as i:
                for v in range(2):
                    for u in range(2):
                        body(i * 4 + (v * 2 + u), v, u, i, i * 2 + v)

        with nc.Block() as block:
            @block.sync
            def _(sp):
                def turn(n, v, u, i, e):
                    if u == 0:
                        sp.wait_ge(w_used, e + 1)
                        sp.dma_start(w1[:, v], m.w1_flat[bass.ds(e * D, D), :].rearrange("(r p) f -> p r f", p=P)).then_inc(w_in[v], 16)
                        sp.dma_start(w2[:, v], m.w2_flat[bass.ds(e * FF, FF), :].rearrange("(q p) d -> p q d", p=P)).then_inc(w_in[v], 16)
                        sp.dma_start(b1[:, v], m.io["L0_ffn_b1"][bass.ds(e, 1), :].rearrange("a (q p) -> p (a q)", p=P)).then_inc(w_in[v], 16)
                        sp.dma_start(b2[:, v, :], m.io["L0_ffn_b2"][bass.ds(e, 1), :]).then_inc(w_in[v], 16)
                    sp.wait_ge(x_used, n + 1)
                    sp.dma_start(xr[:, u], m.xbuf[bass.ds(n * W, W), :].rearrange("(k p) d -> p k d", p=NODES_T)).then_inc(x_in[u], 16)
                turns(nc.sync, turn)

            @block.tensor
            def _(pe):
                def turn(n, v, u, i, e):
                    pe.wait_ge(x_in[u], 32 * i + (16 * v + 16))
                    for c in range(2):
                        for k in range(HT):
                            ins = pe.transpose(pT[c][:, k * NODES_T:(k + 1) * NODES_T], xr[:, u, k, c * P:c * P + P],
                                               m.ident[0:NODES_T, 0:NODES_T])
                    ins.then_inc(xT_done, 1)
                    pe.wait_ge(w_in[v], 64 * i + 64)
                    pe.wait_ge(xT_ready, n + 1)
                    for q in range(FQ):
                        if q >= 4:
                            pe.wait_ge(h_ready if q % 2 == 0 else h_act, n * (FQ // 2) + (q - 4) // 2 + 1)
                        for c in range(2):
                            ins = pe.matmul(pF[q % 4][:, 0:W], w1[:, v, c, q * P:q * P + P], xT[:, c, :],
                                            start=(c == 0), stop=(c == 1))
                        ins.then_inc(fc1_done, 1)
                    pe.wait_ge(h_ready, n * (FQ // 2) + FQ // 2)
                    pe.wait_ge(h_act, n * (FQ // 2) + FQ // 2)
                    for k in range(HT):
                        pe.wait_ge(y_ready, n * HT + (k + 1))
                        at = pY[k % 2][0:NODES_T, 0:D]
                        for q in range(FQ):
                            pe.matmul(at, hT[:, q, k * NODES_T:(k + 1) * NODES_T], w2[:, v, q, :], start=(q == 0), stop=False)
                        ins = pe.matmul(at, m.ones[0:1, 0:NODES_T], b2[:, v, :], start=False, stop=True)
                        ins.then_inc(fc2_done, 1)
                turns(nc.tensor, turn)

            @block.scalar
            def _(act):
                def turn(n, v, u, i, e):
                    act.wait_ge(xT_done, n + 1)
                    act.copy(xT[:, 0, :], pT[0][:, 0:W]).then_inc(m.xTe_own, 1)
                    act.copy(xT[:, 1, :], pT[1][:, 0:W]).then_inc(m.xTe_own, 1)
                    act.wait_ge(m.xTe_own, n * 2 + 2)
                    act.sem_inc(xT_ready, 1)
                    for q in range(1, FQ, 2):
                        act.wait_ge(fc1_done, n * FQ + (q + 1))
                        act.activation(hT[:, q, :], pF[q % 4][:, 0:W], ACT.Relu, bias=b1[:, v, q:q + 1]).then_inc(h_act, 1)
                    act.wait_ge(y_ready, n * HT + (HT + 2))
                    act.dma_start(m.ybuf[bass.ds(n * W, W), :].rearrange("(k p) d -> p k d", p=NODES_T), y[:, u]).then_inc(sent[u], 16)
                turns(nc.scalar, turn)
                for u in range(2):
                    act.wait_ge(sent[u], 16 * EXPERTS + 16)

            @block.vector
            def _(dve):
                for given, k in ((w_used, 2), (x_used, 2), (y_ready, 2), (sent[0], 16), (sent[1], 16)):
                    dve.sem_inc(given, k)

                def turn(n, v, u, i, e):
                    for q in range(0, FQ, 2):
                        dve.wait_ge(fc1_done, n * FQ + (q + 1))
                        dve.tensor_scalar(hT[:, q, :], pF[q % 4][:, 0:W], b1[:, v, q:q + 1], 0.0, ALU.add, ALU.max).then_inc(h_ready, 1)
                    dve.sem_inc(x_used, 1)
                    dve.wait_ge(sent[u], 32 * i + (16 * v + 16))
                    for k in range(HT):
                        dve.wait_ge(fc2_done, n * HT + (k + 1))
                        dve.tensor_copy(y[:, u, k, :], pY[k % 2][0:NODES_T, 0:D]).then_inc(y_ready, 1)
                    if u == 1:
                        dve.sem_inc(w_used, 1)
                turns(nc.vector, turn)


def combine(nc, m, out):
    K = 10
    with ExitStack() as scope:
        at = sb(nc, scope, "read10", [NODES_T, K], I32)
        yr = sb(nc, scope, "yr", [NODES_T, K, D])
        x2 = sb(nc, scope, "x2c", [NODES_T, K, D])
        r = sb(nc, scope, "rc", [NODES_T, K, D])
        mask = sb(nc, scope, "maskc", [NODES_T, K, D], U32)
        lim = sb(nc, scope, "lim", [NODES_T, 2, K, D])
        s = m.sem
        moved, y_in, x_in, done, own, sent = s("read_moved"), s("y_in"), s("x2_in"), s("combined"), s("combine_dve"), s("out_sent")
        lims = s("limits")
        with nc.Block() as block:
            @block.gpsimd
            def _(pool):
                pool.memset(lim[:, 0], 1e4).then_inc(lims, 1)
                pool.memset(lim[:, 1], -1e4).then_inc(lims, 1)
                with nc.gpsimd.Fori(0, NT // K) as i:
                    pool.wait_ge(done, i + 1)
                    pool.sem_inc(m.hold, 1)
                    pool.tensor_copy(at[:, :], m.read_at[:, bass.ds(i * K, K)]).then_inc(moved, 1)
                    pool.wait_ge(moved, i + 1)
                    pool.sem_inc(m.hold, 1)
                    for k in range(K):
                        pool.indirect_dma_start(out=yr[:, k, :], out_offset=None, in_=m.ybuf[:, :],
                                                in_offset=bass.IndirectOffsetOnAxis(ap=at[:, k:k + 1].bitcast(U32), axis=0)
                                                ).then_inc(y_in, 16)

            @block.sync
            def _(sp):
                with nc.sync.Fori(0, NT // K) as i:
                    sp.wait_ge(done, i + 1)
                    sp.wait_ge(sent, 16 * i + 16)
                    sp.dma_start(x2[:, :, :], m.x2_d[bass.ds(i * K * NODES_T, K * NODES_T), :].rearrange("(k p) d -> p k d", p=NODES_T)
                                 ).then_inc(x_in, 16)
                    sp.wait_ge(done, i + 2)
                    sp.dma_start(out[bass.ds(i * K * NODES_T, K * NODES_T), :].rearrange("(k p) d -> p k d", p=NODES_T), x2[:, :, :]
                                 ).then_inc(sent, 16)
                sp.wait_ge(sent, 16 * (NT // K) + 16)

            @block.vector
            def _(dve):
                dve.sem_inc(done, 1)
                dve.sem_inc(sent, 16)
                dve.wait_ge(lims, 2)
                with nc.vector.Fori(0, NT // K) as i:
                    me = Chain(dve, own, i, 9 + K)
                    dve.wait_ge(y_in, 16 * K * i + 16 * K)
                    for k in range(K):
                        me.done(dve.tensor_scalar(yr[:, k, :], yr[:, k, :], m.prob[:, bass.ds(i * K + k, 1)], None, ALU.mult))
                    me.done(dve.memset(r[:, :, :], 0.0))
                    me.wait()
                    me.done(dve.tensor_tensor(mask[:, :, :], yr[:, :, :], yr[:, :, :], ALU.is_equal))
                    me.wait_apart(m.hold)
                    me.done(dve.copy_predicated(r[:, :, :], mask[:, :, :], yr[:, :, :]))
                    me.wait()
                    for k, (op, lo) in enumerate(((ALU.is_gt, 3.4028235e38), (ALU.is_lt, -3.4028235e38))):
                        me.done(dve.tensor_scalar(mask[:, :, :], r[:, :, :], lo, None, op))
                        me.wait_apart(m.hold)
                        me.done(dve.copy_predicated(r[:, :, :], mask[:, :, :], lim[:, k]))
                        me.wait()
                    dve.wait_ge(x_in, 16 * i + 16)
                    me.done(dve.tensor_tensor(x2[:, :, :], x2[:, :, :], r[:, :, :], ALU.add))
                    me.wait()
                    dve.sem_inc(done, 1)
                    me.done(dve.tensor_copy(r[:, 0, 0:1], r[:, 0, 1:2]))
                    me.wait()
                    me.close()


C1, C2 = D1 + 1, D + 1
ROW1, ROW2 = H1 * C1 + H1, C2 + 1


def gps_layer(nc, io, out):
    with ExitStack() as ctx:
        def dram(name, shape, dt=F32):
            return nc.dram_tensor(name, shape, dt, kind="Internal").ap()

        m = Memory()
        in_phase = []

        def new_sem(name):
            in_phase.append(nc.alloc_semaphore(name))
            return in_phase[-1]

        def phase(work, *args):
            work(nc, m, *args)
            nc.clear_and_free_semaphores(in_phase)
            nc.all_engine_barrier()
            in_phase.clear()

        m.sem = new_sem
        m.io = io
        m.x, m.src, m.dst = io["x"], io["src"], io["dst"]
        m.w1_flat = io["L0_ffn_w1"].rearrange("e d f -> (e d) f")
        m.w2_flat = io["L0_ffn_w2"].rearrange("e f d -> (e f) d")
        m.edge_tab = dram("edge_tab", [ET_PAD, ROW_E])
        m.last_step = dram("last_step", [ET_PAD])
        m.step_dl = dram("step_dl", [STEPS, P])
        m.step_flags = dram("step_flags", [2, STEPS, P])
        m.step_node = dram("step_node", [RT * P], I32)
        m.step_cont = dram("step_cont", [RT * P])
        m.tab1 = dram("tab1", [N, ROW1])
        m.tab2 = dram("tab2", [N, ROW2])
        m.z1_d2, m.mix_d, m.xn_d, m.x2_d, m.xn2_d = [dram(n, [N, D]) for n in ("z1_d2", "mix_d", "xn_d", "x2_d", "xn2_d")]
        m.z_d = dram("z_d", [N, 2 * D])
        m.xT_d = dram("xT_d", [NT * P, 2 * NODES_T])
        m.xbuf = dram("xbuf", [XROWS, D])
        m.ybuf = dram("ybuf", [EXPERTS * SLOTS, D])

        t = lambda name, shape, dt=F32: sb(nc, ctx, name, shape, dt)
        m.ident, m.ones, m.lane, m.iota = t("ident", [P, P]), t("ones", [P, P]), t("lane", [P, 1]), t("iota", [P, NODES_T])
        m.zeros, m.half, m.zrow = t("zeros", [P, D + 1]), t("half", [P, 1]), t("zrow", [NODES_T, D])
        m.idx_all, m.dl_all = t("idx_all", [P, STEPS], I32), t("dl_all", [P, STEPS])
        m.in_all = t("in_all", [P, STEPS])
        m.node_tab, m.cont_dl = t("node_tab", [1, STEPS], I32), t("cont_dl", [H1, BATCHES + 2])
        m.norm = t("norm", [NODES_T, NT])
        m.w1e, m.wb0T, m.wb1T = t("w1e", [P, 2, D + 16]), t("wb0T", [P, 2, D]), t("wb1T", [P, 4, D])
        m.w2e, m.wqT, m.wkv = t("w2e", [P, 2, D + 2]), t("wqT", [P, 2, D]), t("wkv", [P, 2, 2 * D])
        m.er1, m.er2 = t("er1", [NODES_T, NT, H1]), t("er2", [NODES_T, NT, 1])
        m.brow, m.bias_b = t("brow", [1, 6, D]), t("bias_b", [P, 2, D])
        m.gate_w, m.gate_bb = t("gate_w", [P, 2, EXPERTS]), t("gate_bb", [P, EXPERTS])
        m.prob, m.read_at, m.slot10 = t("prob", [NODES_T, NT]), t("read_at", [NODES_T, NT], I32), t("slot10", [NODES_T, 10], I32)
        once = lambda name: ctx.enter_context(nc.semaphore(name))
        m.hold = once("hold")
        m.act_own = once("act_own")
        m.gram_ready = once("gram_ready")
        m.mix_bd = once("mix_bd")
        m.mix_max = once("mix_max")
        m.slot_moved = once("slot_moved")
        m.xTe_own = once("xTe_own")

        ctx.enter_context(nc.allow_non_contiguous_dma(reason="small vectors, laid out by partition once"))
        phase(build_steps)
        phase(fold_weights)
        with ExitStack() as mix:
            tm = lambda name, shape: sb(nc, mix, name, shape)
            m.gram, m.wx = tm("gram", [P, 2, D + 1]), tm("wx", [P, 2, D])
            m.wf1, m.wf2 = tm("wf1", [P, 2, HIDDEN]), tm("wf2", [P, 6, D])
            m.gain, m.shift, m.b1col = tm("gain", [P, 2]), tm("shift", [P, 2]), tm("b1col", [P, 6])
            phase(project_nodes)
            phase(mixer_attention)
            phase(mixer)
        with ExitStack() as conv:
            m.acc = sb(nc, conv, "acc", [NODES_T, NT, H1 * C1 + 1])
            phase(convolve, "conv1", H1, D1, m.tab1, m.er1, m.acc, True)
            phase(finish_first)
            phase(convolve, "conv2", 1, D, m.tab2, m.er2, m.acc, False)
            phase(route)
        phase(experts)
        phase(combine, out)


_INS = ['x', 'src', 'dst', 'L0_gnn_fc1_w', 'L0_gnn_attn_l1', 'L0_gnn_attn_r1', 'L0_gnn_bias1', 'L0_gnn_fc2_w',
        'L0_gnn_attn_l2', 'L0_gnn_attn_r2', 'L0_gnn_bias2', 'L0_gnn_wb0', 'L0_gnn_bb0', 'L0_gnn_wb1', 'L0_gnn_bb1',
        'L0_mix_w_qkv', 'L0_mix_b_qkv', 'L0_mix_norm_g', 'L0_mix_norm_b', 'L0_mix_w_fc1', 'L0_mix_b_fc1',
        'L0_mix_w_fc2', 'L0_mix_b_fc2', 'L0_ffn_gate_w', 'L0_ffn_gate_b', 'L0_ffn_w1', 'L0_ffn_b1', 'L0_ffn_w2',
        'L0_ffn_b2']


def kernel(**inputs):
    import numpy as _np
    import concourse.bacc as _bacc
    from concourse import mybir as _mybir
    from concourse.bass_utils import run_bass_kernel_spmd as _run

    nc = _bacc.Bacc("TRN2", target_bir_lowering=False, num_devices=1)
    arrays, io = {}, {}
    for name in _INS:
        a = _np.ascontiguousarray(inputs[name])
        arrays[f"in_{name}_dram"] = a
        io[name] = nc.dram_tensor(f"in_{name}_dram", a.shape, _mybir.dt.from_np(a.dtype), kind="ExternalInput").ap()
    out = nc.dram_tensor("out_0_dram", (N, D), F32, kind="ExternalOutput").ap()
    gps_layer(nc, io, out)
    r = _run(nc, [arrays], core_ids=[0])
    return r.results[0]["out_0_dram"]
```

```python
from contextlib import ExitStack

import concourse.bass as bass
from concourse import mybir

F32 = mybir.dt.float32
I32 = mybir.dt.int32
U32 = mybir.dt.uint32
BF16 = mybir.dt.bfloat16
ALU = mybir.AluOpType
ACT = mybir.ActivationFunctionType
AX = mybir.AxisListType.X

P = 128
N, D = 6250, 256
NODES_T = 125
NT = N // NODES_T
E = 100000
ET = -(-E // P)
ROWS = 112
RT = 7
ET_PAD = ROWS * RT
GROUP = 8
BATCHES = 104
UNROLL = 4
STEPS = (BATCHES + 2) * GROUP
GE = GROUP * P
WIN = P + 2
ROW_E = P + WIN
H1, D1 = 8, 32
BIG = 1e30
PAD_DST = 1000000
EPS = 1e-5
HIDDEN = 3 * D
EXPERTS, FF = 8, 1024
CAP = -(-5 * N // (4 * EXPERTS))
SLOTS = 1000
XROWS = EXPERTS * SLOTS + N
assert NODES_T * NT == N and ET + NT - 1 <= BATCHES * GROUP and ET < ET_PAD and CAP <= SLOTS and BATCHES % UNROLL == 0


class Memory:
    pass


class Chain:

    def __init__(self, eng, sem, turn=0, per_turn=0, base=0):
        self.eng, self.sem, self.turn, self.per_turn, self.base, self.n = eng, sem, turn, per_turn, base, 0

    def done(self, ins):
        ins.then_inc(self.sem, 1)
        self.n += 1
        return self.n

    def wait(self, n=None):
        n = self.n if n is None else n
        self.eng.wait_ge(self.sem, self.turn * self.per_turn + (self.base + n))

    def wait_apart(self, hold):
        self.wait()
        self.eng.sem_inc(hold, 1)

    def close(self):
        assert self.n == self.per_turn, (self.n, self.per_turn)
        return self.base + self.n


def sb(nc, scope, name, shape, dt=F32):
    return scope.enter_context(nc.sbuf_tensor(name, list(shape), dt))


def ps(nc, scope, name, shape=(P, 512), dt=F32):
    return scope.enter_context(nc.psum_tensor("ps_" + name, list(shape), dt))


def over_pairs(eng, body, ring=2):
    pairs = NT // 2
    assert NT % 2 == 0 and pairs % ring == 1
    with eng.Fori(0, pairs // ring) as i:
        for u in range(ring):
            body(i * ring + u, u, i, True)
    body(pairs - 1, 0, pairs // ring, False)


def place(u, i, ring, n, ahead=0):
    return (u + ahead) % n, i * (ring // n) + (u + ahead) // n


def of_pair(dram, p):
    return dram[bass.ds(p * 2 * NODES_T, 2 * NODES_T), :].rearrange("(k p) d -> p k d", p=NODES_T)


def build_steps(nc, m):
    with ExitStack() as scope:
        ei = sb(nc, scope, "ei", [ROWS, RT, ROW_E], I32)
        ef = sb(nc, scope, "ef", [ROWS, RT, ROW_E])
        bounds = sb(nc, scope, "bounds", [P, NT - 1])
        junk = sb(nc, scope, "junk", [P, ET_PAD])
        last = sb(nc, scope, "last", [ROWS, RT])
        tile_no = sb(nc, scope, "tile_no", [ROWS, RT])
        crossed = sb(nc, scope, "crossed", [ROWS, RT])
        fin = sb(nc, scope, "fin", [ROWS, RT])
        fin_b = sb(nc, scope, "fin_b", [P, ET_PAD])
        step_no = sb(nc, scope, "step_no", [P, RT])
        edge_t = sb(nc, scope, "edge_t", [P, RT])
        edge_i = sb(nc, scope, "edge_i", [P, RT], I32)
        node_t = sb(nc, scope, "node_t", [P, RT])
        node_i = sb(nc, scope, "node_i", [P, RT], I32)
        base = sb(nc, scope, "base", [P, RT])
        rows = sb(nc, scope, "rows", [P, RT, ROW_E])
        dl = sb(nc, scope, "dl", [P, RT, P])
        ge = sb(nc, scope, "ge", [P, RT, P])
        valid = sb(nc, scope, "valid", [P, RT, P])
        edge = sb(nc, scope, "edge", [P, 2, RT, P])
        flag = sb(nc, scope, "flag", [P, 3, RT, P])
        cont = sb(nc, scope, "cont", [P, RT])
        tp = [ps(nc, scope, f"tp{k}") for k in range(4)]
        loaded = m.sem("edges_loaded")
        consts = m.sem("consts_made")
        padded = m.sem("pads_written")
        table = m.sem("edge_table_stored")
        fin_ready = m.sem("fin_ready")
        fin_moved = m.sem("fin_moved")
        tiles_known = m.sem("tiles_known")
        gathered = m.sem("rows_of_steps_gathered")
        flags_made = m.sem("flags_made")
        stored = m.sem("step_tables_stored")
        turned = m.sem("steps_turned")
        copied = m.sem("steps_copied")
        own = m.sem("steps_dve")
        n_loads = 0

        def rows_of(t):
            return min(ROWS, E // P - t * ROWS)

        with nc.Block() as block:
            @block.gpsimd
            def _(pool):
                pool.memset(ei[:, :, 0:P], 0).then_inc(padded, 1)
                pool.memset(ei[:, :, P:ROW_E], PAD_DST).then_inc(padded, 1)
                pool.memset(m.ones[:, :], 1.0).then_inc(consts, 1)
                pool.memset(m.ident[:, :], 0.0).then_inc(consts, 1)
                pool.wait_ge(consts, 2)
                pool.affine_select(out=m.ident[:, :], in_=m.ident[:, :], compare_op=ALU.not_equal, fill=1.0,
                                   base=0, pattern=[[-1, P]], channel_multiplier=1).then_inc(consts, 1)
                pool.iota(m.lane[:, :], pattern=[[0, 1]], base=0, channel_multiplier=1,
                          allow_small_or_imprecise_dtypes=True).then_inc(consts, 1)
                pool.iota(m.iota[:, :], pattern=[[1, NODES_T]], base=0, channel_multiplier=0,
                          allow_small_or_imprecise_dtypes=True).then_inc(consts, 1)
                pool.iota(bounds[:, :], pattern=[[NODES_T, NT - 1]], base=NODES_T, channel_multiplier=0,
                          allow_small_or_imprecise_dtypes=True).then_inc(consts, 1)
                pool.iota(tile_no[:, :], pattern=[[ROWS, RT]], base=0, channel_multiplier=1,
                          allow_small_or_imprecise_dtypes=True).then_inc(consts, 1)
                pool.iota(step_no[:, :], pattern=[[P, RT]], base=0, channel_multiplier=1,
                          allow_small_or_imprecise_dtypes=True).then_inc(consts, 1)
                pool.wait_ge(tiles_known, 1)
                pool.wait_ge(table, 16)
                for c in range(RT):
                    pool.indirect_dma_start(
                        out=rows[:, c, :], out_offset=None, in_=m.edge_tab[:, :],
                        in_offset=bass.IndirectOffsetOnAxis(ap=edge_i[:, c:c + 1].bitcast(U32), axis=0),
                    ).then_inc(gathered, 16)

            @block.sync
            def _(sp):
                nonlocal n_loads
                sp.wait_ge(padded, 2)
                for t in range(RT):
                    full = rows_of(t)
                    first = t * ROWS
                    sp.dma_start(ei[0:full, t, 0:P],
                                 bass.AP(tensor=m.src.tensor, offset=first * P, ap=[[P, full], [1, P]])
                                 ).then_inc(loaded, 16)
                    lo = 1 if t == 0 else 0
                    sp.dma_start(ei[lo:full, t, P:ROW_E],
                                 bass.AP(tensor=m.dst.tensor, offset=(first + lo) * P - 1,
                                         ap=[[P, full - lo], [1, WIN]])).then_inc(loaded, 16)
                    n_loads += 2
                rest = E - (E // P) * P
                row = E // P - (RT - 1) * ROWS
                sp.dma_start(ei[0:1, 0, P + 1:ROW_E], m.dst[0:WIN - 1].rearrange("(a b) -> a b", a=1)).then_inc(loaded, 16)
                sp.dma_start(ei[row:row + 1, RT - 1, 0:rest], m.src[E - rest:E].rearrange("(a b) -> a b", a=1)
                             ).then_inc(loaded, 16)
                sp.dma_start(ei[row:row + 1, RT - 1, P:P + 1 + rest],
                             m.dst[E - rest - 1:E].rearrange("(a b) -> a b", a=1)).then_inc(loaded, 16)
                n_loads += 3
                sp.wait_ge(own, 1)
                sp.dma_start(m.edge_tab.rearrange("(t p) c -> p t c", p=ROWS), ef[:, :, :]).then_inc(table, 16)
                sp.wait_ge(fin_ready, 1)
                sp.dma_start(m.last_step.rearrange("(t p) -> p t", p=ROWS), fin[:, :]).then_inc(fin_moved, 16)
                sp.wait_ge(fin_moved, 16)
                sp.dma_start(fin_b[:, :], m.last_step.rearrange("(a b) -> a b", a=1).to_broadcast([P, ET_PAD])
                             ).then_inc(fin_moved, 16)
                sp.wait_ge(tiles_known, 1)
                sp.dma_start(m.step_node.rearrange("(c p) -> p c", p=P), node_i[:, :]).then_inc(stored, 16)
                sp.wait_ge(flags_made, 1)
                whole = STEPS // P
                part = STEPS - whole * P
                for k, t in ((None, dl), (0, flag), (1, flag)):
                    there = m.step_dl if k is None else m.step_flags[k]
                    here = t if k is None else t[:, k]
                    sp.dma_start(there[0:whole * P].rearrange("(c p) e -> p c e", p=P),
                                 here[:, 0:whole, :]).then_inc(stored, 16)
                    sp.dma_start(there[whole * P:STEPS], here[0:part, whole, :]).then_inc(stored, 16)
                sp.dma_start(m.step_cont.rearrange("(c p) -> p c", p=P), cont[:, :]).then_inc(stored, 16)
                sp.wait_ge(stored, 16 * 8)
                sp.dma_start(m.node_tab[:, :], m.step_node[0:STEPS].rearrange("(a b) -> a b", a=1)).then_inc(stored, 16)
                sp.dma_start(m.cont_dl[:, :], bass.AP(tensor=m.step_cont.tensor, offset=0,
                                                      ap=[[0, H1], [GROUP, BATCHES + 2]])).then_inc(stored, 16)
                sp.wait_ge(stored, 16 * 10)

            @block.vector
            def _(dve):
                me = Chain(dve, own)
                dve.wait_ge(loaded, 16 * n_loads)
                me.done(dve.tensor_copy(ef[:, :, :], ei[:, :, :]))
                me.wait()
                dve.wait_ge(consts, 8)
                me.done(dve.tensor_scalar(last[:, :], ef[:, :, ROW_E - 2], float(N - 1), None, ALU.min))
                me.wait()
                for t in range(RT):
                    me.done(dve.tensor_scalar(junk[0:ROWS, 0:NT - 1], bounds[0:ROWS, :], last[:, t:t + 1], None,
                                              ALU.is_le, ALU.add, accum_out=crossed[:, t:t + 1]))
                    me.wait()
                dve.tensor_tensor(fin[:, :], crossed[:, :], tile_no[:, :], ALU.add).then_inc(fin_ready, 1)
                dve.wait_ge(fin_moved, 32)
                for c in range(RT):
                    me.done(dve.tensor_scalar(junk[:, :], fin_b[:, :], step_no[:, c:c + 1], None,
                                              ALU.is_lt, ALU.add, accum_out=edge_t[:, c:c + 1]))
                    me.wait()
                me.done(dve.tensor_tensor(node_t[:, :], step_no[:, :], edge_t[:, :], ALU.subtract))
                me.done(dve.tensor_scalar(edge_i[:, :], edge_t[:, :], float(ET_PAD - 1), None, ALU.min))
                me.wait()
                me.done(dve.tensor_scalar(node_t[:, :], node_t[:, :], float(NT - 1), None, ALU.min))
                me.wait()
                me.done(dve.tensor_scalar(base[:, :], node_t[:, :], float(NODES_T), None, ALU.mult))
                me.wait()
                dve.tensor_copy(node_i[:, :], node_t[:, :]).then_inc(tiles_known, 1)
                dve.wait_ge(gathered, 16 * RT)
                mid = rows[:, :, P + 1:ROW_E - 1]
                for c in range(RT):
                    me.done(dve.tensor_scalar(dl[:, c, :], rows[:, c, P + 1:ROW_E - 1], base[:, c:c + 1], None,
                                              ALU.subtract))
                me.done(dve.tensor_tensor(edge[:, 0], mid, rows[:, :, P:ROW_E - 2], ALU.not_equal))
                me.done(dve.tensor_tensor(edge[:, 1], mid, rows[:, :, P + 2:ROW_E], ALU.not_equal))
                me.wait()
                me.done(dve.tensor_scalar(ge[:, :, :], dl[:, :, :], 0.0, None, ALU.is_ge))
                me.wait()
                me.done(dve.scalar_tensor_tensor(valid[:, :, :], dl[:, :, :], float(NODES_T - 1), ge[:, :, :],
                                                 ALU.is_le, ALU.mult))
                me.wait()
                for k in range(2):
                    me.done(dve.scalar_tensor_tensor(flag[:, k], edge[:, k], -BIG, valid[:, :, :],
                                                     ALU.mult, ALU.mult))
                me.done(dve.tensor_scalar(flag[:, 2], valid[:, :, :], 2 * BIG, -BIG, ALU.mult, ALU.add))
                me.done(dve.tensor_scalar(ge[:, :, 0], edge[:, 0, :, 0], -1.0, 1.0, ALU.mult, ALU.add))
                me.wait()
                me.done(dve.tensor_tensor(ge[:, :, 0], ge[:, :, 0], valid[:, :, 0], ALU.mult))
                me.wait()
                me.done(dve.scalar_tensor_tensor(cont[:, :], dl[:, :, 0], 1.0, ge[:, :, 0], ALU.add, ALU.mult))
                me.wait()
                dve.tensor_scalar(cont[:, :], cont[:, :], -1.0, None, ALU.add).then_inc(flags_made, 1)
                for q in range(3 * RT):
                    c = q // 3
                    w = min(P, STEPS - c * P)
                    there = (m.idx_all, m.dl_all, m.in_all)[q % 3][:, c * P:c * P + w]
                    dve.wait_ge(turned, q + 1)
                    dve.tensor_copy(there, tp[q % 4][:, 0:w]).then_inc(copied, 1)

            @block.tensor
            def _(pe):
                pe.wait_ge(consts, 8)
                pe.wait_ge(gathered, 16 * RT)
                pe.wait_ge(flags_made, 1)
                for q in range(3 * RT):
                    c = q // 3
                    w = min(P, STEPS - c * P)
                    if q >= 4:
                        pe.wait_ge(copied, q - 3)
                    pe.transpose(tp[q % 4][:, 0:w], (rows[0:w, c, 0:P], dl[0:w, c, :], flag[0:w, 2, c, :])[q % 3],
                                 m.ident[0:w, 0:w]).then_inc(turned, 1)


def fold_weights(nc, m):
    with ExitStack() as scope:
        names = ["fc1", "wb0", "fc2", "wb1"]
        raw = sb(nc, scope, "raw", [P, 2, 3 * D + 2 * D])
        wqkv = sb(nc, scope, "wqkv", [P, 2, 3 * D])
        att = sb(nc, scope, "att", [P, 2, 4])
        head_of = sb(nc, scope, "head_of", [P, 2, H1])
        mask = sb(nc, scope, "mask", [P, 2, H1])
        spread = sb(nc, scope, "spread", [P, 2, 2 * H1 + 2])
        tp = [ps(nc, scope, f"wt{k}") for k in range(4)]
        fp = [ps(nc, scope, f"wf{k}") for k in range(2)]
        loaded = m.sem("weights_loaded")
        iota_done = m.sem("weights_iota")
        turned = m.sem("weights_turned")
        copied = m.sem("weights_copied")
        own = m.sem("weights_dve")
        folded = m.sem("weights_folded")
        blocks = []
        for k, (dest, off) in enumerate([(m.w1e, 0), (m.wb0T, 0), (m.w2e, 0)]):
            for r in range(2):
                for c in range(2):
                    blocks.append((raw[:, r, k * D + c * P:k * D + c * P + P], dest[:, c, r * P:r * P + P]))
        for r in range(2):
            for c in range(4):
                blocks.append((raw[:, r, 3 * D + c * P:3 * D + c * P + P], m.wb1T[:, c, r * P:r * P + P]))
        for r in range(2):
            for c in range(2):
                blocks.append((wqkv[:, r, c * P:c * P + P], m.wqT[:, c, r * P:r * P + P]))
        loads = 0

        with nc.Block() as block:
            @block.sync
            def _(sp):
                nonlocal loads
                def load(to, frm):
                    nonlocal loads
                    sp.dma_start(to, frm).then_inc(loaded, 16)
                    loads += 1
                for k, name in enumerate(["L0_gnn_fc1_w", "L0_gnn_wb0", "L0_gnn_fc2_w"]):
                    load(raw[:, :, k * D:k * D + D], m.io[name].rearrange("(r p) c -> p r c", p=P))
                load(raw[:, :, 3 * D:5 * D], m.io["L0_gnn_wb1"].rearrange("(r p) c -> p r c", p=P))
                load(wqkv[:, :, :], m.io["L0_mix_w_qkv"].rearrange("(r p) c -> p r c", p=P))
                for k, name in enumerate(["L0_gnn_attn_l1", "L0_gnn_attn_r1", "L0_gnn_attn_l2", "L0_gnn_attn_r2"]):
                    load(att[:, :, k], m.io[name].rearrange("h d -> (h d)").rearrange("(r p) -> p r", p=P))
                for k, name in enumerate(["L0_gnn_bias1", "L0_gnn_bias2", "L0_ffn_gate_b"]):
                    w = EXPERTS if k == 2 else D
                    to = m.gate_bb[:, :] if k == 2 else m.bias_b[:, k, :]
                    load(to, m.io[name].rearrange("(a b) -> a b", a=1).to_broadcast([P, w]))
                for k, name in enumerate(["L0_gnn_bb0", "L0_gnn_bb1", "L0_mix_b_fc2"]):
                    load(m.brow[:, k, :], m.io[name].rearrange("(a b) -> a b", a=1))
                load(m.brow[:, 3:6, :], m.io["L0_mix_b_qkv"].rearrange("(a k b) -> a k b", a=1, k=3))
                load(m.gate_w[:, :, :], m.io["L0_ffn_gate_w"].rearrange("(r p) c -> p r c", p=P))
                sp.wait_ge(loaded, 16 * loads)

            @block.gpsimd
            def _(pool):
                pool.iota(head_of[:, :, :], pattern=[[P, 2], [-D1, H1]], base=0, channel_multiplier=1,
                          allow_small_or_imprecise_dtypes=True).then_inc(iota_done, 1)
                pool.memset(m.zeros[:, :], 0.0).then_inc(iota_done, 1)
                pool.memset(m.half[:, :], -0.5).then_inc(iota_done, 1)

            @block.tensor
            def _(pe):
                pe.wait_ge(loaded, 16 * loads)
                for q, (frm, _to) in enumerate(blocks):
                    if q >= 4:
                        pe.wait_ge(copied, q - 3)
                    pe.transpose(tp[q % 4][:, 0:P], frm, m.ident[:, :]).then_inc(turned, 1)
                pe.wait_ge(folded, 1)
                for k, (w, cols, c0) in enumerate([(0, 2 * H1, 0), (2, 2, 2 * H1)]):
                    for c in range(2):
                        for r in range(2):
                            ins = pe.matmul(fp[k][:, c * 32:c * 32 + cols], raw[:, r, w * D + c * P:w * D + c * P + P],
                                            spread[:, r, c0:c0 + cols], start=(r == 0), stop=(r == 1))
                ins.then_inc(folded, 1)

            @block.vector
            def _(dve):
                me = Chain(dve, own)
                dve.wait_ge(loaded, 16 * loads)
                dve.wait_ge(iota_done, 3)
                me.done(dve.tensor_scalar(mask[:, :, :], head_of[:, :, :], 0.0, None, ALU.is_ge))
                me.wait()
                me.done(dve.scalar_tensor_tensor(mask[:, :, :], head_of[:, :, :], float(D1 - 1), mask[:, :, :],
                                                 ALU.is_le, ALU.mult))
                me.wait()
                for r in range(2):
                    for k in range(2):
                        me.done(dve.tensor_scalar(spread[:, r, k * H1:k * H1 + H1], mask[:, r, :], att[:, r, k:k + 1],
                                                  None, ALU.mult))
                me.done(dve.tensor_copy(spread[:, :, 2 * H1:2 * H1 + 2], att[:, :, 2:4]))
                me.wait()
                dve.sem_inc(folded, 1)
                for q, (_frm, to) in enumerate(blocks):
                    dve.wait_ge(turned, q + 1)
                    dve.tensor_copy(to, tp[q % 4][:, 0:P]).then_inc(copied, 1)
                dve.wait_ge(folded, 2)
                for c in range(2):
                    me.done(dve.tensor_copy(m.w1e[:, c, D:D + 2 * H1], fp[0][:, c * 32:c * 32 + 2 * H1]))
                    me.done(dve.tensor_copy(m.w2e[:, c, D:D + 2], fp[1][:, c * 32:c * 32 + 2]))
                me.done(dve.tensor_copy(m.wkv[:, :, :], wqkv[:, :, D:3 * D]))
                me.wait()


def project_nodes(nc, m):
    with ExitStack() as scope:
        xt = sb(nc, scope, "xt", [NODES_T, 2, D])
        stats = sb(nc, scope, "stats", [NODES_T, 2, 6])
        mv = sb(nc, scope, "mv", [NODES_T, 2, 2])
        rstd = sb(nc, scope, "rstd", [NODES_T, 2])
        xn = sb(nc, scope, "xn", [NODES_T, 2, D + 1])
        xT = sb(nc, scope, "xT", [P, 2, 2, NODES_T])
        stage = sb(nc, scope, "stage", [NODES_T, 2, ROW1])
        skip = sb(nc, scope, "skip", [NODES_T, 2, 2, D])
        pT = [ps(nc, scope, f"pT{k}") for k in range(2)]
        pA = [ps(nc, scope, f"pA{k}") for k in range(2)]
        pZ = [ps(nc, scope, f"pZ{k}") for k in range(2)]
        pG = [ps(nc, scope, f"pG{k}") for k in range(2)]
        x_in = [m.sem(f"x_loaded{u}") for u in range(2)]
        x_used = m.sem("x_used")
        var_ready = m.sem("var_ready")
        rstd_ready = m.sem("rstd_ready")
        xn_ready = m.sem("xn_ready")
        xn_used = m.sem("xn_used")
        xT_done = m.sem("xT_done")
        xT_ready = m.sem("xT_ready")
        proj_done = m.sem("proj_done")
        sent = [m.sem(f"proj_sent{u}") for u in range(2)]
        xn_sent = [m.sem(f"xn_sent{u}") for u in range(2)]
        own = m.sem("proj_dve")
        base_ready = m.sem("proj_base")
        psum_used = m.sem("proj_psum_used")

        with nc.Block() as block:
            @block.sync
            def _(sp):
                def load(i):
                    for u in range(2):
                        t = i * 2 + u
                        sp.wait_ge(x_used, t + 1)
                        sp.dma_start(xt[:, u, :], m.x[bass.ds(t * NODES_T, NODES_T), :]).then_inc(x_in[u], 16)

                def store(i):
                    for u in range(2):
                        t = i * 2 + u
                        sp.wait_ge(xn_ready, t + 1)
                        sp.dma_start(m.xn_d[bass.ds(t * NODES_T, NODES_T), :], xn[:, u, 0:D]).then_inc(xn_sent[u], 16)
                        sp.wait_ge(xT_ready, t + 1)
                        sp.dma_start(m.xT_d[bass.ds(t * P, P), :], xT[:, u].rearrange("p c n -> p (c n)")).then_inc(xn_sent[u], 16)

                load(0)
                with nc.sync.Fori(0, NT // 2 - 1) as i:
                    load(i + 1)
                    store(i)
                store(NT // 2 - 1)
                for u in range(2):
                    sp.wait_ge(sent[u], 16 * 2 * (NT // 2) + 32)
                    sp.wait_ge(xn_sent[u], 16 * 2 * (NT // 2) + 32)

            @block.gpsimd
            def _(pool):
                pool.memset(xn[:, :, D:D + 1], 1.0).then_inc(base_ready, 1)
                for u in range(2):
                    pool.memset(stage[:, u, 0:H1 * (D1 + 1)], 1.0).then_inc(base_ready, 1)
                with nc.gpsimd.Fori(0, NT) as t:
                    pool.wait_ge(var_ready, t + 1)
                    pool.tensor_tensor(rstd[:, 0:1], mv[:, 0, 1:2], m.half[0:NODES_T, :], ALU.pow).then_inc(rstd_ready, 1)

            @block.vector
            def _(dve):
                dve.sem_inc(x_used, 2)
                dve.sem_inc(xn_used, 2)
                for u in range(2):
                    dve.sem_inc(sent[u], 32)
                    dve.sem_inc(xn_sent[u], 32)
                dve.wait_ge(base_ready, 3)
                with nc.vector.Fori(0, NT // 2) as i:
                    me = Chain(dve, own, i, 8)
                    for u in range(2):
                        t = i * 2 + u
                        dve.wait_ge(x_in[u], 16 * i + 16)
                        me.done(dve.bn_stats(stats[:, u, :], xt[:, u, :]))
                        me.wait_apart(m.hold)
                        me.done(dve.bn_aggr(mv[:, 1, :], stats[:, u, :]))
                        me.wait()
                        dve.tensor_scalar(mv[:, 0, 1:2], mv[:, 1, 1:2], EPS, None, ALU.add).then_inc(var_ready, 1)
                        dve.wait_ge(rstd_ready, t + 1)
                        dve.wait_ge(xn_used, t + 1)
                        dve.wait_ge(xn_sent[u], 32 * i + 32)
                        me.done(dve.tensor_scalar(xn[:, u, 0:D], xt[:, u, :], mv[:, 1, 0:1], rstd[:, 0:1],
                                                  ALU.subtract, ALU.mult))
                        me.wait()
                        dve.sem_inc(xn_ready, 1)
                        me.done(dve.tensor_copy(mv[:, 0, 0:1], mv[:, 1, 0:1]))
                        dve.sem_inc(x_used, 1)
                    me.close()

            @block.tensor
            def _(pe):
                for c in range(2):
                    pe.matmul(pG[c][:, 0:D + 1], m.zeros[:, 0:P], m.zeros[:, 0:D + 1], start=True, stop=False,
                              skip_group_check=True)
                def turn_and_sum(t, u):
                    pe.wait_ge(xn_ready, t + 1)
                    for c in range(2):
                        ins = pe.transpose(pT[u][:, c * NODES_T:(c + 1) * NODES_T], xn[:, u, c * P:c * P + P],
                                           m.ident[0:NODES_T, 0:NODES_T])
                    ins.then_inc(xT_done, 1)
                    for c in range(2):
                        ins = pe.matmul(pG[c][:, 0:D + 1], xn[:, u, c * P:c * P + P], xn[:, u, :], start=False,
                                        stop=False, skip_group_check=True)
                    ins.then_inc(xn_used, 1)

                def project(t, u):
                    pe.wait_ge(xT_ready, t + 1)
                    pe.wait_ge(psum_used, t + 1)
                    for c in range(2):
                        pe.matmul(pA[u][0:NODES_T, 0:D + 16], xT[:, u, c, :], m.w1e[:, c, :],
                                  start=(c == 0), stop=(c == 1))
                    for k, w in enumerate((m.wb0T, m.wb1T)):
                        at = pZ[u][0:NODES_T, k * D:k * D + D]
                        for c in range(2):
                            pe.matmul(at, xT[:, u, c, :], w[:, c, :], start=(c == 0), stop=False)
                        ins = pe.matmul(at, m.ones[0:1, 0:NODES_T], m.brow[:, k, :], start=False, stop=True)
                    ins.then_inc(proj_done, 1)

                turn_and_sum(0, 0)
                with nc.tensor.Fori(0, NT // 2 - 1) as i:
                    for u in range(2):
                        turn_and_sum(i * 2 + (u + 1), 1 - u)
                        project(i * 2 + u, u)
                turn_and_sum(NT - 1, 1)
                project(NT - 2, 0)
                project(NT - 1, 1)

            @block.scalar
            def _(act):
                def take_turned(t, u, fill):
                    act.wait_ge(xT_done, t + 1)
                    act.wait_ge(xn_sent[u], 32 * fill + 32)
                    act.copy(xT[:, u].rearrange("p c n -> p (c n)"), pT[u][:, 0:2 * NODES_T]).then_inc(xT_ready, 1)

                def take_products(t, u, i):
                    act.wait_ge(proj_done, t + 1)
                    act.wait_ge(sent[u], 32 * i + 32)
                    act.copy(stage[:, u, 0:H1 * (D1 + 1)].rearrange("p (h c) -> p h c", h=H1)[:, :, 0:D1],
                             pA[u][0:NODES_T, 0:D].rearrange("p (h c) -> p h c", h=H1)).then_inc(m.act_own, 1)
                    act.copy(stage[:, u, H1 * (D1 + 1):], pA[u][0:NODES_T, D:D + H1]).then_inc(m.act_own, 1)
                    act.copy(m.er1[:, bass.ds(t, 1), :], pA[u][0:NODES_T, D + H1:D + 2 * H1].rearrange("p (a h) -> p a h", a=1)).then_inc(m.act_own, 1)
                    act.copy(skip[:, u].rearrange("p k d -> p (k d)"), pZ[u][0:NODES_T, :]).then_inc(m.act_own, 1)
                    act.wait_ge(m.act_own, t * 4 + 4)
                    act.sem_inc(psum_used, 1)
                    at = bass.ds(t * NODES_T, NODES_T)
                    act.dma_start(m.tab1[at, :], stage[:, u, :]).then_inc(sent[u], 16)
                    act.dma_start(m.z_d[at, :], skip[:, u].rearrange("p k d -> p (k d)")).then_inc(sent[u], 16)

                act.sem_inc(psum_used, 2)
                take_turned(0, 0, 0)
                with nc.scalar.Fori(0, NT // 2 - 1) as i:
                    for u in range(2):
                        take_turned(i * 2 + (u + 1), 1 - u, i + u)
                        take_products(i * 2 + u, u, i)
                take_turned(NT - 1, 1, NT // 2 - 1)
                take_products(NT - 2, 0, NT // 2 - 1)
                take_products(NT - 1, 1, NT // 2 - 1)

        with nc.Block() as block:
            @block.vector
            def _(dve):
                for c in range(2):
                    dve.tensor_copy(m.gram[:, c, :], pG[c][:, 0:D + 1]).then_inc(m.gram_ready, 1)
                dve.wait_ge(m.gram_ready, 2)


def mixer_attention(nc, m):
    with ExitStack() as scope:
        G = m.gram
        srow = sb(nc, scope, "srow", [1, D])
        U = sb(nc, scope, "U", [P, 2, D])
        u0 = sb(nc, scope, "u0", [1, D])
        nrow = sb(nc, scope, "nrow", [1, 1])
        bqT = sb(nc, scope, "bqT", [P, 2])
        L = sb(nc, scope, "L", [P, 2, 64])
        mx = sb(nc, scope, "mx", [P, 2])
        sm = sb(nc, scope, "sm", [P, 2])
        BD = sb(nc, scope, "BD", [P, 2, P])
        BDT = sb(nc, scope, "BDT", [P, 2, P])
        pb = [ps(nc, scope, f"mp{k}") for k in range(6)]
        w1n = sb(nc, scope, "w1n", [P, 2, 1])
        own = m.sem("mix_dve")
        pe_done = m.sem("mix_pe")
        act_done = m.sem("mix_act")
        loaded = m.sem("mix_loaded")
        bq, bk, bv = m.brow[:, 3, :], m.brow[:, 4, :], m.brow[:, 5, :]
        Wk, Wv = m.wkv[:, :, 0:D], m.wkv[:, :, D:2 * D]
        flat = lambda name: m.io[name].rearrange("(r p) -> p r", p=P)

        with nc.Block() as block:
            @block.sync
            def _(sp):
                sp.dma_start(m.wf1[:, :, :], m.io["L0_mix_w_fc1"].rearrange("(r p) c -> p r c", p=P)).then_inc(loaded, 16)
                sp.dma_start(m.wf2[:, :, :], m.io["L0_mix_w_fc2"].rearrange("(r p) c -> p r c", p=P)).then_inc(loaded, 16)
                sp.dma_start(m.gain[:, :], flat("L0_mix_norm_g")).then_inc(loaded, 16)
                sp.dma_start(m.shift[:, :], flat("L0_mix_norm_b")).then_inc(loaded, 16)
                sp.dma_start(m.b1col[:, :], m.io["L0_mix_b_fc1"].rearrange("(r p) -> p r", p=P)).then_inc(loaded, 16)
                sp.dma_start(bqT[:, :], m.io["L0_mix_b_qkv"][0:D].rearrange("(r p) -> p r", p=P)).then_inc(loaded, 16)
                sp.wait_ge(loaded, 96)

            @block.tensor
            def _(pe):
                for c in range(2):
                    ins = pe.transpose(pb[0][0:1, c * P:c * P + P], G[:, c, D:D + 1], m.ident[:, :])
                ins.then_inc(pe_done, 1)
                pe.wait_ge(own, 1)
                for c in range(2):
                    for r in range(2):
                        pe.matmul(pb[1 + c][:, 0:D], G[:, r, c * P:c * P + P], Wv[:, r, :], start=(r == 0), stop=False)
                    pe.matmul(pb[1 + c][:, 0:D], srow[:, c * P:c * P + P], bv, start=False, stop=True)
                for r in range(2):
                    pe.matmul(pb[3][0:1, 0:D], G[:, r, D:D + 1], Wv[:, r, :], start=(r == 0), stop=False)
                pe.wait_ge(own, 2)
                pe.matmul(pb[3][0:1, 0:D], nrow[:, :], bv, start=False, stop=True).then_inc(pe_done, 1)
                pe.wait_ge(own, 5)
                for c in range(2):
                    for r in range(2):
                        pe.matmul(pb[4 + c][:, 0:D], Wk[:, r, c * P:c * P + P], U[:, r, :], start=(r == 0), stop=False)
                    ins = pe.matmul(pb[4 + c][:, 0:D], bk[:, c * P:c * P + P], u0[:, :], start=False, stop=True)
                ins.then_inc(pe_done, 1)
                pe.wait_ge(loaded, 96)
                for q in range(6):
                    for r in range(2):
                        ins = pe.matmul(pb[0][:, 256 + q:257 + q], m.wf1[:, r, q * P:q * P + P], m.shift[:, r:r + 1],
                                        start=(r == 0), stop=(r == 1))
                ins.then_inc(pe_done, 1)
                pe.wait_ge(m.mix_bd, 1)
                for c in range(2):
                    ins = pe.transpose(pb[1][:, c * P:c * P + P], BD[:, c, :], m.ident[:, :])
                ins.then_inc(pe_done, 1)
                pe.wait_ge(m.mix_bd, 3)
                for c in range(2):
                    for r in range(2):
                        pe.matmul(pb[2 + r][:, c * P:c * P + P], m.wqT[:, c, r * P:r * P + P], BDT[:, c, :],
                                  start=True, stop=True)
                    ins = pe.matmul(pb[4][0:1, c * P:c * P + P], bqT[:, c:c + 1], BDT[:, c, :], start=True, stop=True)
                ins.then_inc(pe_done, 1)

            @block.vector
            def _(dve):
                me = Chain(dve, own)
                dve.wait_ge(pe_done, 1)
                me.done(dve.tensor_copy(srow[:, :], pb[0][0:1, 0:D]))
                me.done(dve.memset(nrow[:, :], float(N)))
                dve.wait_ge(pe_done, 2)
                for c in range(2):
                    me.done(dve.tensor_copy(U[:, c, :], pb[1 + c][:, 0:D]))
                me.done(dve.tensor_copy(u0[:, :], pb[3][0:1, 0:D]))
                me.done(dve.memset(BD[:, :, :], 0.0))
                dve.wait_ge(pe_done, 3)
                for c in range(2):
                    for h in range(2):
                        lo = 64 * h
                        me.done(dve.tensor_scalar(L[lo:lo + 64, c, :],
                                                  pb[4 + c][lo:lo + 64, (2 * c + h) * 64:(2 * c + h + 1) * 64],
                                                  64.0 ** -0.5, None, ALU.mult))
                me.wait()
                me.done(dve.tensor_reduce(mx[:, :], L[:, :, :], AX, ALU.max))
                me.wait()
                me.done(dve.tensor_scalar(mx[:, :], mx[:, :], -1.0, None, ALU.mult))
                me.wait()
                dve.sem_inc(m.mix_max, 1)
                dve.wait_ge(act_done, 2)
                me.done(dve.reciprocal(sm[:, :], sm[:, :]))
                me.wait()
                for c in range(2):
                    for h in range(2):
                        lo = 64 * h
                        me.done(dve.tensor_scalar(BD[lo:lo + 64, c, lo:lo + 64], L[lo:lo + 64, c, :],
                                                  sm[lo:lo + 64, c:c + 1], None, ALU.mult))
                me.wait()
                dve.sem_inc(m.mix_bd, 1)
                dve.wait_ge(pe_done, 5)
                for c in range(2):
                    dve.tensor_copy(BDT[:, c, :], pb[1][:, c * P:c * P + P]).then_inc(m.mix_bd, 1)
                me.done(dve.tensor_tensor(m.b1col[:, :], m.b1col[:, :], pb[0][:, 256:262], ALU.add))
                for r in range(2):
                    me.done(dve.tensor_scalar(m.wf1[:, r, :], m.wf1[:, r, :], m.gain[:, r:r + 1], None, ALU.mult))
                dve.wait_ge(pe_done, 6)
                for r in range(2):
                    me.done(dve.tensor_copy(m.wx[:, r, :], pb[2 + r][:, 0:D]))
                me.done(dve.tensor_copy(m.brow[:, 3, :], pb[4][0:1, 0:D]))
                me.wait()

            @block.scalar
            def _(act):
                act.wait_ge(m.mix_max, 1)
                for c in range(2):
                    act.activation(L[:, c, :], L[:, c, :], ACT.Exp, bias=mx[:, c:c + 1],
                                   accum_out=sm[:, c:c + 1]).then_inc(act_done, 1)


def mixer(nc, m):
    W = 2 * NODES_T
    with ExitStack() as scope:
        xn = sb(nc, scope, "mxn", [NODES_T, 2, 2, D])
        xT = sb(nc, scope, "mxT", [P, 2, 2, W])
        r = sb(nc, scope, "mr", [NODES_T, 2, 2, D])
        hn = sb(nc, scope, "mhn", [NODES_T, 2, D])
        stats = sb(nc, scope, "mstats", [NODES_T, 2, 6])
        mv = sb(nc, scope, "mmv", [NODES_T, 2, 2])
        var = sb(nc, scope, "mvar", [NODES_T, 2])
        rstd = sb(nc, scope, "mrstd", [NODES_T, 2])
        hT = sb(nc, scope, "mhT", [P, 2, W])
        gT = sb(nc, scope, "mgT", [P, 6, W])
        bias = sb(nc, scope, "mbias", [NODES_T, 2, D])
        o = sb(nc, scope, "mo", [NODES_T, 2, 2, D])
        pX = ps(nc, scope, "pX")
        pH = ps(nc, scope, "pH")
        pF = [ps(nc, scope, f"pF{k}") for k in range(4)]
        pY = ps(nc, scope, "pY")
        inn = [m.sem(f"mix_in{u}") for u in range(2)]
        used = m.sem("mix_in_used")
        xf_done = m.sem("xf_done")
        var_ready = m.sem("mix_var")
        rstd_ready = m.sem("mix_rstd")
        hn_ready = m.sem("hn_ready")
        hT_done = m.sem("hT_done")
        hT_ready = m.sem("hT_ready")
        fc1_done = m.sem("fc1_done")
        gelu_done = m.sem("gelu_done")
        fc2_done = m.sem("fc2_done")
        out_ready = m.sem("mix_out_ready")
        y_used, rows_spread = m.sem("mix_y_used"), m.sem("mix_rows_spread")
        sent = [m.sem(f"mix_sent{u}") for u in range(2)]
        own = m.sem("mixer_dve")
        pairs = NT // 2

        with nc.Block() as block:
            @block.sync
            def _(sp):
                def load(p, u):
                    at = bass.ds(p * W, W)
                    sp.wait_ge(used, p + 1)
                    sp.dma_start(xn[:, u], m.xn_d[at, :].rearrange("(k p) d -> p k d", p=NODES_T)).then_inc(inn[u], 16)
                    sp.dma_start(xT[:, u], m.xT_d[bass.ds(p * 2 * P, 2 * P), :].rearrange("(k p) d -> p k d", p=P)
                                 ).then_inc(inn[u], 16)

                def turn(p, u, i, more):
                    if more:
                        load(p + 1, 1 - u)
                load(0, 0)
                over_pairs(nc.sync, turn)
                sp.wait_ge(sent[0], 16 * (pairs - pairs // 2) + 16)
                sp.wait_ge(sent[1], 16 * (pairs // 2) + 16)

            @block.gpsimd
            def _(pool):
                def turn(p, u, i, more):
                    pool.wait_ge(var_ready, p + 1)
                    pool.tensor_tensor(rstd[:, :], var[:, :], m.half[0:NODES_T, :].to_broadcast([NODES_T, 2]), ALU.pow).then_inc(rstd_ready, 1)
                over_pairs(nc.gpsimd, turn)

            @block.vector
            def _(dve):
                dve.sem_inc(used, 2)
                for u in range(2):
                    dve.sem_inc(sent[u], 16)

                def normalise(me, p, u):
                    dve.wait_ge(xf_done, p + 1)
                    me.done(dve.tensor_tensor(r[:, u].rearrange("p k d -> p (k d)"), xn[:, u].rearrange("p k d -> p (k d)"),
                                              pX[0:NODES_T, :], ALU.add))
                    me.wait()
                    dve.sem_inc(used, 1)
                    me.done(dve.tensor_tensor(r[:, u], r[:, u], bias[:, 0:1, :].to_broadcast([NODES_T, 2, D]), ALU.add))
                    me.wait()
                    for k in range(2):
                        me.done(dve.bn_stats(stats[:, k, :], r[:, u, k, :]))
                    me.wait_apart(m.hold)
                    for k in range(2):
                        me.done(dve.bn_aggr(mv[:, k, :], stats[:, k, :]))
                    me.wait()
                    dve.tensor_scalar(var[:, :], mv[:, :, 1], EPS, None, ALU.add).then_inc(var_ready, 1)
                    dve.wait_ge(rstd_ready, p + 1)
                    for k in range(2):
                        me.done(dve.tensor_scalar(hn[:, k, :], r[:, u, k, :], mv[:, k, 0:1], rstd[:, k:k + 1],
                                                  ALU.subtract, ALU.mult))
                    me.wait()
                    dve.sem_inc(hn_ready, 1)

                def turn(p, u, i, more):
                    me = Chain(dve, own, p, 10 if more else 2, start.n if more else start.n + 8 * (pairs - 1))
                    if more:
                        normalise(me, p + 1, 1 - u)
                    me.done(dve.tensor_tensor(r[:, u], r[:, u], bias[:, 1:2, :].to_broadcast([NODES_T, 2, D]), ALU.add))
                    me.wait()
                    dve.wait_ge(fc2_done, p + 1)
                    dve.wait_ge(sent[u], 16 * i + 16)
                    me.done(dve.tensor_tensor(o[:, u].rearrange("p k d -> p (k d)"), r[:, u].rearrange("p k d -> p (k d)"),
                                              pY[0:NODES_T, :], ALU.add))
                    me.wait()
                    dve.sem_inc(out_ready, 1)
                    dve.sem_inc(y_used, 1)
                    me.close()
                start = Chain(dve, own)
                dve.wait_ge(rows_spread, 1)
                start.done(dve.tensor_copy(bias[:, :, :].rearrange("p k d -> p (k d)"), pY[0:NODES_T, :]))
                start.wait()
                dve.sem_inc(y_used, 1)
                normalise(start, 0, 0)
                over_pairs(nc.vector, turn)

            @block.tensor
            def _(pe):
                def attend(u, fill):
                    pe.wait_ge(inn[u], 32 * fill + 32)
                    for k in range(2):
                        at = pX[0:NODES_T, k * D:k * D + D]
                        for c in range(2):
                            ins = pe.matmul(at, xT[:, u, k, c * NODES_T:(c + 1) * NODES_T], m.wx[:, c, :],
                                            start=(c == 0), stop=(c == 1))
                    ins.then_inc(xf_done, 1)

                def turn_normed(p):
                    pe.wait_ge(hn_ready, p + 1)
                    for c in range(2):
                        for k in range(2):
                            ins = pe.transpose(pH[:, c * W + k * NODES_T:c * W + (k + 1) * NODES_T],
                                               hn[:, k, c * P:c * P + P], m.ident[0:NODES_T, 0:NODES_T])
                    ins.then_inc(hT_done, 1)

                def turn(p, u, i, more):
                    if more:
                        attend(1 - u, i + u)
                    pe.wait_ge(hT_ready, p + 1)
                    for q in range(6):
                        if q >= 4:
                            pe.wait_ge(gelu_done, p * 6 + (q - 3))
                        for c in range(2):
                            ins = pe.matmul(pF[q % 4][:, 0:W], m.wf1[:, c, q * P:q * P + P], hT[:, c, :],
                                            start=(c == 0), stop=(c == 1))
                        ins.then_inc(fc1_done, 1)
                    pe.wait_ge(gelu_done, p * 6 + 6)
                    pe.wait_ge(y_used, p + 1)
                    for k in range(2):
                        at = pY[0:NODES_T, k * D:k * D + D]
                        for q in range(6):
                            ins = pe.matmul(at, gT[:, q, k * NODES_T:(k + 1) * NODES_T], m.wf2[:, q, :],
                                            start=(q == 0), stop=(q == 5))
                        if k == 0 and more:
                            turn_normed(p + 1)
                    ins.then_inc(fc2_done, 1)
                for k, row in enumerate((3, 2)):
                    ins = pe.matmul(pY[0:NODES_T, k * D:k * D + D], m.ones[0:1, 0:NODES_T], m.brow[:, row, :],
                                    start=True, stop=True)
                ins.then_inc(rows_spread, 1)
                attend(0, 0)
                turn_normed(0)
                over_pairs(nc.tensor, turn)

            @block.scalar
            def _(act):
                def take_turned(p):
                    act.wait_ge(hT_done, p + 1)
                    act.copy(hT[:, :, :].rearrange("p c n -> p (c n)"), pH[:, 0:2 * W]).then_inc(hT_ready, 1)

                def turn(p, u, i, more):
                    for q in range(6):
                        act.wait_ge(fc1_done, p * 6 + (q + 1))
                        act.activation(gT[:, q, :], pF[q % 4][:, 0:W], ACT.Gelu, bias=m.b1col[:, q:q + 1]
                                       ).then_inc(gelu_done, 1)
                    if more:
                        take_turned(p + 1)
                    act.wait_ge(out_ready, p + 1)
                    act.dma_start(of_pair(m.mix_d, p), o[:, u]).then_inc(sent[u], 16)
                take_turned(0)
                over_pairs(nc.scalar, turn)


def convolve(nc, m, name, heads, width, table, er, acc, degree):
    H, C = heads, width + 1
    W = H * C + (1 if degree else 0)
    ROW = H * C + H
    folded = H == 1
    with ExitStack() as scope:
        def t(n, shape, dt=F32):
            return sb(nc, scope, f"{name}_{n}", shape, dt)

        idx = t("idx", [P, UNROLL, GROUP], I32)
        rows = t("rows", [P, UNROLL, GROUP, ROW])
        dl_b = t("dl_b", [NODES_T, 2, GE])
        flags = t("flags", [H, 2, 2, GE])
        hotT = t("hotT", [NODES_T, GE], BF16)
        hot = t("hot", [P, 2, GROUP, NODES_T])
        parts = t("parts", [NODES_T, NT, 3, H], BF16)
        rest = t("rest", [NODES_T, 2, NT, H])
        er_s = t("er_s", [NODES_T, 2, GROUP, 3, H], BF16)
        z = t("z", [P, GROUP, H])
        under = t("under", [P, GROUP, H])
        lz = t("lz", [P, GROUP, H])
        fw = t("fw", [H, GE])
        bw = t("bw", [H, GE])
        carry = t("carry", [H, 1])
        fall = t("fall", [H, 1])
        ln_scale = t("ln_scale", [H, NODES_T])
        scale = t("scale", [NODES_T, H])
        ex = t("ex", [P, GROUP, H])
        wr = t("wr", [P, GROUP, W]) if not folded else None
        pE = ps(nc, scope, f"{name}_pE")
        pT = ps(nc, scope, f"{name}_pT", (P, GE))
        pB = ps(nc, scope, f"{name}_pB")
        pA = [ps(nc, scope, f"{name}_pA{k}") for k in range(4)]
        s = lambda n: m.sem(f"{name}_{n}")
        loaded = [s(f"flags_in{u}") for u in range(2)]
        gathered = [s(f"rows_in{u}") for u in range(UNROLL)]
        idx_ready, rows_used, scans_done = s("idx_ready"), s("rows_used"), s("scans_done")
        hotT_ready, er_ready, er_done = s("hotT_ready"), s("er_ready"), s("er_done")
        lz_ready, lzT_done, c_back = s("lz_ready"), s("lzT_done"), s("c_back")
        sel_ready, sel_done, scale_ready = s("sel_ready"), s("sel_done"), s("scale_ready")
        t_ready, ex_ready, wr_ready = s("t_ready"), s("ex_ready"), s("wr_ready")
        agg_done, add_done, own, parts_ready = s("agg_done"), s("add_done"), s("own"), s("parts_ready")
        hot_ready, own_act, zeroed = s("hot_ready"), s("own_act"), s("expert_rows_zeroed")

        def turns(eng, body):
            with eng.Fori(0, BATCHES // UNROLL) as i:
                for u in range(UNROLL):
                    body(i * UNROLL + u, u, i)

        def after(u, i, ring, ahead=1):
            n = u + ahead
            return n % ring, i * (UNROLL // ring) + n // ring

        with nc.Block() as block:
            @block.sync
            def _(sp):
                def load(n, u):
                    sp.dma_start(dl_b[:, u, :],
                                 m.step_dl[bass.ds(n * GROUP, GROUP), :].rearrange("(a s) e -> a (s e)", a=1)
                                 .to_broadcast([NODES_T, GE])).then_inc(loaded[u], 16)
                    for k in range(2):
                        sp.dma_start(flags[:, u, k, :],
                                     m.step_flags[k, bass.ds(n * GROUP, GROUP), :].rearrange("(a s) e -> a (s e)", a=1)
                                     .to_broadcast([H, GE])).then_inc(loaded[u], 16)

                def turn(b, u, i):
                    sp.wait_ge(scans_done, b + 1)
                    sp.wait_ge(hotT_ready, b + 1)
                    load(b + 2, u % 2)
                load(0, 0)
                load(1, 1)
                if degree:
                    sp.dma_start(m.xbuf[0:EXPERTS * SLOTS, :].rearrange("(k p) d -> p k d", p=NODES_T),
                                 m.zeros[0:NODES_T, 0:D].rearrange("p (a d) -> p a d", a=1)
                                 .to_broadcast([NODES_T, EXPERTS * SLOTS // NODES_T, D])).then_inc(zeroed, 16)
                turns(nc.sync, turn)
                if degree:
                    sp.wait_ge(zeroed, 16)

            @block.gpsimd
            def _(pool):
                def gather(n, u):
                    pool.wait_ge(rows_used, n + 1)
                    pool.sem_inc(m.hold, 1)
                    pool.tensor_copy(idx[:, u, :], m.idx_all[:, bass.ds(n * GROUP, GROUP)]).then_inc(idx_ready, 1)
                    pool.wait_ge(idx_ready, n + 1)
                    pool.sem_inc(m.hold, 1)
                    for k in range(GROUP):
                        pool.indirect_dma_start(
                            out=rows[:, u, k, :], out_offset=None, in_=table[:, :],
                            in_offset=bass.IndirectOffsetOnAxis(ap=idx[:, u, k:k + 1].bitcast(U32), axis=0),
                        ).then_inc(gathered[u], 16)
                gather(0, 0)
                gather(1, 1)
                turns(nc.gpsimd, lambda b, u, i: gather(b + 2, (u + 2) % UNROLL))

            @block.scalar
            def _(act):
                regs = [act.alloc_register(f"{name}_act{k}") for k in range(UNROLL * GROUP)]

                def take_er(par, lot):
                    for k in range(GROUP):
                        j = act.snap(lot[k], min_val=0, max_val=NT - 1)
                        act.copy(er_s[:, par, k:k + 1].rearrange("p a c h -> p a (c h)"),
                                 parts[:, bass.ds(j, 1)].rearrange("p a c h -> p a (c h)")).then_inc(er_ready, 1)

                def one_hot_nodes(me, n, par, fill):
                    act.wait_ge(loaded[par], fill * 48 + 48)
                    me.done(act.activation(dl_b[:, par, :], dl_b[:, par, :], ACT.Abs, bias=m.lane[0:NODES_T, :],
                                           scale=-1.0))
                    me.wait()
                    act.activation(hotT[:, :], dl_b[:, par, :], ACT.Relu, bias=m.ones[0:NODES_T, 0:1], scale=-1.0
                                   ).then_inc(hotT_ready, 1)

                def one_hot_edges(me, n, par):
                    if folded:
                        return
                    for k in range(GROUP):
                        me.done(act.activation(hot[:, par, k, :], m.iota[:, :], ACT.Abs,
                                               bias=m.dl_all[:, bass.ds(n * GROUP + k, 1)], scale=-1.0))
                    me.wait()
                    act.activation(hot[:, par], hot[:, par], ACT.Relu, bias=m.ones[:, 0:1], scale=-1.0
                                   ).then_inc(hot_ready, 1)

                def exps(n):
                    act.wait_ge(sel_done, n + 1)
                    act.activation(scale[:, :], pE[0:NODES_T, 256:256 + H], ACT.Exp).then_inc(scale_ready, 1)
                    act.wait_ge(t_ready, n + 1)
                    act.activation(ex[:, :, :], under[:, :, :], ACT.Exp).then_inc(ex_ready, 1)

                start = Chain(act, own_act)
                act.wait_ge(parts_ready, 1)
                act.load(regs[0:2 * GROUP], m.node_tab[0:1, 0:2 * GROUP])
                one_hot_nodes(start, 0, 0, 0)
                take_er(0, regs[0:GROUP])
                one_hot_edges(start, 0, 0)
                act.wait_ge(er_done, 1)
                one_hot_nodes(start, 1, 1, 0)
                take_er(1, regs[GROUP:2 * GROUP])
                exps(0)

                def turn(b, u, i):
                    me = Chain(act, own_act, b, 1 if folded else 1 + GROUP, start.n)
                    if u == 0:
                        act.load(regs, m.node_tab[0:1, bass.ds(i * (UNROLL * GROUP) + 2 * GROUP, UNROLL * GROUP)])
                    take_er(u % 2, regs[u * GROUP:(u + 1) * GROUP])
                    act.wait_ge(er_done, b + 2)
                    one_hot_nodes(me, b + 2, *after(u, i, 2, 2))
                    act.wait_ge(add_done, b * GROUP + 4)
                    one_hot_edges(me, b + 1, (u + 1) % 2)
                    exps(b + 1)
                    me.close()
                turns(nc.scalar, turn)

            @block.vector
            def _(dve):
                regs = [dve.alloc_register(f"{name}_dve{k}") for k in range(UNROLL * GROUP)]

                def logit_sums(me, n, q, fill):
                    dve.wait_ge(er_done, n + 1)
                    dve.wait_ge(gathered[q], fill * (16 * GROUP) + 16 * GROUP)
                    me.done(dve.tensor_tensor(z[:, :, :], rows[:, q, :, H * C:ROW],
                                              pE[:, 0:GROUP * H].rearrange("p (k h) -> p k h", k=GROUP), ALU.add))

                def edge_logits(me, n):
                    me.wait()
                    me.done(dve.scalar_tensor_tensor(lz[:, :, :], z[:, :, :], 0.2, z[:, :, :], ALU.mult, ALU.max))
                    me.wait()
                    dve.tensor_tensor(lz[:, :, :], lz[:, :, :],
                                      m.in_all[:, bass.ds(n * GROUP, GROUP)].rearrange("p (k a) -> p k a", a=1)
                                      .to_broadcast([P, GROUP, H]), ALU.min).then_inc(lz_ready, 1)

                def forward_max(me, n, par):
                    dve.wait_ge(lzT_done, n + 1)
                    me.forward = me.done(dve.tensor_tensor_scan(fw[:, :], flags[:, par, 0, :], pT[0:H, :], carry[:, 0:1],
                                                                ALU.add, ALU.max))

                def backward_max(me, n, par):
                    me.wait(me.forward)
                    dve.tensor_tensor_scan(bw[:, ::-1], flags[:, par, 1, ::-1], fw[:, ::-1], -BIG, ALU.add, ALU.max
                                           ).then_inc(scans_done, 1)

                def carry_over(me, n):
                    dve.wait_ge(scans_done, n + 1)
                    me.fell = me.done(dve.tensor_tensor(fall[:, :], carry[:, :], bw[:, 0:1], ALU.subtract))

                def carry_scale(me, n):
                    me.wait(me.fell)
                    dve.tensor_scalar(ln_scale[:, :], m.iota[0:H, :], m.cont_dl[0:H, bass.ds(n, 1)], fall[:, 0:1],
                                      ALU.is_equal, ALU.mult).then_inc(sel_ready, 1)
                    me.done(dve.tensor_copy(carry[:, :], fw[:, GE - 1:GE]))

                def running_max(me, n, par):
                    forward_max(me, n, par)
                    backward_max(me, n, par)
                    carry_over(me, n)
                    carry_scale(me, n)

                def shifted(n):
                    dve.wait_ge(c_back, n + 1)
                    dve.tensor_tensor(under[:, :, :], lz[:, :, :],
                                      pB[:, 0:GROUP * H].rearrange("p (k h) -> p k h", k=GROUP), ALU.subtract
                                      ).then_inc(t_ready, 1)

                def weighted(b, u):
                    dve.wait_ge(ex_ready, b + 1)
                    if folded:
                        for k in range(GROUP):
                            ins = dve.tensor_scalar(hot[:, 0, k, :], m.iota[:, :], m.dl_all[:, bass.ds(b * GROUP + k, 1)],
                                                    ex[:, k, :], ALU.is_equal, ALU.mult)
                            ins.then_inc(wr_ready, 1)
                    else:
                        half = GROUP // 2
                        for k in (0, half):
                            dve.tensor_tensor(wr[:, k:k + half, 0:H * C].rearrange("p k (h c) -> p k h c", h=H),
                                              rows[:, u, k:k + half, 0:H * C].rearrange("p k (h c) -> p k h c", h=H),
                                              ex[:, k:k + half, :].rearrange("p k (h a) -> p k h a", a=1)
                                              .to_broadcast([P, half, H, C]), ALU.mult).then_inc(wr_ready, 1)

                start = Chain(dve, own)
                for given, n in ((rows_used, UNROLL), (add_done, 4)):
                    dve.sem_inc(given, n)
                start.done(dve.memset(acc[:, :, :], 0.0))
                start.done(dve.memset(carry[:, :], -BIG))
                if degree:
                    start.done(dve.memset(wr[:, :, W - 1:W], 1.0))
                left = er[:, :, :]
                for k in range(3):
                    start.done(dve.tensor_copy(parts[:, :, k, :], left))
                    start.wait()
                    if k < 2:
                        start.done(dve.tensor_tensor(rest[:, k], left, parts[:, :, k, :], ALU.subtract))
                        start.wait()
                        left = rest[:, k]
                dve.sem_inc(parts_ready, 1)
                logit_sums(start, 0, 0, 0)
                edge_logits(start, 0)
                running_max(start, 0, 0)
                shifted(0)
                logit_sums(start, 1, 1, 0)
                edge_logits(start, 1)
                start.wait()

                def turn(b, u, i):
                    me = Chain(dve, own, b, 6, start.n)
                    if u == 0:
                        dve.load(regs, m.node_tab[0:1, bass.ds(i * (UNROLL * GROUP), UNROLL * GROUP)])
                    nodes = [dve.snap(r, min_val=0, max_val=NT - 1) for r in regs[u * GROUP:(u + 1) * GROUP]]
                    par = (u + 1) % 2

                    def add(k):
                        part = acc[:, bass.ds(nodes[k], 1), 0:W]
                        if k == 0:
                            me.wait(scaled)
                        else:
                            dve.wait_ge(add_done, b * GROUP + (k + 4))
                        dve.wait_ge(agg_done, b * GROUP + (k + 1))
                        dve.tensor_tensor(part, part, pA[k % 4][0:NODES_T, 0:W].rearrange("p (a c) -> p a c", a=1),
                                          ALU.add).then_inc(add_done, 1)

                    part = acc[:, bass.ds(nodes[0], 1), 0:H * C].rearrange("p a (h c) -> p (a h) c", h=H)
                    dve.wait_ge(add_done, b * GROUP + 4)
                    dve.wait_ge(scale_ready, b + 1)
                    scaled = me.done(dve.tensor_tensor(part, part, scale[:, :].rearrange("p (h a) -> p h a", a=1)
                                                       .to_broadcast([NODES_T, H, C]), ALU.mult))
                    weighted(b, u)
                    add(0)
                    forward_max(me, b + 1, par)
                    if not folded:
                        dve.wait_ge(wr_ready, 2 * b + 2)
                        dve.sem_inc(rows_used, 1)
                    add(1)
                    backward_max(me, b + 1, par)
                    add(2)
                    carry_over(me, b + 1)
                    add(3)
                    carry_scale(me, b + 1)
                    add(4)
                    shifted(b + 1)
                    add(5)
                    add(6)
                    logit_sums(me, b + 2, *after(u, i, UNROLL, 2))
                    edge_logits(me, b + 2)
                    add(7)
                    if folded:
                        dve.sem_inc(rows_used, 1)
                    me.close()
                turns(nc.vector, turn)

            @block.tensor
            def _(pe):
                def spread_er(n, par):
                    pe.wait_ge(hotT_ready, n + 1)
                    pe.wait_ge(er_ready, n * GROUP + GROUP)
                    for k in range(GROUP):
                        for c in range(3):
                            ins = pe.matmul(pE[:, k * H:(k + 1) * H], hotT[:, k * P:(k + 1) * P], er_s[:, par, k, c, :],
                                            start=(c == 0), stop=(c == 2))
                    ins.then_inc(er_done, 1)

                def turn_logits(n):
                    pe.wait_ge(lz_ready, n + 1)
                    for k in range(GROUP):
                        ins = pe.transpose(pT[0:H, k * P:(k + 1) * P], lz[:, k, :], m.ident[:, :])
                    ins.then_inc(lzT_done, 1)

                def turn_max(n):
                    pe.wait_ge(scans_done, n + 1)
                    pe.sem_inc(m.hold, 1)
                    for k in range(GROUP):
                        ins = pe.transpose(pB[:, k * H:(k + 1) * H], bw[:, k * P:(k + 1) * P], m.ident[0:H, 0:H])
                    ins.then_inc(c_back, 1)

                def turn_scale(n):
                    pe.wait_ge(sel_ready, n + 1)
                    pe.matmul(pE[0:NODES_T, 256:256 + H], ln_scale[:, :], m.ident[0:H, 0:H], start=True, stop=True
                              ).then_inc(sel_done, 1)

                def sum_step(b, u, k):
                    if folded:
                        pe.wait_ge(wr_ready, b * GROUP + (k + 1))
                    elif k == 0:
                        pe.wait_ge(hot_ready, b + 1)
                        pe.wait_ge(wr_ready, 2 * b + 1)
                    elif k == GROUP // 2:
                        pe.wait_ge(wr_ready, 2 * b + 2)
                    pe.wait_ge(add_done, b * GROUP + (k + 1))
                    pe.matmul(pA[k % 4][0:NODES_T, 0:W], hot[:, 0 if folded else u % 2, k, :],
                              rows[:, u, k, 0:C] if folded else wr[:, k, :], start=True, stop=True).then_inc(agg_done, 1)

                spread_er(0, 0)
                turn_logits(0)
                turn_max(0)
                turn_scale(0)
                pe.wait_ge(scale_ready, 1)
                spread_er(1, 1)
                turn_logits(1)

                def turn(b, u, i):
                    for k in range(GROUP):
                        sum_step(b, u, k)
                        if k == 4:
                            turn_max(b + 1)
                        if k == 5:
                            turn_scale(b + 1)
                        if k == 6:
                            pe.wait_ge(scale_ready, b + 2)
                            spread_er(b + 2, u % 2)
                    turn_logits(b + 2)
                turns(nc.tensor, turn)


def finish_first(nc, m):
    W = 2 * NODES_T
    with ExitStack() as scope:
        z = sb(nc, scope, "z", [NODES_T, 4, 2, 2, D])
        inv = sb(nc, scope, "inv", [NODES_T, NT, H1])
        h = sb(nc, scope, "h", [NODES_T, 2, 2, D])
        hT = sb(nc, scope, "hT", [P, 2, 2, W])
        stage = sb(nc, scope, "stage2", [NODES_T, 2, 2, ROW2])
        z1n = sb(nc, scope, "z1n", [NODES_T, 2, 2, D])
        pT = [ps(nc, scope, f"qT{k}") for k in range(2)]
        pA = [[ps(nc, scope, f"qA{k}{j}") for j in range(2)] for k in range(2)]
        pZ = [ps(nc, scope, f"qZ{k}") for k in range(2)]
        inn = [m.sem(f"skip_in{u}") for u in range(4)]
        used, h_ready, hT_done, hT_ready = m.sem("skip_used"), m.sem("h1_ready"), m.sem("h1T_done"), m.sem("h1T_ready")
        proj_done, z1_ready, psum_used = m.sem("second_done"), m.sem("z1_ready"), m.sem("second_psum_used")
        sent = [m.sem(f"second_sent{u}") for u in range(2)]
        z1_sent = [m.sem(f"z1_sent{u}") for u in range(2)]
        own, own_act, ones_in = m.sem("finish_first_dve"), m.sem("finish_first_act"), m.sem("second_ones")
        flat = lambda a: a.rearrange("p k d -> p (k d)")

        with nc.Block() as block:
            @block.sync
            def _(sp):
                def load(p, u, i, more):
                    sp.wait_ge(used, p + 1)
                    sp.dma_start(z[:, u].rearrange("p k j d -> p k (j d)"), of_pair(m.z_d, p)).then_inc(inn[u], 16)
                over_pairs(nc.sync, load, 4)
                for u in range(2):
                    n = (NT // 2 + 1 - u) // 2
                    sp.wait_ge(sent[u], 16 * n + 16)
                    sp.wait_ge(z1_sent[u], 16 * n + 16)

            @block.gpsimd
            def _(pool):
                pool.memset(stage[:, :, :, :], 1.0).then_inc(ones_in, 1)

            @block.vector
            def _(dve):
                start = Chain(dve, own)
                dve.sem_inc(used, 4)
                dve.sem_inc(psum_used, 1)
                for u in range(2):
                    dve.sem_inc(sent[u], 16)
                    dve.sem_inc(z1_sent[u], 16)
                acc = m.acc[:, :, :]
                start.done(dve.tensor_scalar(inv[:, :, :], acc[:, :, 0:H1 * C1].rearrange("p t (h c) -> p t h c", h=H1)[:, :, :, D1],
                                             1e-30, None, ALU.max))
                start.done(dve.tensor_scalar(m.norm[:, :], acc[:, :, H1 * C1], 1.0, None, ALU.max))
                start.wait()
                start.done(dve.reciprocal(inv[:, :, :], inv[:, :, :]))
                start.done(dve.reciprocal(m.norm[:, :], m.norm[:, :]))
                start.wait()

                def finish(me, p, q, fill, v):
                    dve.wait_ge(inn[q], 16 * fill + 16)
                    for k in range(2):
                        me.done(dve.scalar_tensor_tensor(z[:, q, k, 0, :], z[:, q, k, 0, :], m.norm[:, bass.ds(p * 2 + k, 1)],
                                                         m.bias_b[0:NODES_T, 0, :], ALU.mult, ALU.add))
                    for k in range(2):
                        me.done(dve.tensor_tensor(
                            h[:, v, k, :].rearrange("p (h c) -> p h c", h=H1),
                            m.acc[:, bass.ds(p * 2 + k, 1), 0:H1 * C1].rearrange("p a (h c) -> p (a h) c", h=H1)[:, :, 0:D1],
                            inv[:, bass.ds(p * 2 + k, 1), :].rearrange("p a h -> p h a").to_broadcast([NODES_T, H1, D1]),
                            ALU.mult))
                    me.wait()
                    dve.tensor_tensor(h[:, v], h[:, v], z[:, q, :, 0, :], ALU.add).then_inc(h_ready, 1)

                def turn(p, u, i, more):
                    me = Chain(dve, own, p, 5 if more else 1, start.n if more else start.n + 4 * (NT // 2 - 1))
                    if more:
                        finish(me, p + 1, *place(u, i, 4, 4, 1), (u + 1) % 2)
                    v, fill = place(u, i, 4, 2)
                    dve.wait_ge(proj_done, p + 1)
                    dve.wait_ge(z1_sent[v], fill * 16 + 16)
                    me.done(dve.tensor_tensor(z1n[:, v], z[:, u, :, 1, :],
                                              pZ[v][0:NODES_T, :].rearrange("p (k d) -> p k d", k=2), ALU.add))
                    me.wait()
                    dve.sem_inc(used, 1)
                    dve.sem_inc(z1_ready, 1)
                    me.close()
                finish(start, 0, 0, 0, 0)
                over_pairs(nc.vector, turn, 4)

            @block.tensor
            def _(pe):
                def turn_h(p, u):
                    pe.wait_ge(h_ready, p + 1)
                    for c in range(2):
                        for k in range(2):
                            ins = pe.transpose(pT[u][:, c * W + k * NODES_T:c * W + (k + 1) * NODES_T],
                                               h[:, u, k, c * P:c * P + P], m.ident[0:NODES_T, 0:NODES_T])
                    ins.then_inc(hT_done, 1)

                def turn(p, u, i, more):
                    v = u % 2
                    if more:
                        turn_h(p + 1, 1 - v)
                    pe.wait_ge(hT_ready, p + 1)
                    pe.wait_ge(psum_used, p + 1)
                    for k in range(2):
                        lhs = lambda c: hT[:, v, c, k * NODES_T:(k + 1) * NODES_T]
                        for c in range(2):
                            pe.matmul(pA[v][k][0:NODES_T, 0:D + 2], lhs(c), m.w2e[:, c, :], start=(c == 0), stop=(c == 1))
                        for c in range(2):
                            ins = pe.matmul(pZ[v][0:NODES_T, k * D:k * D + D], lhs(c), m.wb1T[:, 2 + c, :],
                                            start=(c == 0), stop=(c == 1))
                    ins.then_inc(proj_done, 1)
                turn_h(0, 0)
                over_pairs(nc.tensor, turn, 4)

            @block.scalar
            def _(act):
                act.wait_ge(ones_in, 1)

                def take_turned(p, u):
                    act.wait_ge(hT_done, p + 1)
                    act.activation(hT[:, u].rearrange("p c n -> p (c n)"), pT[u][:, 0:2 * W], ACT.Relu).then_inc(hT_ready, 1)

                def turn(p, u, i, more):
                    me = Chain(act, own_act, p, 6)
                    v, fill = place(u, i, 4, 2)
                    if more:
                        take_turned(p + 1, 1 - v)
                    act.wait_ge(proj_done, p + 1)
                    act.wait_ge(sent[v], fill * 16 + 16)
                    for k in range(2):
                        me.done(act.copy(stage[:, v, k, 0:D], pA[v][k][0:NODES_T, 0:D]))
                        me.done(act.copy(stage[:, v, k, C2:C2 + 1], pA[v][k][0:NODES_T, D:D + 1]))
                        me.done(act.copy(m.er2[:, bass.ds(p * 2 + k, 1), :],
                                         pA[v][k][0:NODES_T, D + 1:D + 2].rearrange("p (a h) -> p a h", a=1)))
                    me.wait()
                    act.dma_start(of_pair(m.tab2, p), stage[:, v]).then_inc(sent[v], 16)
                    act.wait_ge(z1_ready, p + 1)
                    act.sem_inc(psum_used, 1)
                    act.dma_start(of_pair(m.z1_d2, p), z1n[:, v]).then_inc(z1_sent[v], 16)
                    me.close()
                act.sem_inc(psum_used, 1)
                take_turned(0, 0)
                over_pairs(nc.scalar, turn, 4)


def route(nc, m):
    W = 2 * NODES_T
    with ExitStack() as scope:
        tin = sb(nc, scope, "tin", [NODES_T, 4, 3, 2, D])
        inv = sb(nc, scope, "inv2", [NODES_T, NT])
        xn = sb(nc, scope, "xn2", [NODES_T, 2, 2, D])
        ring = sb(nc, scope, "scatter_ring", [NODES_T, 2, 5, D])
        xn_all = sb(nc, scope, "xn_all", [NODES_T, NT, D])
        xT = sb(nc, scope, "xT2", [P, 2, 2, W])
        stats = sb(nc, scope, "stats2", [NODES_T, 2, 6])
        mv = sb(nc, scope, "mv2", [NODES_T, 2, 2, 2])
        var = sb(nc, scope, "var2", [NODES_T, 2, 2])
        rstd = sb(nc, scope, "rstd2", [NODES_T, 2, 2])
        logit = sb(nc, scope, "logit", [NODES_T, NT, EXPERTS])
        top = sb(nc, scope, "top", [NODES_T, NT])
        pick = sb(nc, scope, "pick", [NODES_T, NT, EXPERTS])
        hot = sb(nc, scope, "hot2", [NODES_T, NT, EXPERTS])
        first = sb(nc, scope, "first", [NODES_T, NT])
        eid = sb(nc, scope, "eid", [NODES_T, EXPERTS])
        before = sb(nc, scope, "before", [NODES_T, NT, EXPERTS])
        spare = sb(nc, scope, "spare", [NODES_T, NT])
        zero = sb(nc, scope, "zero", [NODES_T, NT])
        pos = sb(nc, scope, "pos", [NODES_T, NT])
        kept = sb(nc, scope, "kept", [NODES_T, NT])
        slot = sb(nc, scope, "slot", [NODES_T, NT])
        slot_i = sb(nc, scope, "slot_i", [NODES_T, NT], I32)
        tri = sb(nc, scope, "tri", [NODES_T, NODES_T])
        pT = [ps(nc, scope, f"rT{k}") for k in range(2)]
        pL = [ps(nc, scope, f"rL{k}") for k in range(2)]
        pC = [ps(nc, scope, f"rC{k}") for k in range(2)]
        s = m.sem
        inn = [s(f"route_in{u}") for u in range(4)]
        used, var_ready, rstd_ready, xn_ready = s("route_used"), s("route_var"), s("route_rstd"), s("route_xn")
        xT_done, xT_ready, gate_done, own = s("route_xT_done"), s("route_xT_ready"), s("gate_done"), s("route_dve")
        own_act, xn_used = s("route_act"), s("route_xn_used")
        made = s("route_consts")
        hot_ready, counted, exp_done = s("hot2_ready"), s("counted"), s("gate_exp")
        slots_ready, slot_moved, scattered = s("slots_ready"), s("slot_moved"), s("rows_scattered")
        ring_used, ring_ready = s("scatter_ring_used"), s("scatter_ring_ready")

        with nc.Block() as block:
            @block.sync
            def _(sp):
                def load(p, u, i, more):
                    sp.wait_ge(used, p + 1)
                    for k, frm in enumerate((m.x, m.mix_d, m.z1_d2)):
                        sp.dma_start(tin[:, u, k], of_pair(frm, p)).then_inc(inn[u], 16)
                over_pairs(nc.sync, load, 4)

            @block.gpsimd
            def _(pool):
                def turn(p, u, i, more):
                    pool.wait_ge(var_ready, p + 1)
                    pool.tensor_tensor(rstd[:, u, :], var[:, u, :], m.half[0:NODES_T, :].to_broadcast([NODES_T, 2]), ALU.pow
                                       ).then_inc(rstd_ready, 1)
                over_pairs(nc.gpsimd, turn)
                pool.iota(eid[:, :], pattern=[[1, EXPERTS]], base=0, channel_multiplier=0,
                          allow_small_or_imprecise_dtypes=True).then_inc(made, 1)
                pool.memset(tri[:, :], 1.0).then_inc(made, 1)
                pool.memset(zero[:, :], 0.0).then_inc(made, 1)
                pool.iota(spare[:, :], pattern=[[NODES_T, NT]], base=EXPERTS * SLOTS, channel_multiplier=1,
                          allow_small_or_imprecise_dtypes=True).then_inc(made, 1)
                pool.wait_ge(made, 4)
                pool.affine_select(out=tri[:, :], in_=tri[:, :], compare_op=ALU.is_ge, fill=0.0, base=0,
                                   pattern=[[1, NODES_T]], channel_multiplier=-1).then_inc(made, 1)

            @block.vector
            def _(dve):
                start = Chain(dve, own)
                dve.sem_inc(used, 4)
                dve.sem_inc(xn_used, 2)
                start.done(dve.tensor_scalar(inv[:, :], m.acc[:, :, D], 1e-30, None, ALU.max))
                start.wait()
                start.done(dve.reciprocal(inv[:, :], inv[:, :]))
                start.wait()

                def add_up(me, p, q, fill, v):
                    dve.wait_ge(inn[q], 48 * fill + 48)
                    for k in range(2):
                        me.done(dve.scalar_tensor_tensor(tin[:, q, 2, k, :], tin[:, q, 2, k, :], m.norm[:, bass.ds(p * 2 + k, 1)],
                                                         m.bias_b[0:NODES_T, 1, :], ALU.mult, ALU.add))
                    me.done(dve.tensor_tensor(tin[:, q, 0], tin[:, q, 0], tin[:, q, 1], ALU.add))
                    me.wait()
                    for k in range(2):
                        me.done(dve.scalar_tensor_tensor(tin[:, q, 2, k, :],
                                                         m.acc[:, bass.ds(p * 2 + k, 1), 0:D].rearrange("p a d -> p (a d)"),
                                                         inv[:, bass.ds(p * 2 + k, 1)], tin[:, q, 2, k, :], ALU.mult, ALU.add))
                    me.wait()
                    me.done(dve.tensor_tensor(m.acc[:, bass.ds(p * 2, 2), 0:D], tin[:, q, 0], tin[:, q, 2], ALU.add))
                    me.wait()
                    dve.sem_inc(used, 1)
                    for k in range(2):
                        me.done(dve.bn_stats(stats[:, k, :], m.acc[:, bass.ds(p * 2 + k, 1), 0:D].rearrange("p a d -> p (a d)")))
                    me.wait_apart(m.hold)
                    for k in range(2):
                        me.done(dve.bn_aggr(mv[:, v, k, :], stats[:, k, :]))
                    me.wait()
                    dve.tensor_scalar(var[:, v, :], mv[:, v, :, 1], EPS, None, ALU.add).then_inc(var_ready, 1)

                def normalise(me, p, v):
                    dve.wait_ge(rstd_ready, p + 1)
                    dve.wait_ge(xn_used, p + 1)
                    for k in range(2):
                        me.done(dve.tensor_scalar(xn[:, v, k, :], m.acc[:, bass.ds(p * 2 + k, 1), 0:D].rearrange("p a d -> p (a d)"),
                                                  mv[:, v, k, 0:1], rstd[:, v, k:k + 1], ALU.subtract, ALU.mult))
                    me.wait()
                    dve.sem_inc(xn_ready, 1)

                def turn(p, u, i, more):
                    me = Chain(dve, own, p, 12 if more else 2, start.n if more else start.n + 10 * (NT // 2 - 1))
                    if more:
                        add_up(me, p + 1, *place(u, i, 4, 4, 1), (u + 1) % 2)
                    normalise(me, p, u % 2)
                    me.close()
                add_up(start, 0, 0, 0, 0)
                over_pairs(nc.vector, turn, 4)

            @block.tensor
            def _(pe):
                def turn(p, u, i, more):
                    pe.wait_ge(xn_ready, p + 1)
                    for c in range(2):
                        for k in range(2):
                            ins = pe.transpose(pT[u][:, c * W + k * NODES_T:c * W + (k + 1) * NODES_T],
                                               xn[:, u, k, c * P:c * P + P], m.ident[0:NODES_T, 0:NODES_T])
                    ins.then_inc(xT_done, 1)
                    pe.wait_ge(xT_ready, p + 1)
                    for k in range(2):
                        for c in range(2):
                            ins = pe.matmul(pL[u][0:NODES_T, k * EXPERTS:(k + 1) * EXPERTS],
                                            xT[:, u, c, k * NODES_T:(k + 1) * NODES_T], m.gate_w[:, c, :],
                                            start=(c == 0), stop=(c == 1))
                    ins.then_inc(gate_done, 1)
                over_pairs(nc.tensor, turn)

            @block.scalar
            def _(act):
                def turn(p, u, i, more):
                    me = Chain(act, own_act, p, 2)
                    act.wait_ge(xT_done, p + 1)
                    act.copy(xT[:, u].rearrange("p c n -> p (c n)"), pT[u][:, 0:2 * W]).then_inc(xT_ready, 1)
                    me.done(act.copy(xn_all[:, bass.ds(p * 2, 2), :], xn[:, u]))
                    act.wait_ge(gate_done, p + 1)
                    me.done(act.copy(logit[:, bass.ds(p * 2, 2), :],
                                     pL[u][0:NODES_T, 0:2 * EXPERTS].rearrange("p (k e) -> p k e", k=2)))
                    me.wait()
                    act.sem_inc(xn_used, 1)
                    me.close()
                over_pairs(nc.scalar, turn)

        wide = [NODES_T, NT, EXPERTS]
        rep = lambda a: a.rearrange("p (t a) -> p t a", a=1).to_broadcast(wide)
        with nc.Block() as block:
            @block.vector
            def _(dve):
                me = Chain(dve, m.sem("places_dve"))
                lab = eid[:, :].rearrange("p (a e) -> p a e", a=1).to_broadcast(wide)
                me.done(dve.tensor_tensor(logit[:, :, :], logit[:, :, :],
                                          m.gate_bb[0:NODES_T, :].rearrange("p (a e) -> p a e", a=1).to_broadcast(wide), ALU.add))
                me.wait()
                me.done(dve.tensor_reduce(top[:, :], logit[:, :, :], AX, ALU.max))
                me.wait()
                me.done(dve.tensor_tensor(logit[:, :, :], logit[:, :, :], rep(top[:, :]), ALU.subtract))
                me.wait()
                me.done(dve.tensor_scalar(pick[:, :, :], logit[:, :, :], 0.0, -float(EXPERTS), ALU.is_ge, ALU.mult))
                me.wait()
                me.done(dve.tensor_tensor(pick[:, :, :], pick[:, :, :], lab, ALU.add))
                me.wait()
                me.done(dve.tensor_reduce(first[:, :], pick[:, :, :], AX, ALU.min))
                me.wait()
                me.done(dve.tensor_scalar(first[:, :], first[:, :], float(EXPERTS), None, ALU.add))
                me.wait()
                me.done(dve.tensor_tensor(hot[:, :, :], lab, rep(first[:, :]), ALU.is_equal))
                me.wait()
                dve.sem_inc(hot_ready, 1)
                dve.wait_ge(exp_done, 1)
                me.done(dve.tensor_reduce(m.prob[:, :], logit[:, :, :], AX, ALU.add))
                me.wait()
                me.done(dve.reciprocal(m.prob[:, :], m.prob[:, :]))
                dve.wait_ge(counted, 1)
                me.done(dve.memset(before[:, 0, :], 0.0))
                me.wait()
                for e in range(EXPERTS):
                    me.done(dve.tensor_tensor_scan(before[:, 1:NT, e], pC[1][0:NODES_T, 0:(NT - 1) * EXPERTS]
                                                   .rearrange("p (t e) -> p t e", e=EXPERTS)[:, :, e],
                                                   zero[:, 0:NT - 1], 0.0, ALU.add, ALU.add))
                me.wait()
                me.done(dve.tensor_tensor(before[:, :, :], before[:, :, :], pC[0][0:NODES_T, 0:NT * EXPERTS]
                                          .rearrange("p (t e) -> p t e", e=EXPERTS), ALU.add))
                me.wait()
                me.done(dve.tensor_tensor(before[:, :, :], before[:, :, :], hot[:, :, :], ALU.mult))
                me.wait()
                me.done(dve.tensor_reduce(pos[:, :], before[:, :, :], AX, ALU.add))
                me.wait()
                me.done(dve.tensor_scalar(pos[:, :], pos[:, :], -1.0, None, ALU.add))
                me.wait()
                me.done(dve.tensor_scalar(kept[:, :], pos[:, :], float(CAP), None, ALU.is_lt))
                me.done(dve.tensor_scalar(pos[:, :], pos[:, :], float(CAP - 1), None, ALU.min))
                me.wait()
                me.done(dve.tensor_tensor(m.prob[:, :], m.prob[:, :], kept[:, :], ALU.mult))
                me.done(dve.scalar_tensor_tensor(slot[:, :], first[:, :], float(SLOTS), pos[:, :], ALU.mult, ALU.add))
                me.wait()
                me.done(dve.tensor_copy(m.read_at[:, :], slot[:, :]))
                me.done(dve.tensor_tensor(slot[:, :], slot[:, :], spare[:, :], ALU.subtract))
                me.wait()
                me.done(dve.tensor_tensor(slot[:, :], slot[:, :], kept[:, :], ALU.mult))
                me.wait()
                me.done(dve.tensor_tensor(slot[:, :], slot[:, :], spare[:, :], ALU.add))
                me.wait()
                dve.tensor_copy(slot_i[:, :], slot[:, :]).then_inc(slots_ready, 1)

            @block.tensor
            def _(pe):
                pe.wait_ge(hot_ready, 1)
                flat = hot[:, :, :].rearrange("p t e -> p (t e)")
                pe.matmul(pC[0][0:NODES_T, 0:NT * EXPERTS], tri[:, :], flat, start=True, stop=True)
                pe.matmul(pC[1][0:NODES_T, 0:NT * EXPERTS], m.ones[0:NODES_T, 0:NODES_T], flat, start=True, stop=True
                          ).then_inc(counted, 1)

            @block.scalar
            def _(act):
                act.wait_ge(hot_ready, 1)
                act.activation(logit[:, :, :], logit[:, :, :], ACT.Exp).then_inc(exp_done, 1)
                with nc.scalar.Fori(0, NT // 10) as i:
                    act.wait_ge(ring_used, i + 1)
                    for u in range(2):
                        act.copy(ring[:, u], xn_all[:, bass.ds(i * 10 + u * 5, 5), :]).then_inc(ring_ready, 1)

            @block.gpsimd
            def _(pool):
                pool.sem_inc(ring_used, 1)
                pool.wait_ge(slots_ready, 1)
                with nc.gpsimd.Fori(0, NT // 10) as i:
                    pool.tensor_copy(m.slot10[:, :], slot_i[:, bass.ds(i * 10, 10)]).then_inc(slot_moved, 1)
                    pool.wait_ge(slot_moved, i + 1)
                    for k in range(10):
                        if k % 5 == 0:
                            pool.wait_ge(ring_ready, i * 2 + (k // 5 + 1))
                            pool.sem_inc(m.hold, 1)
                        pool.indirect_dma_start(
                            out=m.xbuf[:, :], out_offset=bass.IndirectOffsetOnAxis(ap=m.slot10[:, k:k + 1].bitcast(U32), axis=0),
                            in_=ring[:, k // 5, k % 5, :], in_offset=None).then_inc(scattered, 16)
                    pool.wait_ge(scattered, 160 * i + 160)
                    pool.sem_inc(ring_used, 1)


def experts(nc, m):
    HT = 4
    W = HT * NODES_T
    FQ = FF // P
    with ExitStack() as scope:
        xr = sb(nc, scope, "xr", [NODES_T, 2, HT, D])
        xT = sb(nc, scope, "xTe", [P, 2, 2, W])
        hT = sb(nc, scope, "hTe", [P, FQ, W])
        y = sb(nc, scope, "ye", [NODES_T, 2, HT, D])
        w1 = sb(nc, scope, "w1", [P, 2, 2, FF])
        w2 = sb(nc, scope, "w2", [P, 2, FQ, D])
        b1 = sb(nc, scope, "b1", [P, 2, FQ])
        b2 = sb(nc, scope, "b2", [NODES_T, 2, D])
        pT = [ps(nc, scope, f"eT{k}") for k in range(2)]
        pF = [ps(nc, scope, f"eF{k}") for k in range(4)]
        pY = [ps(nc, scope, f"eY{k}") for k in range(2)]
        s = m.sem
        w_in = [s(f"expert_w{u}") for u in range(2)]
        x_in = [s(f"expert_x{u}") for u in range(2)]
        w_used, x_used = s("expert_w_used"), s("expert_x_used")
        xT_done, xT_ready, fc1_done, h_ready = s("expert_xT_done"), s("expert_xT_ready"), s("expert_fc1"), s("expert_h")
        h_act = s("expert_h_act")
        fc2_done, y_ready = s("expert_fc2"), s("expert_y")
        sent = [s(f"expert_sent{u}") for u in range(2)]

        def turns(eng, body):
            with eng.Fori(0, EXPERTS // 2) as i:
                for v in range(2):
                    for u in range(2):
                        body(i * 4 + (v * 2 + u), v, u, i, i * 2 + v)

        with nc.Block() as block:
            @block.sync
            def _(sp):
                def turn(n, v, u, i, e):
                    if u == 0:
                        sp.wait_ge(w_used, e + 1)
                        sp.dma_start(w1[:, v], m.w1_flat[bass.ds(e * D, D), :].rearrange("(r p) f -> p r f", p=P)).then_inc(w_in[v], 16)
                        sp.dma_start(w2[:, v], m.w2_flat[bass.ds(e * FF, FF), :].rearrange("(q p) d -> p q d", p=P)).then_inc(w_in[v], 16)
                        sp.dma_start(b1[:, v], m.io["L0_ffn_b1"][bass.ds(e, 1), :].rearrange("a (q p) -> p (a q)", p=P)).then_inc(w_in[v], 16)
                        sp.dma_start(b2[:, v, :], m.io["L0_ffn_b2"][bass.ds(e, 1), :].to_broadcast([NODES_T, D])).then_inc(w_in[v], 16)
                    sp.wait_ge(x_used, n + 1)
                    sp.dma_start(xr[:, u], m.xbuf[bass.ds(n * W, W), :].rearrange("(k p) d -> p k d", p=NODES_T)).then_inc(x_in[u], 16)
                turns(nc.sync, turn)
                sp.wait_ge(x_used, EXPERTS * 2 + 1)
                sp.dma_start(xr[:, 0], m.xbuf[0:W, :].rearrange("(k p) d -> p k d", p=NODES_T)).then_inc(x_in[0], 16)

            @block.tensor
            def _(pe):
                def turn_rows(u, arrived):
                    pe.wait_ge(x_in[u], arrived)
                    for c in range(2):
                        for k in range(HT):
                            ins = pe.transpose(pT[c][:, k * NODES_T:(k + 1) * NODES_T], xr[:, u, k, c * P:c * P + P],
                                               m.ident[0:NODES_T, 0:NODES_T])
                    ins.then_inc(xT_done, 1)

                def turn(n, v, u, i, e):
                    pe.wait_ge(w_in[v], 64 * i + 64)
                    pe.wait_ge(xT_ready, n * 2 + 2)
                    for q in range(FQ):
                        if q >= 4:
                            pe.wait_ge(h_ready if q % 2 == 0 else h_act, n * (FQ // 2) + (q - 4) // 2 + 1)
                        for c in range(2):
                            ins = pe.matmul(pF[q % 4][:, 0:W], w1[:, v, c, q * P:q * P + P], xT[:, u, c, :],
                                            start=(c == 0), stop=(c == 1))
                        ins.then_inc(fc1_done, 1)
                    turn_rows(1 - u, 32 * i + (16 * (v + u) + 16))
                    pe.wait_ge(h_ready, n * (FQ // 2) + FQ // 2)
                    pe.wait_ge(h_act, n * (FQ // 2) + FQ // 2)
                    for k in range(HT):
                        pe.wait_ge(y_ready, n * HT + (k + 1))
                        at = pY[k % 2][0:NODES_T, 0:D]
                        for q in range(FQ):
                            ins = pe.matmul(at, hT[:, q, k * NODES_T:(k + 1) * NODES_T], w2[:, v, q, :],
                                            start=(q == 0), stop=(q == FQ - 1))
                        ins.then_inc(fc2_done, 1)
                turn_rows(0, 16)
                turns(nc.tensor, turn)

            @block.scalar
            def _(act):
                def take_turned(n, u):
                    act.wait_ge(xT_done, n + 1)
                    for c in range(2):
                        act.copy(xT[:, u, c, :], pT[c][:, 0:W]).then_inc(xT_ready, 1)

                def turn(n, v, u, i, e):
                    for q in range(1, FQ, 2):
                        act.wait_ge(fc1_done, n * FQ + (q + 1))
                        act.activation(hT[:, q, :], pF[q % 4][:, 0:W], ACT.Relu, bias=b1[:, v, q:q + 1]).then_inc(h_act, 1)
                    take_turned(n + 1, 1 - u)
                    act.wait_ge(y_ready, n * HT + (HT + 2))
                    act.dma_start(m.ybuf[bass.ds(n * W, W), :].rearrange("(k p) d -> p k d", p=NODES_T), y[:, u]).then_inc(sent[u], 16)
                take_turned(0, 0)
                turns(nc.scalar, turn)
                for u in range(2):
                    act.wait_ge(sent[u], 16 * EXPERTS + 16)

            @block.vector
            def _(dve):
                for given, k in ((w_used, 2), (x_used, 2), (y_ready, 2), (sent[0], 16), (sent[1], 16)):
                    dve.sem_inc(given, k)

                def turn(n, v, u, i, e):
                    for q in range(0, FQ, 2):
                        dve.wait_ge(fc1_done, n * FQ + (q + 1))
                        dve.tensor_scalar(hT[:, q, :], pF[q % 4][:, 0:W], b1[:, v, q:q + 1], 0.0, ALU.add, ALU.max).then_inc(h_ready, 1)
                    dve.wait_ge(xT_ready, n * 2 + 2)
                    dve.sem_inc(x_used, 1)
                    dve.wait_ge(sent[u], 32 * i + (16 * v + 16))
                    for k in range(HT):
                        dve.wait_ge(fc2_done, n * HT + (k + 1))
                        dve.tensor_tensor(y[:, u, k, :], pY[k % 2][0:NODES_T, 0:D], b2[:, v, :], ALU.add).then_inc(y_ready, 1)
                    if u == 1:
                        dve.wait_ge(y_ready, n * HT + (HT + 2))
                        dve.sem_inc(w_used, 1)
                turns(nc.vector, turn)


def combine(nc, m, out):
    K = 5
    with ExitStack() as scope:
        at = sb(nc, scope, "read_now", [NODES_T, 2, K], I32)
        yr = sb(nc, scope, "yr", [NODES_T, 2, K, D])
        mask = sb(nc, scope, "maskc", [NODES_T, K, D], U32)
        clipped = sb(nc, scope, "clipped", [NODES_T, K, D])
        zero = sb(nc, scope, "zeroc", [NODES_T, K, D])
        s = m.sem
        moved, scaled, done, own, zero_made = s("read_moved"), s("y_scaled"), s("combined"), s("combine_dve"), s("zero_made")
        y_in = [s(f"y_in{u}") for u in range(2)]
        sent = [s(f"out_sent{u}") for u in range(2)]

        def turns(eng, body):
            with eng.Fori(0, NT // K // 2) as i:
                for u in range(2):
                    body(i * 2 + u, u, i)

        with nc.Block() as block:
            @block.gpsimd
            def _(pool):
                pool.memset(zero[:, :, :], 0.0).then_inc(zero_made, 1)

                def turn(n, u, i):
                    pool.wait_ge(sent[u], 16 * i + 16)
                    pool.sem_inc(m.hold, 1)
                    pool.tensor_copy(at[:, u, :], m.read_at[:, bass.ds(n * K, K)]).then_inc(moved, 1)
                    pool.wait_ge(moved, n + 1)
                    pool.sem_inc(m.hold, 1)
                    for k in range(K):
                        pool.indirect_dma_start(out=yr[:, u, k, :], out_offset=None, in_=m.ybuf[:, :],
                                                in_offset=bass.IndirectOffsetOnAxis(ap=at[:, u, k:k + 1].bitcast(U32), axis=0)
                                                ).then_inc(y_in[u], 16)
                turns(nc.gpsimd, turn)

            @block.scalar
            def _(act):
                def turn(n, u, i):
                    act.wait_ge(y_in[u], 16 * K * i + 16 * K)
                    for k in range(K):
                        act.activation(yr[:, u, k, :], yr[:, u, k, :], ACT.Copy, scale=m.prob[:, bass.ds(n * K + k, 1)]
                                       ).then_inc(scaled, 1)
                turns(nc.scalar, turn)

            @block.sync
            def _(sp):
                def turn(n, u, i):
                    sp.wait_ge(done, n + 1)
                    sp.dma_start(out[bass.ds(n * K * NODES_T, K * NODES_T), :].rearrange("(k p) d -> p k d", p=NODES_T), yr[:, u]
                                 ).then_inc(sent[u], 16)
                turns(nc.sync, turn)
                for u in range(2):
                    sp.wait_ge(sent[u], 16 * (NT // K // 2) + 16)

            @block.vector
            def _(dve):
                for u in range(2):
                    dve.sem_inc(sent[u], 16)
                dve.wait_ge(zero_made, 1)

                def turn(n, u, i):
                    me = Chain(dve, own, n, 5)
                    y = yr[:, u]
                    dve.wait_ge(scaled, n * K + K)
                    me.done(dve.tensor_tensor(mask[:, :, :], y, y, ALU.not_equal))
                    me.wait_apart(m.hold)
                    me.done(dve.copy_predicated(y, mask[:, :, :], zero[:, :, :]))
                    me.wait()
                    me.done(dve.tensor_scalar(mask[:, :, :], y, 0.0, 0.0, ALU.mult, ALU.not_equal))
                    me.done(dve.tensor_scalar(clipped[:, :, :], y, 1e4, -1e4, ALU.min, ALU.max))
                    me.wait_apart(m.hold)
                    me.done(dve.copy_predicated(y, mask[:, :, :], clipped[:, :, :]))
                    me.wait()
                    dve.tensor_tensor(y, y, m.acc[:, bass.ds(n * K, K), 0:D], ALU.add).then_inc(done, 1)
                    me.close()
                turns(nc.vector, turn)


C1, C2 = D1 + 1, D + 1
ROW1, ROW2 = H1 * C1 + H1, C2 + 1


def gps_layer(nc, io, out):
    with ExitStack() as ctx:
        def dram(name, shape, dt=F32):
            return nc.dram_tensor(name, shape, dt, kind="Internal").ap()

        m = Memory()
        in_phase = []

        def new_sem(name):
            in_phase.append(nc.alloc_semaphore(name))
            return in_phase[-1]

        def phase(work, *args):
            work(nc, m, *args)
            nc.clear_and_free_semaphores(in_phase)
            nc.all_engine_barrier()
            in_phase.clear()

        m.sem = new_sem
        m.io = io
        m.x, m.src, m.dst = io["x"], io["src"], io["dst"]
        m.w1_flat = io["L0_ffn_w1"].rearrange("e d f -> (e d) f")
        m.w2_flat = io["L0_ffn_w2"].rearrange("e f d -> (e f) d")
        m.edge_tab = dram("edge_tab", [ET_PAD, ROW_E])
        m.last_step = dram("last_step", [ET_PAD])
        m.step_dl = dram("step_dl", [STEPS, P])
        m.step_flags = dram("step_flags", [2, STEPS, P])
        m.step_node = dram("step_node", [RT * P], I32)
        m.step_cont = dram("step_cont", [RT * P])
        m.tab1 = dram("tab1", [N, ROW1])
        m.tab2 = dram("tab2", [N, ROW2])
        m.z1_d2, m.mix_d, m.xn_d = [dram(n, [N, D]) for n in ("z1_d2", "mix_d", "xn_d")]
        m.z_d = dram("z_d", [N, 2 * D])
        m.xT_d = dram("xT_d", [NT * P, 2 * NODES_T])
        m.xbuf = dram("xbuf", [XROWS, D])
        m.ybuf = dram("ybuf", [EXPERTS * SLOTS, D])

        t = lambda name, shape, dt=F32: sb(nc, ctx, name, shape, dt)
        m.ident, m.ones, m.lane, m.iota = t("ident", [P, P]), t("ones", [P, P]), t("lane", [P, 1]), t("iota", [P, NODES_T])
        m.zeros, m.half = t("zeros", [P, D + 1]), t("half", [P, 1])
        m.idx_all, m.dl_all = t("idx_all", [P, STEPS], I32), t("dl_all", [P, STEPS])
        m.in_all = t("in_all", [P, STEPS])
        m.node_tab, m.cont_dl = t("node_tab", [1, STEPS], I32), t("cont_dl", [H1, BATCHES + 2])
        m.norm = t("norm", [NODES_T, NT])
        m.w1e, m.wb0T, m.wb1T = t("w1e", [P, 2, D + 16]), t("wb0T", [P, 2, D]), t("wb1T", [P, 4, D])
        m.w2e, m.wqT, m.wkv = t("w2e", [P, 2, D + 2]), t("wqT", [P, 2, D]), t("wkv", [P, 2, 2 * D])
        m.er1, m.er2 = t("er1", [NODES_T, NT, H1]), t("er2", [NODES_T, NT, 1])
        m.brow, m.bias_b = t("brow", [1, 6, D]), t("bias_b", [P, 2, D])
        m.gate_w, m.gate_bb = t("gate_w", [P, 2, EXPERTS]), t("gate_bb", [P, EXPERTS])
        m.prob, m.read_at, m.slot10 = t("prob", [NODES_T, NT]), t("read_at", [NODES_T, NT], I32), t("slot10", [NODES_T, 10], I32)
        once = lambda name: ctx.enter_context(nc.semaphore(name))
        m.hold = once("hold")
        m.act_own = once("act_own")
        m.gram_ready = once("gram_ready")
        m.mix_bd = once("mix_bd")
        m.mix_max = once("mix_max")

        ctx.enter_context(nc.allow_non_contiguous_dma(reason="small vectors, laid out by partition once"))
        phase(build_steps)
        phase(fold_weights)
        with ExitStack() as mix:
            tm = lambda name, shape: sb(nc, mix, name, shape)
            m.gram, m.wx = tm("gram", [P, 2, D + 1]), tm("wx", [P, 2, D])
            m.wf1, m.wf2 = tm("wf1", [P, 2, HIDDEN]), tm("wf2", [P, 6, D])
            m.gain, m.shift, m.b1col = tm("gain", [P, 2]), tm("shift", [P, 2]), tm("b1col", [P, 6])
            phase(project_nodes)
            phase(mixer_attention)
            phase(mixer)
        m.acc = sb(nc, ctx, "acc", [NODES_T, NT, H1 * C1 + 1])
        phase(convolve, "conv1", H1, D1, m.tab1, m.er1, m.acc, True)
        phase(finish_first)
        phase(convolve, "conv2", 1, D, m.tab2, m.er2, m.acc, False)
        phase(route)
        phase(experts)
        phase(combine, out)


_INS = ['x', 'src', 'dst', 'L0_gnn_fc1_w', 'L0_gnn_attn_l1', 'L0_gnn_attn_r1', 'L0_gnn_bias1', 'L0_gnn_fc2_w',
        'L0_gnn_attn_l2', 'L0_gnn_attn_r2', 'L0_gnn_bias2', 'L0_gnn_wb0', 'L0_gnn_bb0', 'L0_gnn_wb1', 'L0_gnn_bb1',
        'L0_mix_w_qkv', 'L0_mix_b_qkv', 'L0_mix_norm_g', 'L0_mix_norm_b', 'L0_mix_w_fc1', 'L0_mix_b_fc1',
        'L0_mix_w_fc2', 'L0_mix_b_fc2', 'L0_ffn_gate_w', 'L0_ffn_gate_b', 'L0_ffn_w1', 'L0_ffn_b1', 'L0_ffn_w2',
        'L0_ffn_b2']


def kernel(**inputs):
    import numpy as _np
    import concourse.bacc as _bacc
    from concourse import mybir as _mybir
    from concourse.bass_utils import run_bass_kernel_spmd as _run

    nc = _bacc.Bacc("TRN2", target_bir_lowering=False, num_devices=1)
    arrays, io = {}, {}
    for name in _INS:
        a = _np.ascontiguousarray(inputs[name])
        arrays[f"in_{name}_dram"] = a
        io[name] = nc.dram_tensor(f"in_{name}_dram", a.shape, _mybir.dt.from_np(a.dtype), kind="ExternalInput").ap()
    out = nc.dram_tensor("out_0_dram", (N, D), F32, kind="ExternalOutput").ap()
    gps_layer(nc, io, out)
    r = _run(nc, [arrays], core_ids=[0])
    return r.results[0]["out_0_dram"]
```
